# Optimizing a Trainium2 kernel written in Bass

```python
import numpy as np
import jax
import jax.numpy as jnp

def _softmax(x, axis=-1):
    return jax.nn.softmax(x, axis=axis)

def _gelu(x):
    return jax.nn.gelu(x, approximate=True)

def _silu(x):
    return jax.nn.silu(x)

def _sigmoid(x):
    return jax.nn.sigmoid(x)

def _layernorm(x, axis=-1, eps=1e-05):
    m = jnp.mean(x, axis=axis, keepdims=True)
    v = jnp.var(x, axis=axis, keepdims=True)
    return (x - m) / jnp.sqrt(v + eps)

def _scatter_add(tgt, idx, src, axis=0):
    return tgt.at[idx].add(src)

def _segment_sum(src, seg, n):
    return jax.ops.segment_sum(src, seg, n)
kernel_name = 'mk_seq_preln_d2_jaxref_r8_aaabb5'

def setup_inputs(seed: int=0):
    np.random.seed(seed)
    _w = jnp.asarray

    def _L0_attn_setup():
        import jax, jax.numpy as jnp
        import numpy as np
        D_MODEL = 256
        D_INNER = 256
        D_XB = 128
        D_STATE = 128
        NHEADS = D_INNER // D_STATE
        NKV = D_XB // D_STATE
        NREP = NHEADS // NKV
        D_CONV = 4
        CHUNK = 128
        INTER = 1024
        EPS = 1e-05
        BATCH, SEQ = (2, 256)

        def _rmsnorm(x, w, eps=EPS):
            v = jnp.mean(x * x, axis=-1, keepdims=True)
            return x * jax.lax.rsqrt(v + eps) * w

        def _segsum(x):
            T = x.shape[-1]
            cs = jnp.cumsum(x, axis=-1)
            seg = cs[..., :, None] - cs[..., None, :]
            mask = jnp.tril(jnp.ones((T, T), bool))
            return jnp.where(mask, seg, -jnp.inf)

        def _ssd(X, dA, Bm, Cm, chunk):
            b, l, h, p = X.shape
            c = l // chunk
            X = X.reshape(b, c, chunk, h, p)
            Bm = Bm.reshape(b, c, chunk, h, -1)
            Cm = Cm.reshape(b, c, chunk, h, -1)
            dA = dA.reshape(b, c, chunk, h).transpose(0, 3, 1, 2)
            dA_cs = jnp.cumsum(dA, axis=-1)
            L = jnp.exp(_segsum(dA))
            Y_diag = jnp.einsum('bclhn,bcshn,bhcls,bcshp->bclhp', Cm, Bm, L, X)
            decay_states = jnp.exp(dA_cs[..., -1:] - dA_cs)
            states = jnp.einsum('bcshn,bhcs,bcshp->bchpn', Bm, decay_states, X)
            states = jnp.concatenate([jnp.zeros_like(states[:, :1]), states], axis=1)
            chunk_decay = jnp.exp(_segsum(jnp.pad(dA_cs[..., -1], ((0, 0), (0, 0), (1, 0)))))
            new_states = jnp.einsum('bhzc,bchpn->bzhpn', chunk_decay, states)
            prev_states = new_states[:, :-1]
            Y_off = jnp.einsum('bclhn,bchpn,bhcl->bclhp', Cm, prev_states, jnp.exp(dA_cs))
            return (Y_diag + Y_off).reshape(b, l, h, p)
        key = jax.random.key(seed)
        ks = jax.random.split(key, 8)
        conv_dim = 2 * D_XB + D_INNER
        proj_dim = 2 * D_INNER + 2 * D_XB + NHEADS
        g = lambda k, shape, sc: jax.random.normal(k, shape, jnp.float32) * sc
        return {'hidden_states': jax.random.normal(ks[0], (BATCH, SEQ, D_MODEL), jnp.float32), 'ln1_w': jnp.ones((D_MODEL,), jnp.float32), 'W_in': g(ks[1], (D_MODEL, proj_dim), 0.02), 'conv_w': g(ks[2], (D_CONV, conv_dim), 0.2), 'conv_b': jnp.zeros((conv_dim,), jnp.float32), 'dt_bias': jnp.log(jnp.expm1(jnp.linspace(0.001, 0.1, NHEADS))).astype(jnp.float32), 'A_log': jnp.log(jnp.linspace(1.0, 16.0, NHEADS)).astype(jnp.float32), 'D': jnp.ones((NHEADS,), jnp.float32), 'norm_w': jnp.ones((D_INNER,), jnp.float32), 'W_out': g(ks[3], (D_INNER, D_MODEL), 0.02), 'ln2_w': jnp.ones((D_MODEL,), jnp.float32), 'w1': g(ks[4], (D_MODEL, INTER), 0.02), 'w3': g(ks[5], (D_MODEL, INTER), 0.02), 'w2': g(ks[6], (INTER, D_MODEL), 0.02)}
    _L0_attn_in = _L0_attn_setup()

    def _L0_ffn_setup():
        import math
        import jax, jax.numpy as jnp
        import numpy as np
        DIM = 256
        RANK = 8
        B, T = (4, 512)

        def _orthogonal(key, n):
            a = jax.random.normal(key, (n, n), dtype=jnp.float32)
            q, r = jnp.linalg.qr(a)
            q = q * jnp.sign(jnp.diagonal(r))[None, :]
            return q
        key = jax.random.key(seed)
        kx, kf = jax.random.split(key)
        x = jax.random.normal(kx, (B, T, DIM), dtype=jnp.float32)
        fkeys = jax.random.split(kf, RANK)
        factors = jnp.stack([_orthogonal(fkeys[r], DIM) * (r + 1) ** (-0.5) for r in range(RANK)])
        bias = jnp.zeros((DIM,), dtype=jnp.float32)
        return {'x': x, 'factors': factors, 'bias': bias}
    _L0_ffn_in = _L0_ffn_setup()

    def _L1_attn_setup():
        import jax, jax.numpy as jnp
        import numpy as np
        IGNORE = -100000.0
        key = jax.random.key(seed)
        ks = jax.random.split(key, 5)
        b, s, d_model = (4, 256, 256)
        n_q, n_kv, d_head = (32, 8, 64)
        std = 0.02
        return {'normalized_resid_pre': jax.random.normal(ks[0], (b, s, d_model), jnp.float32), 'W_Q': jax.random.normal(ks[1], (n_q, d_model, d_head), jnp.float32) * std, 'W_K': jax.random.normal(ks[2], (n_kv, d_model, d_head), jnp.float32) * std, 'W_V': jax.random.normal(ks[3], (n_kv, d_model, d_head), jnp.float32) * std, 'W_O': jax.random.normal(ks[4], (n_kv, d_head, d_model), jnp.float32) * std}
    _L1_attn_in = _L1_attn_setup()

    def _L1_ffn_setup():
        import jax, jax.numpy as jnp
        import numpy as np
        E, TOP_K, H, I = (8, 2, 256, 704)
        key = jax.random.key(seed)
        k1, k2, k3, k4, k5 = jax.random.split(key, 5)
        s = 0.02
        return {'hidden_states': jax.random.normal(k1, (2, 128, H), dtype=jnp.float32), 'gate_w': jax.random.normal(k2, (E, H), dtype=jnp.float32) * s, 'w1': jax.random.normal(k3, (E, I, H), dtype=jnp.float32) * s, 'w3': jax.random.normal(k4, (E, I, H), dtype=jnp.float32) * s, 'w2': jax.random.normal(k5, (E, H, I), dtype=jnp.float32) * s}
    _L1_ffn_in = _L1_ffn_setup()
    _d = {'L0_attn_hidden_states': _L0_attn_in['hidden_states'], 'L0_attn_ln1_w': _L0_attn_in['ln1_w'], 'L0_attn_W_in': _L0_attn_in['W_in'], 'L0_attn_conv_w': _L0_attn_in['conv_w'], 'L0_attn_conv_b': _L0_attn_in['conv_b'], 'L0_attn_dt_bias': _L0_attn_in['dt_bias'], 'L0_attn_A_log': _L0_attn_in['A_log'], 'L0_attn_D': _L0_attn_in['D'], 'L0_attn_norm_w': _L0_attn_in['norm_w'], 'L0_attn_W_out': _L0_attn_in['W_out'], 'L0_attn_ln2_w': _L0_attn_in['ln2_w'], 'L0_attn_w1': _L0_attn_in['w1'], 'L0_attn_w3': _L0_attn_in['w3'], 'L0_attn_w2': _L0_attn_in['w2'], 'L0_ffn_factors': _L0_ffn_in['factors'], 'L0_ffn_bias': _L0_ffn_in['bias'], 'L1_attn_W_Q': _L1_attn_in['W_Q'], 'L1_attn_W_K': _L1_attn_in['W_K'], 'L1_attn_W_V': _L1_attn_in['W_V'], 'L1_attn_W_O': _L1_attn_in['W_O'], 'L1_ffn_gate_w': _L1_ffn_in['gate_w'], 'L1_ffn_w1': _L1_ffn_in['w1'], 'L1_ffn_w3': _L1_ffn_in['w3'], 'L1_ffn_w2': _L1_ffn_in['w2']}
    _x0 = _d['L0_attn_hidden_states']
    _d['L0_attn_hidden_states'] = jax.random.normal(jax.random.fold_in(jax.random.key(seed), 1), (1, 1024, 256), dtype=_x0.dtype)
    del _x0
    return _d

def reference(L0_attn_hidden_states, L0_attn_ln1_w, L0_attn_W_in, L0_attn_conv_w, L0_attn_conv_b, L0_attn_dt_bias, L0_attn_A_log, L0_attn_D, L0_attn_norm_w, L0_attn_W_out, L0_attn_ln2_w, L0_attn_w1, L0_attn_w3, L0_attn_w2, L0_ffn_factors, L0_ffn_bias, L1_attn_W_Q, L1_attn_W_K, L1_attn_W_V, L1_attn_W_O, L1_ffn_gate_w, L1_ffn_w1, L1_ffn_w3, L1_ffn_w2):

    def _L0_attn_ref(hidden_states, ln1_w, W_in, conv_w, conv_b, dt_bias, A_log, D, norm_w, W_out, ln2_w, w1, w3, w2):
        import jax, jax.numpy as jnp
        import numpy as np
        D_MODEL = 256
        D_INNER = 256
        D_XB = 128
        D_STATE = 128
        NHEADS = D_INNER // D_STATE
        NKV = D_XB // D_STATE
        NREP = NHEADS // NKV
        D_CONV = 4
        CHUNK = 128
        INTER = 1024
        EPS = 1e-05
        BATCH, SEQ = (2, 256)

        def _rmsnorm(x, w, eps=EPS):
            v = jnp.mean(x * x, axis=-1, keepdims=True)
            return x * jax.lax.rsqrt(v + eps) * w

        def _segsum(x):
            T = x.shape[-1]
            cs = jnp.cumsum(x, axis=-1)
            seg = cs[..., :, None] - cs[..., None, :]
            mask = jnp.tril(jnp.ones((T, T), bool))
            return jnp.where(mask, seg, -jnp.inf)

        def _ssd(X, dA, Bm, Cm, chunk):
            b, l, h, p = X.shape
            c = l // chunk
            X = X.reshape(b, c, chunk, h, p)
            Bm = Bm.reshape(b, c, chunk, h, -1)
            Cm = Cm.reshape(b, c, chunk, h, -1)
            dA = dA.reshape(b, c, chunk, h).transpose(0, 3, 1, 2)
            dA_cs = jnp.cumsum(dA, axis=-1)
            L = jnp.exp(_segsum(dA))
            Y_diag = jnp.einsum('bclhn,bcshn,bhcls,bcshp->bclhp', Cm, Bm, L, X)
            decay_states = jnp.exp(dA_cs[..., -1:] - dA_cs)
            states = jnp.einsum('bcshn,bhcs,bcshp->bchpn', Bm, decay_states, X)
            states = jnp.concatenate([jnp.zeros_like(states[:, :1]), states], axis=1)
            chunk_decay = jnp.exp(_segsum(jnp.pad(dA_cs[..., -1], ((0, 0), (0, 0), (1, 0)))))
            new_states = jnp.einsum('bhzc,bchpn->bzhpn', chunk_decay, states)
            prev_states = new_states[:, :-1]
            Y_off = jnp.einsum('bclhn,bchpn,bhcl->bclhp', Cm, prev_states, jnp.exp(dA_cs))
            return (Y_diag + Y_off).reshape(b, l, h, p)
        b, l, _ = hidden_states.shape
        res = hidden_states
        h = _rmsnorm(hidden_states, ln1_w)
        zxbcdt = h @ W_in
        splits = np.cumsum([D_INNER, D_XB, D_XB, D_INNER]).tolist()
        z, xv, Bv, Cv, dt = jnp.split(zxbcdt, splits, axis=-1)
        xBC = jnp.concatenate([xv, Bv, Cv], axis=-1)
        xp = jnp.pad(xBC, ((0, 0), (D_CONV - 1, 0), (0, 0)))
        conv = sum((xp[:, k:k + l, :] * conv_w[k] for k in range(D_CONV))) + conv_b
        xBC = jax.nn.silu(conv)
        xv, Bv, Cv = jnp.split(xBC, [D_XB, 2 * D_XB], axis=-1)
        xh = jnp.repeat(xv.reshape(b, l, NKV, D_STATE), NREP, axis=2)
        Bh = jnp.repeat(Bv.reshape(b, l, NKV, D_STATE), NREP, axis=2)
        Ch = Cv.reshape(b, l, NHEADS, D_STATE)
        dt = jax.nn.softplus(dt + dt_bias)
        a = -jnp.exp(A_log)
        dA = dt * a
        X = xh * dt[..., None]
        y = _ssd(X, dA, Bh, Ch, CHUNK)
        y = y + D[None, None, :, None] * xh
        y = y.reshape(b, l, D_INNER)
        y = _rmsnorm(y * jax.nn.silu(z), norm_w)
        h = y @ W_out
        h = res + h
        res2 = h
        h = _rmsnorm(h, ln2_w)
        h = jax.nn.silu(h @ w1) * (h @ w3) @ w2
        return res2 + h

    def _L0_ffn_ref(x, factors, bias):
        import math
        import jax, jax.numpy as jnp
        import numpy as np
        DIM = 256
        RANK = 8
        B, T = (4, 512)

        def _orthogonal(key, n):
            a = jax.random.normal(key, (n, n), dtype=jnp.float32)
            q, r = jnp.linalg.qr(a)
            q = q * jnp.sign(jnp.diagonal(r))[None, :]
            return q
        rank = factors.shape[0]
        mixed = jnp.einsum('btd,rde->bte', x, factors)
        mixed = mixed / math.sqrt(rank) + bias
        return mixed

    def _L1_attn_ref(normalized_resid_pre, W_Q, W_K, W_V, W_O):
        import jax, jax.numpy as jnp
        import numpy as np
        IGNORE = -100000.0
        x = normalized_resid_pre
        b, s, _ = x.shape
        n_kv, d_head = (W_K.shape[0], W_K.shape[2])
        n_q = W_Q.shape[0]
        g = n_q // n_kv
        q = jnp.einsum('bpd,hdk->bphk', x, W_Q)
        k = jnp.einsum('bpd,ndk->bpnk', x, W_K)
        v = jnp.einsum('bpd,ndk->bpnk', x, W_V)
        gq = q.reshape(b, s, n_kv, g, d_head).transpose(0, 1, 3, 2, 4)
        scores = jnp.einsum('bqgnh,bknh->bnqk', gq, k) / jnp.sqrt(jnp.float32(d_head))
        causal = jnp.triu(jnp.ones((s, s), dtype=bool), k=1)
        scores = jnp.where(causal, IGNORE, scores)
        pattern = jax.nn.softmax(scores, axis=-1)
        z = jnp.einsum('bknh,bnqk->bqnh', v, pattern)
        attn_out = jnp.einsum('bqnh,nhd->bqd', z, W_O)
        return attn_out

    def _L1_ffn_ref(hidden_states, gate_w, w1, w3, w2):
        import jax, jax.numpy as jnp
        import numpy as np
        E, TOP_K, H, I = (8, 2, 256, 704)
        orig_shape = hidden_states.shape
        x = hidden_states.reshape(-1, H)
        T = x.shape[0]
        router_logits = x @ gate_w.T
        probs = jax.nn.softmax(router_logits, axis=-1)
        topk_vals, topk_idx = jax.lax.top_k(probs, TOP_K)
        topk_vals = topk_vals / jnp.sum(topk_vals, axis=-1, keepdims=True)
        combine = jnp.zeros((T, E), dtype=x.dtype)
        combine = combine.at[jnp.arange(T)[:, None], topk_idx].add(topk_vals)
        g = jnp.einsum('th,eih->tei', x, w1)
        u = jnp.einsum('th,eih->tei', x, w3)
        a = jax.nn.silu(g) * u
        y = jnp.einsum('tei,ehi->teh', a, w2)
        out = jnp.einsum('te,teh->th', combine, y)
        return out.reshape(orig_shape)
    x = L0_attn_hidden_states
    x = x + _L0_attn_ref(_layernorm(x, axis=-1), L0_attn_ln1_w, L0_attn_W_in, L0_attn_conv_w, L0_attn_conv_b, L0_attn_dt_bias, L0_attn_A_log, L0_attn_D, L0_attn_norm_w, L0_attn_W_out, L0_attn_ln2_w, L0_attn_w1, L0_attn_w3, L0_attn_w2)
    x = x + _L0_ffn_ref(_layernorm(x, axis=-1), L0_ffn_factors, L0_ffn_bias)
    x = x + _L1_attn_ref(_layernorm(x, axis=-1), L1_attn_W_Q, L1_attn_W_K, L1_attn_W_V, L1_attn_W_O)
    x = x + _L1_ffn_ref(_layernorm(x, axis=-1), L1_ffn_gate_w, L1_ffn_w1, L1_ffn_w3, L1_ffn_w2)
    return x

_drawn_inputs = setup_inputs


def setup_inputs(seed=0):
    import zlib

    import numpy as np

    out = dict(_drawn_inputs(seed))
    spreads = {'L0_attn_ln1_w': (1.0, 0.2),
     'L0_attn_conv_b': (0.0, 0.1),
     'L0_attn_D': (1.0, 0.6),
     'L0_attn_norm_w': (1.0, 0.2),
     'L0_attn_ln2_w': (1.0, 0.6),
     'L0_ffn_bias': (0.0, 0.1)}
    factors = {'L0_attn_dt_bias': 8.0,
     'L0_attn_A_log': 8.0,
     'L0_attn_w1': 3.056,
     'L0_attn_w3': 3.011,
     'L0_attn_w2': 3.011,
     'L1_attn_W_Q': 8.0,
     'L1_attn_W_K': 8.0,
     'L1_attn_W_V': 8.0,
     'L1_attn_W_O': 8.0,
     'L1_ffn_gate_w': 6.842,
     'L1_ffn_w1': 6.034,
     'L1_ffn_w3': 5.946,
     'L1_ffn_w2': 5.966}
    for name, (base, spread) in spreads.items():
        noise = np.random.default_rng([zlib.crc32(name.encode()), seed]).standard_normal(out[name].shape)
        drawn = base * np.exp(spread * noise) if base else spread * noise
        out[name] = jnp.asarray(drawn.astype(out[name].dtype))
    for name, factor in factors.items():
        out[name] = (out[name] * factor).astype(out[name].dtype)
    return out
```

```python
from contextlib import ExitStack

import numpy as np

import concourse.bass as bass
from concourse import mybir

F32 = mybir.dt.float32
BF16 = mybir.dt.bfloat16
I32 = mybir.dt.int32
U32 = mybir.dt.uint32
ALU = mybir.AluOpType
ACT = mybir.ActivationFunctionType
AX_X = mybir.AxisListType.X

P = 128
T = 1024
TT = T // P
D = 256
KD = D // P
GT = 4
GROUPS = TT // GT
GW = GT * P
EPS = 1e-5
H_SSD = 2
N_IN = 770
CONV_BLOCKS = 4
TAPS = 4
FF = 1024
FB = FF // P
RANK = 8
HEADS = 8
DH = 64
QH = 32 // HEADS
QKV = HEADS * DH
QB = QKV // P
E = 8
I = 704
IH = I // 2
IB = (I + P - 1) // P
ILAST = I - (IB - 1) * P
TOP = 2
TILES_MAX = TOP * T // P + E - 1
MASK = -1.0e30

C_LN1, C_NORM, C_LN2, C_CONVW, C_CONVB, C_DTB, C_ALOG, C_D = 0, 2, 4, 6, 22, 26, 28, 30
N_SMALL = 32
C_IDENT, C_LE, C_GT, C_LT, C_ONES, C_NEGS, C_NEGA, C_IOTA = 0, 128, 256, 384, 512, 640, 768, 896
N_CONST = C_IOTA + 24


def build(nc, x_in, small_in, const_in, w_in, w_out, f_w13, f_w2, factors, ffn_bias, wq, wk, wv, wo,
          gate, m_w1, m_w3, m_w2, m_w2t, out):
    slots_in = nc.dram_tensor("expert_in", [TILES_MAX * P, D], F32, kind="Internal").ap()
    slots_out = nc.dram_tensor("expert_out", [TILES_MAX * P, D], F32, kind="Internal").ap()
    with ExitStack() as ctx:
        def sb(name, cols, dt=F32):
            return ctx.enter_context(nc.sbuf_tensor(name, [P, cols], dt))

        def sem(name):
            return ctx.enter_context(nc.semaphore(name))

        def view(tensor, start, *dims):
            n = int(np.prod(dims))
            a = tensor[:, start:start + n]
            if len(dims) == 2:
                return a.rearrange("p (a b) -> p a b", a=dims[0])
            if len(dims) == 3:
                return a.rearrange("p (a b c) -> p a b c", a=dims[0], b=dims[1])
            return a

        early = sb("early", 2 * E * KD * I)
        mid = sb("mid", E * IB * D)
        at = 0
        win_sb = view(early, at, KD, N_IN); at += KD * N_IN
        fac_sb = view(early, at, RANK, KD * D); at += RANK * KD * D
        wq_sb = view(early, at, QH, KD * QKV); at += QH * KD * QKV
        zs = view(early, at, KD, T); kv_at = at; at += KD * T
        yg = view(early, at, KD, T); at += KD * T
        xpad = view(early, at, CONV_BLOCKS, T + TAPS - 1); ffn_a = [view(early, at, FB, GW)]
        at += CONV_BLOCKS * (T + TAPS - 1)
        cv = view(early, at, CONV_BLOCKS, T); ffn_a.append(view(early, at, FB, GW))
        at += CONV_BLOCKS * T
        assert at <= 2 * E * KD * I
        mixed_w = view(early, KD * N_IN, KD, D)
        wq_sum = view(early, KD * N_IN + RANK * KD * D, KD, QKV)
        wk_sb = view(early, kv_at, KD, QKV)
        wv_sb = view(early, kv_at + KD * QKV, KD, QKV)
        ew1 = view(early, 0, E, KD * I)
        ew3 = view(early, E * KD * I, E, KD * I)

        at = 0
        fw13 = view(mid, at, 2, KD, FF); at += 2 * KD * FF
        fw2 = view(mid, at, FB, D); at += FB * D
        wout_sb = view(mid, at, KD, D); at += KD * D
        tok = view(mid, at, 2, 2 * P); at += 4 * P
        ddx = view(mid, at, 2, H_SSD * P); at += 4 * P
        ramp = view(mid, at, 2, H_SSD * P); at += 4 * P
        decays = view(mid, at, 2, 4 * P); at += 8 * P
        mt = view(mid, at, 2, H_SSD * P); at += 4 * P
        ce = view(mid, at, 2, H_SSD * P); at += 4 * P
        sq = view(mid, at, 2, H_SSD * P); at += 4 * P
        state = view(mid, at, 2, H_SSD, P); at += 2 * H_SSD * P
        assert at <= E * IB * D
        qT = view(mid, 0, QB, T)
        kT = view(mid, QB * T, QB, T)
        v_sb = view(mid, 2 * QB * T, TT, QKV)
        ew2 = view(mid, 0, E, IB * D)

        x_t = sb("x", TT * D); x = view(x_t, 0, TT, D)
        xn_t = sb("xn", TT * D); xn = view(xn_t, 0, TT, D)
        hh_t = sb("hh", TT * D); hh = view(hh_t, 0, TT, D)
        hT_t = sb("hT", KD * T); hT = view(hT_t, 0, KD, T)
        work = sb("work", 7 * 1024)
        probs = view(work, 0, 3, 1024)
        pT = view(work, 3072, 2, 1024)
        zn = work[:, 5120:5632]
        zT = view(work, 5632, QB, P)
        wo_sb = view(work, 6144, QB, D)
        sgate = [view(work, 0, GW), view(work, GW, GW)]
        at = 0
        xs = view(work, at, 2, D); at += 2 * D
        xsT = view(work, at, 2, KD, P); at += 2 * D
        eg = view(work, at, 2, IH); at += I
        ea = view(work, at, 2, I); at += 2 * I
        eaT = view(work, at, 2, IB, P); at += 2 * IB * P
        ey = view(work, at, 2, D); at += 2 * D
        assert at <= 7 * 1024
        cst = sb("cst", N_CONST)
        ident, le_m, gt_m, lt_m, ones = (cst[:, c:c + P] for c in (C_IDENT, C_LE, C_GT, C_LT, C_ONES))
        iota = cst[:, C_IOTA:C_IOTA + 24]
        small = sb("small", N_SMALL)
        bias_sb = sb("bias_sb", D)
        gate_t = sb("gate_sb", KD * E); gate_sb = view(gate_t, 0, KD, E)
        ident_b = sb("ident_b", P, BF16)
        neg_s = sb("neg_s", H_SSD * P, BF16)
        neg_a = sb("neg_a", P, BF16)
        stats_t = sb("stats", TT * 6); stats = view(stats_t, 0, TT, 6)
        mv_t = sb("mv", TT * 2); mv = view(mv_t, 0, TT, 2)
        veps = sb("veps", TT); rstd = sb("rstd", TT)
        veps2 = sb("veps2", TT); rstd2 = sb("rstd2", TT)
        mhalf = sb("mhalf", TT)
        zero = sb("zero", D)
        dts_t = sb("dts", 10 * TT * H_SSD)
        dts = [view(dts_t, i * TT * H_SSD, TT, H_SSD) for i in range(10)]
        ea_log = sb("ea_log", H_SSD)
        dec_t = sb("dec", 2 * TT * H_SSD)
        dec = view(dec_t, 0, 2, TT, H_SSD)
        nmax = sb("nmax", TT * HEADS)
        psums = sb("psums", TT * HEADS)
        pinv = sb("pinv", TT * HEADS)
        rt_t = sb("rt", 8 * TT * E)
        rt = [view(rt_t, i * TT * E, TT, E) for i in range(8)]
        rs_t = sb("rs", 12 * TT)
        rs = [rs_t[:, i * TT:(i + 1) * TT] for i in range(12)]
        top_i_t = sb("top_i", TT * 8, U32); top_i = view(top_i_t, 0, TT, 8)
        slot_i_t = sb("slot_i", TOP * TT, U32); slot_i = view(slot_i_t, 0, TOP, TT)
        ecmp = view(bias_sb, 0, 24, E)
        eid_f = sb("eid_f", 24)
        eid = sb("eid", 24, I32)
        ps = ctx.enter_context(nc.psum_tensor("ps", [P, 8, 512], F32))

        s_x = [sem(f"x_loaded{g}") for g in range(GROUPS)]
        s_small, s_const, s_win, s_mixw, s_ffnw = (sem(n) for n in (
            "small_loaded", "const_loaded", "win_loaded", "wout_loaded", "ffnw_loaded"))
        s_fac, s_wq, s_kv, s_wo, s_gate = (sem(n) for n in (
            "factors_loaded", "wq_loaded", "kv_loaded", "wo_loaded", "gate_loaded"))
        s_e13, s_e2 = sem("expert_w13_loaded"), sem("expert_w2_loaded")
        s_zeroed, s_zerodma = sem("zero_set"), sem("slots_cleared")
        s_cbf = sem("bf16_constants")
        s_pool0 = sem("pool_constants")
        s_var, s_rstd, s_hh, s_tr, s_hT = (sem(n) for n in (
            "variance", "rstd", "normalised", "transposed", "feature_major"))
        s_var2, s_rstd2 = sem("variance2"), sem("rstd2")
        s_proj, s_evac, s_conv, s_xbc = (sem(n) for n in ("in_proj", "in_evac", "conv_tap", "conv_silu"))
        s_dtp, s_dtv, s_dta = sem("dt_proj"), sem("dt_vector"), sem("dt_scalar")
        s_decp, s_dec, s_dd = sem("decay_sum"), sem("decay_exp"), sem("decay_dt")
        s_ramp, s_front_tr, s_front_seg, s_front_g = (sem(n) for n in (
            "ramp", "chunk_transposed", "segments", "bc_product"))
        s_tok, s_exp, s_mt, s_ce, s_ddx = (sem(n) for n in ("chunk_tokens", "decays", "mt", "ce", "ddx"))
        s_y, s_st, s_state, s_yg, s_sq, s_ss = (sem(n) for n in (
            "y_sum", "state_sum", "state", "y_gated", "y_squared", "square_sum"))
        s_yv, s_yr = sem("y_variance"), sem("y_rstd")
        s_wn = sem("wout_scaled")
        s_mo, s_r2 = sem("mixer_out"), sem("mixer_residual")
        s_xr = sem("x_plus_residual")
        s_gu, s_sg, s_fa, s_fo, s_x1 = (sem(n) for n in (
            "ffn_gate_up", "ffn_silu", "ffn_act", "ffn_out", "x1"))
        s_fsum, s_wqsum = sem("factors_summed"), sem("wq_summed")
        s_xb, s_mx, s_x2 = sem("x_plus_bias"), sem("mixing"), sem("x2")
        s_qkv, s_qa, s_qd = sem("qkv"), sem("qkv_scalar"), sem("qkv_vector")
        s_sc, s_max, s_pr, s_pt, s_pta, s_ptd, s_pv = (sem(n) for n in (
            "scores", "row_max", "probs", "probs_transposed", "pT_scalar", "pT_vector", "attended"))
        s_zn, s_zt, s_zT, s_ao, s_x3 = (sem(n) for n in (
            "z_normalised", "z_transposed", "zT", "attn_out", "x3"))
        s_lg, s_rv, s_ra, s_cnt = sem("logits"), sem("router_vector"), sem("router_scalar"), sem("counts")
        s_slots, s_scat = sem("slots"), sem("scattered")
        s_xs = [sem(f"slot_tile_loaded{b}") for b in range(2)]
        s_ext, s_exT, s_eg, s_eu, s_esg, s_ea = (sem(n) for n in (
            "slot_tile_transposed", "slot_tile_T", "expert_gate", "expert_up", "expert_silu", "expert_act"))
        s_eat, s_eaa, s_ead, s_ey, s_eyc = (sem(n) for n in (
            "act_transposed", "act_T_scalar", "act_T_vector", "expert_y", "expert_y_copied"))
        s_eys = [sem(f"expert_y_stored{b}") for b in range(2)]
        s_gath = sem("gathered")
        s_fin, s_out = sem("final"), sem("stored")
        s_dve, s_act, s_pool = sem("vector_chain"), sem("scalar_chain"), sem("pool_chain")

        def qkv_dst(q):
            g, j = divmod(q, 12)
            if j < 4:
                return qT[:, j, g * GW:(g + 1) * GW], float(DH) ** -0.5
            if j < 8:
                return kT[:, j - 4, g * GW:(g + 1) * GW], 1.0
            return v_sb[:, g * GT + j - 8, :], 1.0

        block = ctx.enter_context(nc.Block())
        PH_MIX, PH_FFN, PH_FAC, PH_ATT, PH_MOE = range(5)
        LAST = TILES_MAX - 1

        @block.sync
        def _(sp):
            xv = x_in.rearrange("(t p) d -> p t d", p=P)
            for g in range(GROUPS):
                sp.dma_start(x[:, g * GT:(g + 1) * GT, :], xv[:, g * GT:(g + 1) * GT, :]).then_inc(s_x[g], 16)
                if g == 0:
                    sp.dma_start(cst[:, :], const_in).then_inc(s_const, 16)
                    sp.dma_start(small[:, :], small_in).then_inc(s_small, 16)
            sp.dma_start(win_sb, w_in.rearrange("(k p) n -> p k n", p=P)).then_inc(s_win, 16)
            sp.dma_start(wout_sb, w_out.rearrange("(k p) n -> p k n", p=P)).then_inc(s_mixw, 16)
            sp.dma_start(fac_sb, factors).then_inc(s_fac, 16)
            sp.dma_start(wq_sb, wq).then_inc(s_wq, 16)
            sp.dma_start(fw13, f_w13).then_inc(s_ffnw, 16)
            sp.dma_start(fw2, f_w2.rearrange("(f p) n -> p f n", p=P)).then_inc(s_ffnw, 16)
            sp.dma_start(bias_sb[:, :], ffn_bias).then_inc(s_gate, 16)
            sp.dma_start(gate_sb, gate).then_inc(s_gate, 16)
            sp.wait_ge(s_zeroed, 1)
            for i in range(TILES_MAX):
                sp.dma_start(slots_in[i * P:(i + 1) * P, :], zero[:, :]).then_inc(s_zerodma, 16)
            sp.wait_ge(s_r2, TT)
            sp.dma_start(wk_sb, wk).then_inc(s_kv, 16)
            sp.dma_start(wv_sb, wv).then_inc(s_kv, 16)
            sp.wait_ge(s_x1, TT)
            sp.dma_start(wo_sb, wo.rearrange("(c p) n -> p c n", p=P)).then_inc(s_wo, 16)
            sp.wait_ge(s_qa, GROUPS * 6)
            sp.wait_ge(s_qd, GROUPS * 6)
            for e in range(E):
                sp.dma_start(ew1[:, e], m_w1[:, e]).then_inc(s_e13, 16)
                sp.dma_start(ew3[:, e], m_w3[:, e]).then_inc(s_e13, 16)
            sp.wait_ge(s_x3, TT)
            for e in range(E):
                sp.dma_start(ew2[:, e, 0:(IB - 1) * D], m_w2[:, e]).then_inc(s_e2, 16)
            sp.dma_start(mid[0:ILAST, :].rearrange("p (e r) -> p e r", e=E)[:, :, (IB - 1) * D:],
                         m_w2t).then_inc(s_e2, 16)

            def load_slots(i, b):
                sp.dma_start(xs[:, b], slots_in[bass.ts(i, P), :]).then_inc(s_xs[b], 16)

            sp.wait_ge(s_scat, TOP * TT * 16)
            for b in range(2):
                load_slots(b, b)
            with sp.Fori(0, LAST // 2 - 1) as j:
                for b in range(2):
                    sp.wait_ge(s_ext, 2 * j + b + 1)
                    load_slots(2 * j + b + 2, b)
            sp.wait_ge(s_ext, LAST - 1)
            load_slots(LAST, 0)

            for t in range(TT):
                sp.wait_ge(s_fin, t + 1)
                sp.dma_start(out[t * P:(t + 1) * P, :], x[:, t, :]).then_inc(s_out, 16)
            sp.wait_ge(s_out, TT * 16)

        @block.gpsimd
        def _(pool):
            n_pool = [0]

            def link(ins):
                n_pool[0] += 1
                ins.then_inc(s_pool, 1)
                pool.wait_ge(s_pool, n_pool[0])

            nc.gpsimd.memset(mhalf[:, :], -0.5).then_inc(s_pool0, 1)
            nc.gpsimd.memset(zero[:, :], 0.0).then_inc(s_zeroed, 1)
            nc.gpsimd.memset(xpad[:, :, 0:TAPS - 1], 0.0).then_inc(s_pool0, 1)
            pool.wait_ge(s_pool0, 2)

            def rstds(ph):
                for g in range(GROUPS):
                    n = GROUPS * ph + g + 1
                    pool.wait_ge(s_var, n)
                    c = slice(g * GT, (g + 1) * GT)
                    nc.gpsimd.tensor_tensor(rstd[:, c], veps[:, c], mhalf[:, c], ALU.pow).then_inc(s_rstd, 1)
                    if ph == PH_MIX:
                        pool.wait_ge(s_var2, g + 1)
                        nc.gpsimd.tensor_tensor(rstd2[:, c], veps2[:, c], mhalf[:, c],
                                                ALU.pow).then_inc(s_rstd2, 1)

            rstds(PH_MIX)
            pool.wait_ge(s_fac, 16)
            for r in range(1, RANK):
                link(nc.gpsimd.tensor_tensor(fac_sb[:, 0], fac_sb[:, 0], fac_sb[:, r], ALU.add))
            nc.gpsimd.tensor_scalar(fac_sb[:, 0], fac_sb[:, 0], float(1.0 / np.sqrt(RANK)), None,
                                    ALU.mult).then_inc(s_fsum, 1)
            for c in range(TT):
                b = c % 2
                if c == 0:
                    pool.wait_ge(s_dtv, 4)
                if c >= 2:
                    pool.wait_ge(s_front_seg, c - 1)
                for h in range(H_SSD):
                    last = nc.gpsimd.tensor_scalar(ramp[:, b, h * P:(h + 1) * P], le_m, dts[1][:, c, h:h + 1],
                                                   None, ALU.mult)
                last.then_inc(s_ramp, 1)
                if c == 0:
                    pool.wait_ge(s_dd, 1)
                pool.wait_ge(s_tok, c + 1)
                if c >= 2:
                    pool.wait_ge(s_y, c - 1)
                    pool.wait_ge(s_st, c - 1)
                if c < TT - 1:
                    for h in range(H_SSD):
                        last = nc.gpsimd.tensor_scalar(ddx[:, b, h * P:(h + 1) * P], tok[:, b, 0:P],
                                                       dts[2][:, c, h:h + 1], None, ALU.mult)
                    last.then_inc(s_ddx, 1)
                if c > 0:
                    pool.wait_ge(s_exp, c + 1)
                    nc.gpsimd.tensor_tensor(ce[:, b].rearrange("p (h l) -> p h l", h=H_SSD),
                                            cv[:, 2:4, c * P:(c + 1) * P],
                                            decays[:, b, 2 * P:].rearrange("p (h l) -> p h l", h=H_SSD),
                                            ALU.mult).then_inc(s_ce, 1)
            pool.wait_ge(s_yv, 1)
            nc.gpsimd.tensor_tensor(rstd2[:, :], veps2[:, :], mhalf[:, :], ALU.pow).then_inc(s_yr, 1)
            pool.wait_ge(s_wq, 16)
            for r in range(1, QH):
                ins = nc.gpsimd.tensor_tensor(wq_sb[:, 0], wq_sb[:, 0], wq_sb[:, r], ALU.add)
                if r < QH - 1:
                    link(ins)
            ins.then_inc(s_wqsum, 1)
            rstds(PH_FFN)
            for t in range(TT):
                pool.wait_ge(s_r2, t + 1)
                nc.gpsimd.tensor_tensor(x[:, t, :], x[:, t, :], xn[:, t, :], ALU.add).then_inc(s_xr, 1)
            rstds(PH_FAC)
            pool.wait_ge(s_gate, 32)
            for t in range(TT):
                pool.wait_ge(s_hh, TT * PH_FAC + t + 1)
                nc.gpsimd.tensor_tensor(x[:, t, :], x[:, t, :], bias_sb[:, :], ALU.add).then_inc(s_xb, 1)
            rstds(PH_ATT)
            rstds(PH_MOE)
            pool.wait_ge(s_zerodma, TILES_MAX * 16)
            pool.wait_ge(s_slots, 1)
            pool.wait_ge(s_hh, TT * PH_MOE + TT)
            for t in range(TT):
                for k in range(TOP):
                    nc.gpsimd.indirect_dma_start(
                        out=slots_in, out_offset=bass.IndirectOffsetOnAxis(ap=slot_i[:, k, t:t + 1], axis=0),
                        in_=hh[:, t, :], in_offset=None).then_inc(s_scat, 16)
            pool.wait_ge(s_scat, TOP * TT * 16)
            for b in range(2):
                pool.wait_ge(s_eys[b], 16 * ((TILES_MAX + 1 - b) // 2))
            for t in range(TT):
                for k, dst in enumerate((xn, hh)):
                    nc.gpsimd.indirect_dma_start(
                        out=dst[:, t, :], out_offset=None, in_=slots_out,
                        in_offset=bass.IndirectOffsetOnAxis(ap=slot_i[:, k, t:t + 1], axis=0)).then_inc(s_gath, 16)

        @block.scalar
        def _(act):
            n_act = [0]

            def link(ins):
                n_act[0] += 1
                ins.then_inc(s_act, 1)
                act.wait_ge(s_act, n_act[0])

            def feature_major(ph, scale_col=None):
                for g in range(GROUPS):
                    act.wait_ge(s_tr, GROUPS * ph + g + 1)
                    for k in range(KD):
                        dst = hT[:, k, g * GW:(g + 1) * GW]
                        if scale_col is None:
                            last = nc.scalar.copy(dst, ps[:, k, :])
                        else:
                            last = nc.scalar.activation(dst, ps[:, k, :], ACT.Copy,
                                                        scale=small[:, scale_col + k:scale_col + k + 1])
                    last.then_inc(s_hT, 1)

            act.wait_ge(s_small, 16)
            act.wait_ge(s_pool0, 2)
            feature_major(PH_MIX, C_LN1)
            for q in range(GROUPS * 6):
                g, fb = divmod(q, 6)
                act.wait_ge(s_proj, q + 1)
                bank = ps[:, 2 + q % 4, :]
                if fb < 2:
                    last = nc.scalar.activation(zs[:, fb, g * GW:(g + 1) * GW], bank, ACT.Silu)
                else:
                    c = fb - 2
                    nc.scalar.copy(xpad[:, c, TAPS - 1 + g * GW:TAPS - 1 + (g + 1) * GW], bank)
                    last = nc.scalar.activation(
                        cv[:, c, g * GW:(g + 1) * GW], bank, ACT.Identity,
                        scale=small[:, C_CONVW + 4 * c + 3:C_CONVW + 4 * c + 4],
                        bias=small[:, C_CONVB + c:C_CONVB + c + 1])
                last.then_inc(s_evac, 1)
            for g in range(GROUPS):
                for c in range(CONV_BLOCKS):
                    act.wait_ge(s_conv, g * 12 + 8 + c + 1)
                    a = cv[:, c, g * GW:(g + 1) * GW]
                    nc.scalar.activation(a, a, ACT.Silu).then_inc(s_xbc, 1)
            act.wait_ge(s_dtv, 1)
            nc.scalar.activation(dts[3], dts[3], ACT.Exp).then_inc(s_dta, 1)
            nc.scalar.activation(ea_log[:, :], small[:, C_ALOG:C_ALOG + H_SSD], ACT.Exp).then_inc(s_dta, 1)
            act.wait_ge(s_dtv, 2)
            nc.scalar.activation(dts[5], dts[4], ACT.Ln).then_inc(s_dta, 1)
            act.wait_ge(s_decp, 1)
            nc.scalar.activation(dec_t[:, :], ps[:, 6, 0:2 * TT * H_SSD], ACT.Exp).then_inc(s_dec, 1)

            def squares(c):
                act.wait_ge(s_yg, c + 1)
                if c >= 2:
                    act.wait_ge(s_ss, c - 1)
                nc.scalar.activation(sq[:, c % 2].rearrange("p (h l) -> p h l", h=H_SSD),
                                     yg[:, :, c * P:(c + 1) * P], ACT.Square).then_inc(s_sq, 1)

            for c in range(TT):
                b = c % 2
                act.wait_ge(s_front_tr, c + 1)
                if c >= 2:
                    act.wait_ge(s_st, c - 1)
                nc.scalar.copy(tok[:, b], ps[:, 0, 0:2 * P]).then_inc(s_tok, 1)
                act.wait_ge(s_front_seg, c + 1)
                nc.scalar.activation(decays[:, b], ps[:, 2, :], ACT.Exp).then_inc(s_exp, 1)
                if c >= 1:
                    squares(c - 1)
            squares(TT - 1)
            feature_major(PH_FFN, C_LN2)
            for q in range(GROUPS * FB):
                act.wait_ge(s_gu, q + 1)
                if q >= 2:
                    act.wait_ge(s_fa, q - 1)
                nc.scalar.activation(sgate[q % 2], ps[:, 2 + q % 2, :], ACT.Silu).then_inc(s_sg, 1)
            feature_major(PH_FAC)
            feature_major(PH_ATT)
            for q in range(0, GROUPS * 12, 2):
                act.wait_ge(s_qkv, q + 1)
                dst, scale = qkv_dst(q)
                nc.scalar.activation(dst, ps[:, 2 + q % 6, :], ACT.Copy, scale=scale).then_inc(s_qa, 1)

            def attend(u):
                i, n = divmod(u, HEADS)
                w = (i + 1) * P
                act.wait_ge(s_max, u + 1)
                if u >= 3:
                    act.wait_ge(s_pt, u - 2)
                src = ps[:, 2 * (u % 2):2 * (u % 2) + 2, :].rearrange("p a b -> p (a b)")[:, 0:w]
                nc.scalar.activation(probs[:, u % 3, 0:w], src, ACT.Exp, bias=nmax[:, u:u + 1],
                                     accum_out=psums[:, u:u + 1]).then_inc(s_pr, 1)

            def second_half(u):
                i, n = divmod(u, HEADS)
                if i >= 4:
                    act.wait_ge(s_pt, u + 1)
                    if u >= 2:
                        act.wait_ge(s_pv, u - 1)
                    nc.scalar.copy(pT[:, u % 2, 512:(i + 1) * P], ps[:, 5, 0:(i - 3) * P]).then_inc(s_pta, 1)

            def z_feature_major(i):
                act.wait_ge(s_zt, i + 1)
                nc.scalar.copy(zT.rearrange("p a b -> p (a b)"), ps[:, 6 + i % 2, :]).then_inc(s_zT, 1)

            for u in range(TT * HEADS + 4):
                if u < TT * HEADS:
                    attend(u)
                if 2 <= u < TT * HEADS + 2:
                    second_half(u - 2)
                if u >= HEADS and u % HEADS == 3:
                    z_feature_major(u // HEADS - 1)
            feature_major(PH_MOE)
            act.wait_ge(s_rv, 1)
            nc.scalar.activation(rt[1], rt[0], ACT.Exp).then_inc(s_ra, 1)

            def expert_silu(i):
                act.wait_ge(s_eg, i + 1)
                act.wait_ge(s_ea, i)
                nc.scalar.activation(eg, ps[:, 0:2, 0:IH], ACT.Silu).then_inc(s_esg, 1)

            def expert_aT(i, b):
                act.wait_ge(s_eat, i + 1)
                nc.scalar.copy(eaT[:, b, 0:4, :].rearrange("p a b -> p (a b)"), ps[:, 4, :]).then_inc(s_eaa, 1)

            def expert_y(i, b, first=False):
                act.wait_ge(s_ey, i + 1)
                if not first:
                    act.wait_ge(s_eys[b], 8 * (i - b))
                nc.scalar.copy(ey[:, b], ps[:, 6, 0:D]).then_inc(s_eyc, 1)
                act.wait_ge(s_eyc, i + 1)
                act.dma_start(slots_out[bass.ts(i, P), :], ey[:, b]).then_inc(s_eys[b], 16)

            act.wait_ge(s_eg, 1)
            nc.scalar.activation(eg, ps[:, 0:2, 0:IH], ACT.Silu).then_inc(s_esg, 1)
            for i in range(2):
                expert_aT(i, i)
                expert_silu(i + 1)
                expert_y(i, i, first=True)
            with act.Fori(1, LAST // 2) as j:
                for b in range(2):
                    expert_aT(2 * j + b, b)
                    expert_silu(2 * j + b + 1)
                    expert_y(2 * j + b, b)
            expert_aT(LAST, 0)
            expert_y(LAST, 0)

        @block.vector
        def _(dve):
            n_dve = [0]

            def link(ins):
                n_dve[0] += 1
                ins.then_inc(s_dve, 1)
                dve.wait_ge(s_dve, n_dve[0])

            V = nc.vector

            def variances(ph, src, g):
                for t in range(g * GT, (g + 1) * GT):
                    if ph == PH_FFN:
                        dve.wait_ge(s_r2, t + 1)
                    elif ph == PH_FAC:
                        dve.wait_ge(s_x1, t + 1)
                    elif ph == PH_ATT:
                        dve.wait_ge(s_x2, t + 1)
                    elif ph == PH_MOE:
                        dve.wait_ge(s_x3, t + 1)
                    ins = V.bn_stats(stats[:, t, :], src[:, t, :])
                link(ins)
                for t in range(g * GT, (g + 1) * GT):
                    ins = V.bn_aggr(mv[:, t, :], stats[:, t, :])
                link(ins)
                c = slice(g * GT, (g + 1) * GT)
                if ph == PH_FFN:
                    link(V.tensor_tensor(veps2[:, c], mv[:, c, 0], mv[:, c, 0], ALU.mult))
                    V.scalar_tensor_tensor(veps[:, c], mv[:, c, 1], EPS, veps2[:, c], ALU.add,
                                           ALU.add).then_inc(s_var, 1)
                else:
                    V.tensor_scalar(veps[:, c], mv[:, c, 1], EPS, None, ALU.add).then_inc(s_var, 1)

            def normalise(ph, src, g):
                dve.wait_ge(s_rstd, GROUPS * ph + g + 1)
                for t in range(g * GT, (g + 1) * GT):
                    if ph > 0:
                        dve.wait_ge(s_tr, GROUPS * (ph - 1) + g + 1)
                    if ph == PH_FFN:
                        V.tensor_scalar(hh[:, t, :], src[:, t, :], rstd[:, t:t + 1], None,
                                        ALU.mult).then_inc(s_hh, 1)
                    else:
                        V.tensor_scalar(hh[:, t, :], src[:, t, :], mv[:, t, 0:1], rstd[:, t:t + 1],
                                        ALU.subtract, ALU.mult).then_inc(s_hh, 1)

            dve.wait_ge(s_const, 16)
            V.tensor_copy(ident_b[:, :], ident)
            for h in range(H_SSD):
                V.tensor_copy(neg_s[:, h * P:(h + 1) * P], cst[:, C_NEGS:C_NEGS + P])
            V.tensor_copy(neg_a[:, :], cst[:, C_NEGA:C_NEGA + P]).then_inc(s_cbf, 1)

            for g in range(GROUPS):
                dve.wait_ge(s_x[g], 16)
                variances(PH_MIX, x, g)
            for g in range(GROUPS):
                c = slice(g * GT, (g + 1) * GT)
                dve.wait_ge(s_rstd, g + 1)
                link(V.tensor_tensor(veps2[:, c], rstd[:, c], rstd[:, c], ALU.mult))
                link(V.tensor_tensor(veps2[:, c], veps2[:, c], mv[:, c, 1], ALU.mult))
                V.tensor_scalar(veps2[:, c], veps2[:, c], EPS, None, ALU.add).then_inc(s_var2, 1)
                for t in range(g * GT, (g + 1) * GT):
                    V.tensor_scalar(xn[:, t, :], x[:, t, :], mv[:, t, 0:1], rstd[:, t:t + 1],
                                    ALU.subtract, ALU.mult)
                dve.wait_ge(s_rstd2, g + 1)
                link(V.tensor_tensor(rstd2[:, c], rstd2[:, c], rstd[:, c], ALU.mult))
                for t in range(g * GT, (g + 1) * GT):
                    V.tensor_scalar(hh[:, t, :], x[:, t, :], mv[:, t, 0:1], rstd2[:, t:t + 1],
                                    ALU.subtract, ALU.mult).then_inc(s_hh, 1)

            dve.wait_ge(s_small, 16)
            dve.wait_ge(s_mixw, 16)
            for k in range(KD):
                V.tensor_scalar(wout_sb[:, k, :], wout_sb[:, k, :], small[:, C_NORM + k:C_NORM + k + 1], None,
                                ALU.mult).then_inc(s_wn, 1)

            def row(c):
                return small[:, c:c + H_SSD].unsqueeze(1).broadcast_to([P, TT, H_SSD])

            dve.wait_ge(s_dtp, 1)
            link(V.tensor_tensor(dts[6], ps[:, 6, 64:64 + TT * H_SSD].rearrange("p (t h) -> p t h", h=H_SSD),
                                 row(C_DTB), ALU.add))
            V.scalar_tensor_tensor(dts_t[:, 48:64], dts_t[:, 96:112], -1.0, dts_t[:, 96:112], ALU.mult,
                                   ALU.min).then_inc(s_dtv, 1)

            n = 0
            for g in range(GROUPS):
                dve.wait_ge(s_evac, g * 6 + 6)
                for k in range(TAPS - 1):
                    for c in range(CONV_BLOCKS):
                        if k:
                            dve.wait_ge(s_conv, n - CONV_BLOCKS + 1)
                        a = cv[:, c, g * GW:(g + 1) * GW]
                        V.scalar_tensor_tensor(a, xpad[:, c, k + g * GW:k + (g + 1) * GW],
                                               small[:, C_CONVW + 4 * c + k:C_CONVW + 4 * c + k + 1], a,
                                               ALU.mult, ALU.add).then_inc(s_conv, 1)
                        n += 1

            dve.wait_ge(s_dta, 1)
            V.tensor_scalar(dts[4], dts[3], 1.0, None, ALU.add).then_inc(s_dtv, 1)
            dve.wait_ge(s_dtv, 2)
            link(V.tensor_scalar(dts[7], dts[4], -1.0, None, ALU.add))
            link(V.tensor_scalar(dts[8], dts[7], 0.0, None, ALU.is_equal))
            link(V.tensor_tensor(dts[7], dts[7], dts[8], ALU.add))
            link(V.reciprocal(dts[9], dts[7]))
            dve.wait_ge(s_dta, 3)
            link(V.tensor_tensor(dts[9], dts[9], dts[5], ALU.mult))
            link(V.tensor_tensor(dts[9], dts[9], dts[8], ALU.add))
            link(V.tensor_tensor(dts[9], dts[9], dts[3], ALU.mult))
            V.scalar_tensor_tensor(dts_t[:, 0:16], dts_t[:, 96:112], 0.0, dts_t[:, 144:160], ALU.max,
                                   ALU.add).then_inc(s_dtv, 1)
            dve.wait_ge(s_dtv, 3)
            link(V.tensor_scalar(ea_log[:, :], ea_log[:, :], -1.0, None, ALU.mult))
            V.tensor_tensor(dts[1], dts[0], ea_log[:, :].unsqueeze(1).broadcast_to([P, TT, H_SSD]),
                            ALU.mult).then_inc(s_dtv, 1)
            dve.wait_ge(s_dec, 1)
            V.tensor_tensor(dts[2], dec[:, 0], dts[0], ALU.mult).then_inc(s_dd, 1)

            def masked(c):
                b = c % 2
                dve.wait_ge(s_front_g, c + 1)
                dve.wait_ge(s_exp, c + 1)
                if c >= 2:
                    dve.wait_ge(s_y, c - 1)
                for h in range(H_SSD):
                    last = V.scalar_tensor_tensor(
                        mt[:, b, h * P:(h + 1) * P], ps[:, 1, h * P:(h + 1) * P], dts[0][:, c, h:h + 1],
                        decays[:, b, h * P:(h + 1) * P], ALU.mult, ALU.mult)
                last.then_inc(s_mt, 1)

            masked(0)
            for c in range(TT):
                b = c % 2
                if c < TT - 1:
                    masked(c + 1)
                    dve.wait_ge(s_st, c + 1)
                    for h in range(H_SSD):
                        if c == 0:
                            last = V.tensor_copy(state[:, 1, h], ps[:, 5, h * P:(h + 1) * P])
                        else:
                            dve.wait_ge(s_state, c)
                            last = V.scalar_tensor_tensor(state[:, 1 - b, h], state[:, b, h], dec[:, 1, c, h:h + 1],
                                                          ps[:, 5, h * P:(h + 1) * P], ALU.mult, ALU.add)
                    last.then_inc(s_state, 1)
                dve.wait_ge(s_y, c + 1)
                for h in range(H_SSD):
                    ins = V.scalar_tensor_tensor(
                        yg[:, h, c * P:(c + 1) * P], cv[:, 0, c * P:(c + 1) * P], small[:, C_D + h:C_D + h + 1],
                        ps[:, 3 + b, h * P:(h + 1) * P], ALU.mult, ALU.add)
                link(ins)
                V.tensor_tensor(yg[:, :, c * P:(c + 1) * P], yg[:, :, c * P:(c + 1) * P],
                                zs[:, :, c * P:(c + 1) * P], ALU.mult).then_inc(s_yg, 1)
            dve.wait_ge(s_ss, TT)
            V.tensor_scalar(veps2[:, :], ps[:, 7, 0:TT], 1.0 / D, EPS, ALU.mult, ALU.add).then_inc(s_yv, 1)
            dve.wait_ge(s_yr, 1)
            for t in range(TT):
                dve.wait_ge(s_mo, t + 1)
                V.scalar_tensor_tensor(xn[:, t, :], ps[:, t % 2, 0:D], rstd2[:, t:t + 1], xn[:, t, :],
                                       ALU.mult, ALU.add).then_inc(s_r2, 1)
            for g in range(GROUPS):
                variances(PH_FFN, xn, g)
            for g in range(GROUPS):
                normalise(PH_FFN, xn, g)
            for g in range(GROUPS):
                for f in range(FB):
                    q = g * FB + f
                    dve.wait_ge(s_sg, q + 1)
                    V.tensor_tensor(ffn_a[g][:, f, :], sgate[q % 2], ps[:, 4 + q % 2, :],
                                    ALU.mult).then_inc(s_fa, 1)
                for t in range(g * GT, (g + 1) * GT):
                    dve.wait_ge(s_fo, t + 1)
                    dve.wait_ge(s_xr, t + 1)
                    V.tensor_tensor(x[:, t, :], x[:, t, :], ps[:, 6 + t % 2, 0:D], ALU.add).then_inc(s_x1, 1)
            for g in range(GROUPS):
                variances(PH_FAC, x, g)
            for g in range(GROUPS):
                normalise(PH_FAC, x, g)
            for t in range(TT):
                dve.wait_ge(s_mx, t + 1)
                dve.wait_ge(s_xb, t + 1)
                V.tensor_tensor(x[:, t, :], x[:, t, :], ps[:, 6 + t % 2, 0:D], ALU.add).then_inc(s_x2, 1)
            for g in range(GROUPS):
                variances(PH_ATT, x, g)
            for g in range(GROUPS):
                normalise(PH_ATT, x, g)
            for q in range(1, GROUPS * 12, 2):
                dve.wait_ge(s_qkv, q + 1)
                dst, scale = qkv_dst(q)
                V.tensor_scalar(dst, ps[:, 2 + q % 6, :], scale, None, ALU.mult).then_inc(s_qd, 1)

            def row_max(u):
                w = (u // HEADS + 1) * P
                dve.wait_ge(s_sc, u + 1)
                src = ps[:, 2 * (u % 2):2 * (u % 2) + 2, :].rearrange("p a b -> p (a b)")[:, 0:w]
                V.tensor_reduce(nmax[:, u:u + 1], src, AX_X, ALU.max, negate=True).then_inc(s_max, 1)

            def first_half(u):
                w = min(u // HEADS + 1, 4) * P
                dve.wait_ge(s_pt, u + 1)
                if u >= 2:
                    dve.wait_ge(s_pv, u - 1)
                V.tensor_copy(pT[:, u % 2, 0:w], ps[:, 4, 0:w]).then_inc(s_ptd, 1)

            def z_normalise(i):
                dve.wait_ge(s_pr, HEADS * (i + 1))
                link(V.reciprocal(pinv[:, i * HEADS:(i + 1) * HEADS], psums[:, i * HEADS:(i + 1) * HEADS]))
                dve.wait_ge(s_pv, HEADS * (i + 1))
                if i >= 1:
                    dve.wait_ge(s_zt, i)
                V.tensor_tensor(zn.rearrange("p (n d) -> p n d", n=HEADS),
                                ps[:, 6 + i % 2, :].rearrange("p (n d) -> p n d", n=HEADS),
                                pinv[:, i * HEADS:(i + 1) * HEADS].unsqueeze(2).broadcast_to([P, HEADS, DH]),
                                ALU.mult).then_inc(s_zn, 1)

            def add_attention(i):
                dve.wait_ge(s_ao, i + 1)
                V.tensor_tensor(x[:, i, :], x[:, i, :], ps[:, 6 + i % 2, 0:D], ALU.add).then_inc(s_x3, 1)

            for u in range(TT * HEADS + 6):
                if u < TT * HEADS:
                    row_max(u)
                if 2 <= u < TT * HEADS + 2:
                    first_half(u - 2)
                if u >= HEADS and u % HEADS == 2:
                    z_normalise(u // HEADS - 1)
                if u >= HEADS and u % HEADS == 5:
                    add_attention(u // HEADS - 1)
            for g in range(GROUPS):
                variances(PH_MOE, x, g)
            for g in range(GROUPS):
                normalise(PH_MOE, x, g)

            dve.wait_ge(s_lg, 1)
            logits = ps[:, 2, 0:TT * E].rearrange("p (t e) -> p t e", e=E)

            def over_e(a):
                return a.unsqueeze(2).broadcast_to([P, TT, E])

            link(V.tensor_reduce(rs[0], logits, AX_X, ALU.max))
            V.tensor_tensor(rt[0], logits, over_e(rs[0]), ALU.subtract).then_inc(s_rv, 1)
            dve.wait_ge(s_ra, 1)
            link(V.tensor_reduce(rs[1], rt[1], AX_X, ALU.add))
            link(V.reciprocal(rs[2], rs[1]))
            link(V.tensor_tensor(rt[1], rt[1], over_e(rs[2]), ALU.mult))
            for t in range(TT):
                ins = V.max(rt[2][:, t, :], rt[1][:, t, :])
            link(ins)
            for t in range(TT):
                ins = V.max_index(top_i[:, t, :], rt[2][:, t, :], rt[1][:, t, :])
            link(ins)
            iota_e = iota[:, 0:E].unsqueeze(1).broadcast_to([P, TT, E])
            for k in range(TOP):
                V.tensor_copy(rs[3 + k], top_i[:, :, k])
            link(V.tensor_tensor(rs[5], rt[2][:, :, 0], rt[2][:, :, 1], ALU.add))
            for k in range(TOP):
                ins = V.tensor_tensor(rt[3 + k], iota_e, over_e(rs[3 + k]), ALU.is_equal)
            link(ins)
            V.tensor_tensor(rt[5], rt[3], rt[4], ALU.add).then_inc(s_rv, 1)
            link(V.reciprocal(rs[6], rs[5]))
            for k in range(TOP):
                V.tensor_tensor(rs[7 + k], rt[2][:, :, k], rs[6], ALU.mult)
            dve.wait_ge(s_cnt, 1)
            before = ps[:, 3, 0:TT * E].rearrange("p (t e) -> p t e", e=E)
            totals = ps[:, 3, TT * E:2 * TT * E].rearrange("p (t e) -> p t e", e=E)
            link(V.memset(rt[6][:, 0, :], 0.0))
            for t in range(1, TT):
                link(V.tensor_tensor(rt[6][:, t, :], rt[6][:, t - 1, :], totals[:, t - 1, :], ALU.add))
            link(V.tensor_tensor(rs[9], rt[6][:, TT - 1, :], totals[:, TT - 1, :], ALU.add))
            link(V.tensor_scalar(rs[10], iota[:, 0:E], float(P), None, ALU.mult))
            link(V.tensor_tensor(rt[7], rs[9].unsqueeze(2).broadcast_to([P, E, TT]),
                                 rs[10].unsqueeze(1).broadcast_to([P, E, TT]), ALU.is_gt))
            link(V.tensor_reduce(rs[9], rt[7], AX_X, ALU.add))
            link(V.tensor_tensor_scan(rs[10], cst[:, C_ONES:C_ONES + E], rs[9], 0.0, ALU.mult, ALU.add))
            link(V.tensor_tensor(rs[9], rs[10], rs[9], ALU.subtract))
            link(V.tensor_scalar(rs[9], rs[9], float(P), None, ALU.mult))
            link(V.tensor_tensor(rt[6], rt[6], rs[9].unsqueeze(1).broadcast_to([P, TT, E]), ALU.add))
            link(V.tensor_tensor(rt[6], rt[6], before, ALU.add))
            for k in range(TOP):
                link(V.tensor_tensor(rt[7], rt[3 + k], rt[6], ALU.mult))
                link(V.tensor_reduce(rs[3 + k], rt[7], AX_X, ALU.add))
            for k in range(TOP):
                ins = V.tensor_copy(slot_i[:, k, :], rs[3 + k])
            ins.then_inc(s_slots, 1)
            link(V.tensor_tensor(ecmp, iota.unsqueeze(2).broadcast_to([P, 24, E]),
                                 rs[10].unsqueeze(1).broadcast_to([P, 24, E]), ALU.is_ge))
            link(V.tensor_reduce(eid_f[:, :], ecmp, AX_X, ALU.add))
            V.tensor_scalar(eid[:, :], eid_f[:, :], float(E - 1), None, ALU.min).then_inc(s_slots, 1)

            def expert_act(i, b):
                dve.wait_ge(s_esg, i + 1)
                dve.wait_ge(s_eu, i + 1)
                V.tensor_tensor(ea[:, b].rearrange("p (a c) -> p a c", a=2), eg, ps[:, 2:4, 0:IH],
                                ALU.mult).then_inc(s_ea, 1)

            def expert_xT(i, b):
                dve.wait_ge(s_ext, i + 1)
                V.tensor_copy(xsT[:, b].rearrange("p a b -> p (a b)"), ps[:, 7, 0:D]).then_inc(s_exT, 1)

            def expert_aT(i, b):
                dve.wait_ge(s_eat, i + 1)
                V.tensor_copy(eaT[:, b, 4, :], ps[:, 5, 0:P])
                V.tensor_copy(eaT[0:ILAST, b, 5, :], ps[0:ILAST, 5, P:2 * P]).then_inc(s_ead, 1)

            expert_xT(0, 0)
            expert_xT(1, 1)
            expert_act(0, 0)
            with dve.Fori(0, LAST // 2 - 1) as j:
                for b in range(2):
                    expert_xT(2 * j + b + 2, b)
                    expert_aT(2 * j + b, b)
                    expert_act(2 * j + b + 1, 1 - b)
            expert_xT(LAST, 0)
            expert_aT(LAST - 2, 0)
            expert_act(LAST - 1, 1)
            expert_aT(LAST - 1, 1)
            expert_act(LAST, 0)
            expert_aT(LAST, 0)
            for t in range(TT):
                dve.wait_ge(s_gath, TOP * TT * 16)
                link(V.scalar_tensor_tensor(x[:, t, :], xn[:, t, :], rs[7][:, t:t + 1], x[:, t, :],
                                            ALU.mult, ALU.add))
                V.scalar_tensor_tensor(x[:, t, :], hh[:, t, :], rs[8][:, t:t + 1], x[:, t, :],
                                       ALU.mult, ALU.add).then_inc(s_fin, 1)

        @block.tensor
        def _(pe):
            mm = nc.tensor.matmul

            def transposes(ph):
                for g in range(GROUPS):
                    if ph or g:
                        pe.wait_ge(s_hT, GROUPS * ph + g)
                    for t in range(g * GT, (g + 1) * GT):
                        pe.wait_ge(s_hh, TT * ph + t + 1)
                        for k in range(KD):
                            last = nc.tensor.transpose(ps[:, k, (t % GT) * P:(t % GT + 1) * P],
                                                       hh[:, t, k * P:(k + 1) * P], ident)
                    last.then_inc(s_tr, 1)

            pe.wait_ge(s_const, 16)
            transposes(PH_MIX)
            pe.wait_ge(s_win, 16)
            for g in range(GROUPS):
                pe.wait_ge(s_hT, g + 1)
                for fb in range(6):
                    q = g * 6 + fb
                    if q >= 4:
                        pe.wait_ge(s_evac, q - 3)
                    for k in range(KD):
                        last = mm(ps[:, 2 + q % 4, :], win_sb[:, k, fb * P:(fb + 1) * P],
                                  hT[:, k, g * GW:(g + 1) * GW], start=(k == 0), stop=(k == KD - 1))
                    last.then_inc(s_proj, 1)
                for t in range(g * GT, (g + 1) * GT):
                    for k in range(KD):
                        last = mm(ps[:, 6, 64 + H_SSD * t:64 + H_SSD * (t + 1)], hT[:, k, t * P:(t + 1) * P],
                                  win_sb[:, k, 6 * P:], start=(k == 0), stop=(k == KD - 1))
            last.then_inc(s_dtp, 1)
            pe.wait_ge(s_dtv, 4)
            da = dts_t[:, 16:32]
            mm(ps[:, 6, 0:16], gt_m, da, start=True, stop=True)
            mm(ps[:, 6, 16:32], ones, da, start=True, stop=True).then_inc(s_decp, 1)

            def front(c):
                cols = slice(c * P, (c + 1) * P)
                if c == 0:
                    pe.wait_ge(s_cbf, 1)
                if c in (0, GT):
                    pe.wait_ge(s_xbc, (c // GT + 1) * CONV_BLOCKS)
                if c >= 1:
                    pe.wait_ge(s_tok, c)
                for k in range(2):
                    last = nc.tensor.transpose(ps[:, 0, k * P:(k + 1) * P], cv[:, k, cols], ident)
                last.then_inc(s_front_tr, 1)
                pe.wait_ge(s_ramp, c + 1)
                if c >= 1:
                    pe.wait_ge(s_exp, c)
                rmp = ramp[:, c % 2]
                mm(ps[:, 2, 0:2 * P], gt_m, rmp, start=True, stop=False)
                mm(ps[:, 2, 0:2 * P], ident_b[:, :], neg_s[:, :], start=False, stop=True)
                mm(ps[:, 2, 2 * P:4 * P], ones, rmp, start=True, stop=True).then_inc(s_front_seg, 1)
                if c >= 1:
                    pe.wait_ge(s_mt, c)
                mm(ps[:, 1, 0:2 * P], cv[:, 1, cols], cv[:, 2:4, cols], start=True, stop=True).then_inc(s_front_g, 1)

            def back(c):
                b = c % 2
                if c >= 1:
                    pe.wait_ge(s_state, c)
                if c < TT - 1:
                    pe.wait_ge(s_ddx, c + 1)
                    mm(ps[:, 5, 0:2 * P], tok[:, b, P:2 * P], ddx[:, b], start=True, stop=True).then_inc(s_st, 1)
                pe.wait_ge(s_mt, c + 1)
                if c >= 2:
                    pe.wait_ge(s_yg, c - 1)
                last = mm(ps[:, 3 + b, 0:2 * P], tok[:, b, 0:P], mt[:, b], start=True, stop=(c == 0))
                if c:
                    pe.wait_ge(s_ce, c)
                    for h in range(H_SSD):
                        last = mm(ps[:, 3 + b, h * P:(h + 1) * P], state[:, b, h], ce[:, b, h * P:(h + 1) * P],
                                  start=False, stop=(h == 1))
                last.then_inc(s_y, 1)

            def square_sum(c):
                pe.wait_ge(s_sq, c + 1)
                for h in range(H_SSD):
                    last = mm(ps[:, 7, c:c + 1], sq[:, c % 2, h * P:(h + 1) * P], ones[:, 0:1],
                              start=(h == 0), stop=(h == 1))
                last.then_inc(s_ss, 1)

            front(0)
            for c in range(TT):
                if c < TT - 1:
                    front(c + 1)
                back(c)
                if c:
                    square_sum(c - 1)
            square_sum(TT - 1)
            pe.wait_ge(s_wn, KD)
            for t in range(TT):
                if t >= 2:
                    pe.wait_ge(s_r2, t - 1)
                for k in range(KD):
                    last = mm(ps[:, t % 2, 0:D], yg[:, k, t * P:(t + 1) * P], wout_sb[:, k, :],
                              start=(k == 0), stop=(k == KD - 1))
                last.then_inc(s_mo, 1)
            pe.wait_ge(s_r2, TT)
            transposes(PH_FFN)
            pe.wait_ge(s_ffnw, 32)
            for g in range(GROUPS):
                pe.wait_ge(s_hT, GROUPS * PH_FFN + g + 1)
                for f in range(FB):
                    q = g * FB + f
                    if q >= 2:
                        pe.wait_ge(s_fa, q - 1)
                    for w in range(2):
                        for k in range(KD):
                            last = mm(ps[:, 2 + 2 * w + q % 2, :], fw13[:, w, k, f * P:(f + 1) * P],
                                      hT[:, k, g * GW:(g + 1) * GW], start=(k == 0), stop=(k == KD - 1))
                    last.then_inc(s_gu, 1)
                for t in range(g * GT, (g + 1) * GT):
                    if t >= 2:
                        pe.wait_ge(s_x1, t - 1)
                    pe.wait_ge(s_fa, (g + 1) * FB)
                    for f in range(FB):
                        last = mm(ps[:, 6 + t % 2, 0:D], ffn_a[g][:, f, (t % GT) * P:(t % GT + 1) * P],
                                  fw2[:, f, :], start=(f == 0), stop=(f == FB - 1))
                    last.then_inc(s_fo, 1)
            transposes(PH_FAC)
            pe.wait_ge(s_fsum, 1)
            for t in range(TT):
                if t % GT == 0:
                    pe.wait_ge(s_hT, GROUPS * PH_FAC + t // GT + 1)
                pe.wait_ge(s_x1, TT)
                if t >= 2:
                    pe.wait_ge(s_x2, t - 1)
                for k in range(KD):
                    last = mm(ps[:, 6 + t % 2, 0:D], hT[:, k, t * P:(t + 1) * P], mixed_w[:, k, :],
                              start=(k == 0), stop=(k == KD - 1))
                last.then_inc(s_mx, 1)
            transposes(PH_ATT)
            pe.wait_ge(s_wqsum, 1)
            pe.wait_ge(s_kv, 32)
            pe.wait_ge(s_x2, TT)
            for q in range(GROUPS * 12):
                g, j = divmod(q, 12)
                if j == 0:
                    pe.wait_ge(s_hT, GROUPS * PH_ATT + g + 1)
                if q >= 6:
                    pe.wait_ge(s_qd if q % 2 else s_qa, (q - 6) // 2 + 1)
                for k in range(KD):
                    bank = ps[:, 2 + q % 6, :]
                    if j < 8:
                        w = wq_sum if j < 4 else wk_sb
                        last = mm(bank, w[:, k, (j % 4) * P:(j % 4 + 1) * P], hT[:, k, g * GW:(g + 1) * GW],
                                  start=(k == 0), stop=(k == KD - 1))
                    else:
                        t = g * GT + j - 8
                        last = mm(bank, hT[:, k, t * P:(t + 1) * P], wv_sb[:, k, :],
                                  start=(k == 0), stop=(k == KD - 1))
                last.then_inc(s_qkv, 1)
            pe.wait_ge(s_qa, GROUPS * 6)
            pe.wait_ge(s_qd, GROUPS * 6)

            def scores(u):
                i, n = divmod(u, HEADS)
                half = slice(64 * (n % 2), 64 * (n % 2) + 64)
                if u >= 2:
                    pe.wait_ge(s_pr, u - 1)
                for a in range(i // 4 + 1):
                    w = min((i + 1) * P - a * 512, 512)
                    mm(ps[:, 2 * (u % 2) + a, 0:w], qT[half, n // 2, i * P:(i + 1) * P],
                       kT[half, n // 2, a * 512:a * 512 + w], start=True, stop=(a < i // 4))
                c = (i % 4) * P
                mm(ps[:, 2 * (u % 2) + i // 4, c:c + P], ident_b[:, :], neg_a[:, :],
                   start=False, stop=True).then_inc(s_sc, 1)

            def probs_transposed(u):
                i, n = divmod(u, HEADS)
                pe.wait_ge(s_pr, u + 1)
                if u >= 1:
                    pe.wait_ge(s_ptd, u)
                    if u - 1 >= 4 * HEADS:
                        pe.wait_ge(s_pta, u - 4 * HEADS)
                for j in range(i + 1):
                    last = nc.tensor.transpose(ps[:, 4 + j // 4, (j % 4) * P:(j % 4 + 1) * P],
                                               probs[:, u % 3, j * P:(j + 1) * P], ident)
                last.then_inc(s_pt, 1)

            def attended(u):
                i, n = divmod(u, HEADS)
                pe.wait_ge(s_ptd, u + 1)
                if i >= 4:
                    pe.wait_ge(s_pta, u + 1 - 4 * HEADS)
                if n == 0 and i >= 2:
                    pe.wait_ge(s_x3, i - 1)
                for j in range(i + 1):
                    last = mm(ps[:, 6 + i % 2, n * DH:(n + 1) * DH], pT[:, u % 2, j * P:(j + 1) * P],
                              v_sb[:, j, n * DH:(n + 1) * DH], start=(j == 0), stop=(j == i))
                last.then_inc(s_pv, 1)

            def z_transposed(i):
                pe.wait_ge(s_zn, i + 1)
                for c in range(QB):
                    last = nc.tensor.transpose(ps[:, 6 + i % 2, c * P:(c + 1) * P], zn[:, c * P:(c + 1) * P], ident)
                last.then_inc(s_zt, 1)

            def attention_out(i):
                pe.wait_ge(s_zT, i + 1)
                for c in range(QB):
                    last = mm(ps[:, 6 + i % 2, 0:D], zT[:, c, :], wo_sb[:, c, :], start=(c == 0), stop=(c == QB - 1))
                last.then_inc(s_ao, 1)

            pe.wait_ge(s_wo, 16)
            for u in range(TT * HEADS + 6):
                if u < TT * HEADS:
                    scores(u)
                if 2 <= u < TT * HEADS + 2:
                    probs_transposed(u - 2)
                if u >= HEADS and u % HEADS == 3:
                    z_transposed(u // HEADS - 1)
                if u >= HEADS and u % HEADS == 5:
                    attention_out(u // HEADS - 1)
                if 3 <= u < TT * HEADS + 3:
                    attended(u - 3)
            transposes(PH_MOE)
            pe.wait_ge(s_gate, 32)
            for t in range(TT):
                if t % GT == 0:
                    pe.wait_ge(s_hT, GROUPS * PH_MOE + t // GT + 1)
                for k in range(KD):
                    last = mm(ps[:, 2, t * E:(t + 1) * E], hT[:, k, t * P:(t + 1) * P], gate_sb[:, k, :],
                              start=(k == 0), stop=(k == KD - 1))
            last.then_inc(s_lg, 1)
            pe.wait_ge(s_rv, 2)
            chosen = rt_t[:, 5 * TT * E:6 * TT * E]
            mm(ps[:, 3, 0:TT * E], lt_m, chosen, start=True, stop=True)
            mm(ps[:, 3, TT * E:2 * TT * E], ones, chosen, start=True, stop=True).then_inc(s_cnt, 1)

            def expert_x(i, b):
                pe.wait_ge(s_xs[b], 8 * (i - b) + 16)
                for k in range(KD):
                    last = nc.tensor.transpose(ps[:, 7, k * P:(k + 1) * P], xs[:, b, k * P:(k + 1) * P], ident)
                last.then_inc(s_ext, 1)

            def expert_up(i, b):
                e = nc.tensor.value_load(eid[0:1, bass.ds(i, 1)], min_val=0, max_val=E - 1)
                pe.wait_ge(s_exT, i + 1)
                for w, (weights, done) in enumerate(((ew1, s_eg), (ew3, s_eu))):
                    we = weights[:, bass.ds(e, 1), :].rearrange("p e (k n) -> p (e k) n", k=KD)
                    for k in range(KD):
                        for a in range(2):
                            last = mm(ps[:, 2 * w + a, 0:IH], xsT[:, b, k, :], we[:, k, a * IH:(a + 1) * IH],
                                      start=(k == 0), stop=(k == KD - 1))
                    last.then_inc(done, 1)
                return e

            def expert_aT(i, b):
                pe.wait_ge(s_ea, i + 1)
                for c in range(IB):
                    w = min(P, I - c * P)
                    last = nc.tensor.transpose(ps[0:w, 4 + c // 4, (c % 4) * P:(c % 4 + 1) * P],
                                               ea[:, b, c * P:c * P + w], ident)
                last.then_inc(s_eat, 1)

            def expert_down(i, b, first=False):
                e = nc.tensor.value_load(eid[0:1, bass.ds(i, 1)], min_val=0, max_val=E - 1)
                pe.wait_ge(s_eaa, i + 1)
                pe.wait_ge(s_ead, i + 1)
                if not first:
                    pe.wait_ge(s_eyc, i)
                we = ew2[:, bass.ds(e, 1), :].rearrange("p e (c n) -> p (e c) n", c=IB)
                for c in range(IB):
                    w = min(P, I - c * P)
                    last = mm(ps[:, 6, 0:D], eaT[0:w, b, c, :], we[0:w, c, :], start=(c == 0), stop=(c == IB - 1))
                last.then_inc(s_ey, 1)

            pe.wait_ge(s_e13, 2 * E * 16)
            pe.wait_ge(s_slots, 2)
            expert_x(0, 0)
            pe.wait_ge(s_exT, 1)
            expert_x(1, 1)
            expert_up(0, 0)
            pe.wait_ge(s_e2, (E + 1) * 16)

            def body(i, b, first=False):
                pe.wait_ge(s_exT, i + 2)
                expert_x(i + 2, b)
                expert_aT(i, b)
                expert_up(i + 1, 1 - b)
                expert_down(i, b, first)

            body(0, 0, first=True)
            body(1, 1)
            with pe.Fori(1, LAST // 2 - 1) as j:
                for b in range(2):
                    body(2 * j + b, b)
            body(LAST - 2, 0)
            expert_aT(LAST - 1, 1)
            expert_up(LAST, 0)
            expert_down(LAST - 1, 1)
            expert_aT(LAST, 0)
            expert_down(LAST, 0)


def constants():
    c = np.zeros((P, N_CONST), np.float32)
    r = np.arange(P)
    c[:, C_IDENT:C_IDENT + P] = np.eye(P)
    c[:, C_LE:C_LE + P] = r[:, None] <= r[None, :]
    c[:, C_GT:C_GT + P] = r[:, None] > r[None, :]
    c[:, C_LT:C_LT + P] = r[:, None] < r[None, :]
    c[:, C_ONES:C_ONES + P] = 1.0
    c[:, C_NEGS:C_NEGS + P] = np.where(r[None, :] < r[:, None], MASK, 0.0)
    c[:, C_NEGA:C_NEGA + P] = np.where(r[None, :] > r[:, None], MASK, 0.0)
    c[:, C_IOTA:C_IOTA + 24] = np.arange(24)[None, :]
    return c


def kernel(**inputs):
    import concourse.bacc as bacc
    from concourse.bass_utils import run_bass_kernel_spmd as run

    a = {k: np.asarray(v) for k, v in inputs.items()}

    def cols(v, n):
        return v.reshape(n, P).T

    def chunks(w):
        return w.reshape(w.shape[0] // P, P, w.shape[1]).transpose(1, 0, 2)

    small = np.concatenate(
        [cols(a["L0_attn_ln1_w"], 2), cols(a["L0_attn_norm_w"], 2), cols(a["L0_attn_ln2_w"], 2),
         a["L0_attn_conv_w"].reshape(TAPS, CONV_BLOCKS, P).transpose(2, 1, 0).reshape(P, -1),
         cols(a["L0_attn_conv_b"], CONV_BLOCKS)]
        + [np.broadcast_to(a[n][None, :], (P, H_SSD)) for n in ("L0_attn_dt_bias", "L0_attn_A_log", "L0_attn_D")],
        axis=1)
    heads_q = a["L1_attn_W_Q"].reshape(HEADS, QH, KD, P, DH).transpose(3, 1, 2, 0, 4).reshape(P, QH, KD * QKV)

    def heads(w):
        return w.reshape(HEADS, KD, P, DH).transpose(2, 1, 0, 3).reshape(P, KD, QKV)

    def expert_up(w):
        return w.transpose(2, 0, 1).reshape(KD, P, E, I).transpose(1, 2, 0, 3).reshape(P, E, KD * I)

    w2 = a["L1_ffn_w2"].transpose(0, 2, 1)
    full = (IB - 1) * P
    data = {
        "x_in": a["L0_attn_hidden_states"].reshape(T, D),
        "small_in": small,
        "const_in": constants(),
        "w_in": a["L0_attn_W_in"],
        "w_out": a["L0_attn_W_out"],
        "f_w13": np.stack([chunks(a["L0_attn_w1"]), chunks(a["L0_attn_w3"])], axis=1),
        "f_w2": a["L0_attn_w2"],
        "factors": a["L0_ffn_factors"].reshape(RANK, KD, P, D).transpose(2, 0, 1, 3).reshape(P, RANK, KD * D),
        "ffn_bias": np.broadcast_to(a["L0_ffn_bias"][None, :], (P, D)),
        "wq": heads_q,
        "wk": heads(a["L1_attn_W_K"]),
        "wv": heads(a["L1_attn_W_V"]),
        "wo": a["L1_attn_W_O"].reshape(QKV, D),
        "gate": a["L1_ffn_gate_w"].T.reshape(KD, P, E).transpose(1, 0, 2),
        "m_w1": expert_up(a["L1_ffn_w1"]),
        "m_w3": expert_up(a["L1_ffn_w3"]),
        "m_w2": w2[:, :full].reshape(E, IB - 1, P, D).transpose(2, 0, 1, 3).reshape(P, E, full // P * D),
        "m_w2t": w2[:, full:].transpose(1, 0, 2),
    }
    nc = bacc.Bacc("TRN2", target_bir_lowering=False, num_devices=1)
    arrays, args = {}, []
    for name, v in data.items():
        v = np.ascontiguousarray(v)
        arrays[name] = v
        args.append(nc.dram_tensor(name, v.shape, mybir.dt.from_np(v.dtype), kind="ExternalInput").ap())
    out = nc.dram_tensor("out", (T, D), F32, kind="ExternalOutput").ap()
    build(nc, *args, out)
    r = run(nc, [arrays], core_ids=[0])
    return r.results[0]["out"].reshape(1, T, D)
```

```python
from contextlib import ExitStack

import numpy as np

import concourse.bass as bass
from concourse import mybir

F32 = mybir.dt.float32
F32R = mybir.dt.float32r
BF16 = mybir.dt.bfloat16
I32 = mybir.dt.int32
U32 = mybir.dt.uint32
ALU = mybir.AluOpType
ACT = mybir.ActivationFunctionType
AX_X = mybir.AxisListType.X

P = 128
T = 1024
TT = T // P
D = 256
KD = D // P
GT = 4
GROUPS = TT // GT
GW = GT * P
EPS = 1e-5
H_SSD = 2
N_IN = 770
CONV_BLOCKS = 4
TAPS = 4
FF = 1024
FB = FF // P
RANK = 8
HEADS = 8
DH = 64
QH = 32 // HEADS
QKV = HEADS * DH
QB = QKV // P
E = 8
I = 704
IH = I // 2
IB = (I + P - 1) // P
ILAST = I - (IB - 1) * P
TOP = 2
TILES_MAX = TOP * T // P + E - 1
SLOT_TILES = E * TT + 1
SLOT_W = D + 4
MASK = -1.0e30

C_LN1, C_NORM, C_LN2, C_CONVW, C_CONVB, C_DTB, C_ALOG, C_D = 0, 2, 4, 6, 22, 26, 28, 30
N_SMALL = 32
C_IDENT, C_LE, C_GT, C_LT, C_ONES, C_NEGS, C_NEGA, C_IOTA = 0, 128, 256, 384, 512, 640, 768, 896
C_TOKEN = C_IOTA + 24
N_CONST = C_TOKEN + TT + 1


def build(nc, x_in, small_in, const_in, w_in, w_out, f_w13, f_w2, factors, ffn_bias, wq, wk, wv, wo,
          gate, m_w1, m_w3, m_w2, m_w2t, out):
    slots_in = nc.dram_tensor("expert_in", [SLOT_TILES * P, SLOT_W], F32, kind="Internal").ap()
    with ExitStack() as ctx:
        def sb(name, cols, dt=F32):
            return ctx.enter_context(nc.sbuf_tensor(name, [P, cols], dt))

        def sem(name):
            return ctx.enter_context(nc.semaphore(name))

        def view(tensor, start, *dims):
            n = int(np.prod(dims))
            a = tensor[:, start:start + n]
            if len(dims) == 2:
                return a.rearrange("p (a b) -> p a b", a=dims[0])
            if len(dims) == 3:
                return a.rearrange("p (a b c) -> p a b c", a=dims[0], b=dims[1])
            return a

        def overlay(name, below, cols):
            with nc.sbuf_tensor(name + "_below", [P, below], F32):
                with nc.sbuf_tensor(name, [P, cols], F32R) as t:
                    return t

        K_AT = 2 * E * KD * I - HEADS * T
        k_hi = view(overlay("k_hi", K_AT, HEADS * T), 0, HEADS, T)
        early = sb("early", 2 * E * KD * I)
        k_lo = view(overlay("k_lo", QB * T, QB * T), 0, QB, T)
        mid = sb("mid", E * IB * D)
        at = 0
        win_sb = view(early, at, KD, N_IN); at += KD * N_IN
        fac_sb = view(early, at, RANK, KD * D); at += RANK * KD * D
        wq_sb = view(early, at, QH, KD * QKV); at += QH * KD * QKV
        zs = view(early, at, KD, T); kv_at = at; at += KD * T
        yg = view(early, at, KD, T); at += KD * T
        xpad = view(early, at, CONV_BLOCKS, T + TAPS - 1); ffn_a = [view(early, at, FB, GW)]
        at += CONV_BLOCKS * (T + TAPS - 1)
        cv = view(early, at, CONV_BLOCKS, T); ffn_a.append(view(early, at, FB, GW))
        at += CONV_BLOCKS * T
        assert at <= 2 * E * KD * I
        mixed_w = view(early, KD * N_IN, KD, D)
        wq_sum = view(early, KD * N_IN + RANK * KD * D, KD, QKV)
        wk_sb = view(early, kv_at, KD, QKV)
        wv_sb = view(early, kv_at + KD * QKV, KD, QKV)
        ew1 = view(early, 0, E, KD * I)
        ew3 = view(early, E * KD * I, E, KD * I)

        at = 0
        fw13 = view(mid, at, 2, KD, FF); at += 2 * KD * FF
        fw2 = view(mid, at, FB, D); at += FB * D
        wout_sb = view(mid, at, KD, D); at += KD * D
        tok = view(mid, at, 2, 2 * P); at += 4 * P
        ddx = view(mid, at, 2, H_SSD * P); at += 4 * P
        ramp = view(mid, at, 2, H_SSD * P); at += 4 * P
        decays = view(mid, at, 2, 4 * P); at += 8 * P
        mt = view(mid, at, 2, H_SSD * P); at += 4 * P
        ce = view(mid, at, 2, H_SSD * P); at += 4 * P
        sq = view(mid, at, 2, H_SSD * P); at += 4 * P
        state = view(mid, at, 2, H_SSD, P); at += 2 * H_SSD * P
        assert at <= E * IB * D
        qT = view(mid, 0, QB, T)
        v_sb = view(mid, 2 * QB * T, TT, QKV)
        ew2 = view(mid, 0, E, IB * D)

        q_split = view(overlay("q_split", 5120, HEADS * P), 0, HEADS, P)
        work = sb("work", 7 * 1024)
        wo_sb = view(work, 6144, QB, D)
        sgate = [view(work, 0, GW), view(work, GW, GW)]
        at = 0
        xs = view(work, at, 2, SLOT_W); at += 2 * SLOT_W
        eg = view(work, at, 2, IH); at += I
        ea = view(work, at, 2, I); at += 2 * I
        eaT = view(work, at, 2, IB, P); at += 2 * IB * P
        ey = view(work, at, 2, D); at += 2 * D
        assert at <= 7 * 1024
        cst = sb("cst", N_CONST)
        ident, le_m, gt_m, lt_m, ones = (cst[:, c:c + P] for c in (C_IDENT, C_LE, C_GT, C_LT, C_ONES))
        iota = cst[:, C_IOTA:C_IOTA + 24]
        small = sb("small", N_SMALL)
        bias_sb = sb("bias_sb", D)
        gate_t = sb("gate_sb", KD * E); gate_sb = view(gate_t, 0, KD, E)
        ident_b = sb("ident_b", P, BF16)
        neg_s = sb("neg_s", H_SSD * P, BF16)
        neg_a = sb("neg_a", P, BF16)
        stats_t = sb("stats", TT * 6); stats = view(stats_t, 0, TT, 6)
        mv_t = sb("mv", TT * 2); mv = view(mv_t, 0, TT, 2)
        veps = sb("veps", TT); rstd = sb("rstd", TT)
        veps2 = sb("veps2", TT); rstd2 = sb("rstd2", TT)
        mhalf = sb("mhalf", TT)
        idle_act = veps2
        pad = sb("pad", SLOT_W)
        dts_t = sb("dts", 10 * TT * H_SSD)
        dts = [view(dts_t, i * TT * H_SSD, TT, H_SSD) for i in range(10)]
        ea_log = sb("ea_log", H_SSD)
        dec_t = sb("dec", 2 * TT * H_SSD)
        dec = view(dec_t, 0, 2, TT, H_SSD)
        nmax = sb("nmax", TT * HEADS)
        psums = sb("psums", TT * HEADS)
        pinv = sb("pinv", TT * HEADS)
        rt_t = sb("rt", 8 * TT * E)
        prob_e, top_v, chosen = (view(rt_t, i * TT * E, TT, E) for i in range(3))
        onehot = view(rt_t, 3 * TT * E, TT, TOP, E)
        slot_e = view(rt_t, 5 * TT * E, TT, TOP, E)
        rank_e = view(rt_t, 7 * TT * E, TT, E)
        base_e = view(dts_t, 0, TT + 1, E)
        rs_t = sb("rs", 12 * TT)
        rs = [rs_t[:, i * TT:(i + 1) * TT] for i in range(12)]
        top_f = view(rs_t, 8 * TT, TT, TOP)
        slot_f = view(rs_t, 10 * TT, TT, TOP)
        top_i_t = sb("top_i", TT * 8, U32); top_i = view(top_i_t, 0, TT, 8)
        slot_i_t = sb("slot_i", TOP * TT, U32); slot_i = view(slot_i_t, 0, TT, TOP)
        ecmp = view(bias_sb, 0, 24, E)
        eid_f = bias_sb[:, 216:240]
        eid = sb("eid", 24, I32)
        region = sb("region", 24, I32)
        dest = top_i_t[:, 0:24]
        w_first, w_second = bias_sb[:, 0:24], bias_sb[:, 24:48]
        dest_now = slot_i_t[:, 0:2]
        w_now = rs_t[:, 0:2]
        with nc.sbuf_tensor("rows", [P, 2 * TT * D + KD * T + TT * SLOT_W], F32) as rows_t:
            x = view(rows_t, 0, TT, D)
            xn_t = rows_t[:, TT * D:2 * TT * D]
            xn = view(xn_t, 0, TT, D)
            hT_t = rows_t[:, 2 * TT * D:2 * TT * D + KD * T]
            hT = view(hT_t, 0, KD, T)
            slot_rows = view(rows_t, 2 * TT * D + KD * T, TT, SLOT_W); hh = slot_rows[:, :, 0:D]
        zT = view(hT_t, 1024, QB, P)
        routed_T = view(hT_t, 1536, 2, KD * P)
        probs = [work[:, b * 1024:(b + 1) * 1024] for b in range(3)] + [hT_t[:, 0:1024]]
        pT = [work[:, 3072:4096], work[:, 4096:5120], xn_t[:, 0:1024], xn_t[:, 1024:2048]]
        split_t = sb("split", 4 * KD * I, F32R)
        split_w = [[view(split_t, (w * 2 + part) * KD * I, KD, I) for part in range(2)] for w in range(2)]
        xsT_t = sb("xsT", 4 * D, F32R)
        xsT = [[view(xsT_t, (2 * part + b) * D, KD, P) for b in range(2)] for part in range(2)]
        ps = ctx.enter_context(nc.psum_tensor("ps", [P, 8, 512], F32))

        s_x = [sem(f"x_loaded{g}") for g in range(GROUPS)]
        s_ident = sem("identity_loaded")
        s_small, s_const, s_win, s_mixw, s_ffnw = (sem(n) for n in (
            "small_loaded", "const_loaded", "win_loaded", "wout_loaded", "ffnw_loaded"))
        s_fac, s_wq, s_kv, s_wo, s_gate = (sem(n) for n in (
            "factors_loaded", "wq_loaded", "kv_loaded", "wo_loaded", "gate_loaded"))
        s_e13, s_e2 = sem("expert_w13_loaded"), sem("expert_w2_loaded")
        s_pad, s_padded = sem("pad_set"), sem("slots_padded")
        s_cbf = sem("bf16_constants")
        s_pool0 = sem("pool_constants")
        s_var, s_rstd, s_hh, s_tr, s_hT = (sem(n) for n in (
            "variance", "rstd", "normalised", "transposed", "feature_major"))
        s_var2, s_rstd2 = sem("variance2"), sem("rstd2")
        s_proj, s_evac, s_conv, s_xbc = (sem(n) for n in ("in_proj", "in_evac", "conv_tap", "conv_silu"))
        s_dtp, s_dtv, s_dta = sem("dt_proj"), sem("dt_vector"), sem("dt_scalar")
        s_decp, s_dec, s_dd = sem("decay_sum"), sem("decay_exp"), sem("decay_dt")
        s_ramp, s_front_tr, s_front_seg, s_front_g = (sem(n) for n in (
            "ramp", "chunk_transposed", "segments", "bc_product"))
        s_tok, s_exp, s_mt, s_ce, s_ddx = (sem(n) for n in ("chunk_tokens", "decays", "mt", "ce", "ddx"))
        s_y, s_st, s_state, s_yg, s_sq, s_ss = (sem(n) for n in (
            "y_sum", "state_sum", "state", "y_gated", "y_squared", "square_sum"))
        s_yv, s_yr = sem("y_variance"), sem("y_rstd")
        s_wn = sem("wout_scaled")
        s_mo, s_r2 = sem("mixer_out"), sem("mixer_residual")
        s_xr = sem("x_plus_residual")
        s_gu, s_sg, s_fa, s_fo, s_x1 = (sem(n) for n in (
            "ffn_gate_up", "ffn_silu", "ffn_act", "ffn_out", "x1"))
        s_fsum, s_wqsum = sem("factors_summed"), sem("wq_summed")
        s_xb, s_mx, s_x2 = sem("x_plus_bias"), sem("mixing"), sem("x2")
        s_qkv, s_qa, s_qd = sem("qkv"), sem("qkv_scalar"), sem("qkv_vector")
        s_qhi, s_qs = sem("q_hi"), sem("q_split")
        s_sc, s_max, s_pr, s_pt, s_pT, s_pv = (sem(n) for n in (
            "scores", "row_max", "exponentials", "probs_transposed", "pT", "attended"))
        s_pinv, s_pn = sem("sum_reciprocal"), sem("probs_normalised")
        s_zT, s_ao, s_x3 = sem("zT"), sem("attn_out"), sem("x3")
        s_rT, s_rTc, s_lg, s_lmax, s_lexp, s_chosen, s_cnt = (sem(n) for n in (
            "routed_transposed", "routed_T", "logits", "logit_max", "logit_exp", "chosen", "counts"))
        s_slots, s_scat, s_table, s_dest = sem("slots"), sem("scattered"), sem("tile_table"), sem("destinations")
        s_now, s_idle = sem("slot_tails_ready"), sem("pool_waited")
        s_xs = [sem(f"slot_tile_loaded{b}") for b in range(2)]
        s_ext, s_exT, s_eg, s_eu, s_esg, s_ea = (sem(n) for n in (
            "slot_tile_transposed", "slot_tile_T", "expert_gate", "expert_up", "expert_silu", "expert_act"))
        s_eat, s_eaa, s_ead, s_ey, s_eyc = (sem(n) for n in (
            "act_transposed", "act_T_scalar", "act_T_vector", "expert_y", "expert_y_copied"))
        s_eys = sem("expert_y_scattered")
        s_xhi = sem("slot_tile_hi")
        s_whi = [sem(f"expert_w{w}_hi") for w in (1, 3)]
        s_wlo = [sem(f"expert_w{w}_lo") for w in (1, 3)]
        s_out = sem("residual_stored")
        s_dve, s_act, s_pool = sem("vector_chain"), sem("scalar_chain"), sem("pool_chain")

        FILLS = GROUPS * 12

        def is_k(q):
            return 4 <= q % 12 < 8

        def scalar_fills(q):
            return sum(is_k(i) or i % 2 == 0 for i in range(q + 1))

        def vector_fills(q):
            return sum(is_k(i) or i % 2 == 1 for i in range(q + 1))

        def qv_dst(q):
            g, j = divmod(q, 12)
            if j < 4:
                return qT[:, j, g * GW:(g + 1) * GW], float(DH) ** -0.5
            return v_sb[:, g * GT + j - 8, :], 1.0

        def k_parts(q):
            g, j = divmod(q, 12)
            c = slice(g * GW, (g + 1) * GW)
            for h in range(2):
                half, other = slice(h * DH, (h + 1) * DH), slice((1 - h) * DH, (2 - h) * DH)
                n = 2 * (j - 4) + h
                yield half, k_hi[half, n, c], k_hi[other, n, c], k_lo[half, j - 4, c]

        block = ctx.enter_context(nc.Block())
        PH_MIX, PH_FFN, PH_FAC, PH_ATT, PH_MOE = range(5)
        IN_FILLS = [(g, fb) for g in range(GROUPS) for fb in range(2, 6)] + [(g, fb) for g in range(GROUPS)
                                                                            for fb in range(2)]
        LAST = TILES_MAX - 1

        @block.sync
        def _(sp):
            xv = x_in.rearrange("(t p) d -> p t d", p=P)
            for g in range(GROUPS):
                sp.dma_start(x[:, g * GT:(g + 1) * GT, :], xv[:, g * GT:(g + 1) * GT, :]).then_inc(s_x[g], 16)
            sp.dma_start(win_sb, w_in.rearrange("(k p) n -> p k n", p=P)).then_inc(s_win, 16)
            sp.dma_start(wout_sb, w_out.rearrange("(k p) n -> p k n", p=P)).then_inc(s_mixw, 16)
            sp.dma_start(fac_sb, factors).then_inc(s_fac, 16)
            sp.dma_start(wq_sb, wq).then_inc(s_wq, 16)
            sp.dma_start(fw13, f_w13).then_inc(s_ffnw, 16)
            sp.dma_start(fw2, f_w2.rearrange("(f p) n -> p f n", p=P)).then_inc(s_ffnw, 16)
            sp.dma_start(bias_sb[:, :], ffn_bias).then_inc(s_gate, 16)
            sp.dma_start(gate_sb, gate).then_inc(s_gate, 16)
            sp.wait_ge(s_pad, 1)
            for e in range(E):
                sp.dma_start(slots_in[e * T:(e + 1) * T, :].rearrange("(t p) w -> p t w", p=P),
                             pad[:, :].unsqueeze(1).broadcast_to([P, TT, SLOT_W])).then_inc(s_padded, 16)
            sp.dma_start(slots_in[E * T:, :], pad[:, :]).then_inc(s_padded, 16)
            sp.wait_ge(s_r2, TT)
            sp.dma_start(wk_sb, wk).then_inc(s_kv, 16)
            sp.dma_start(wv_sb, wv).then_inc(s_kv, 16)
            sp.wait_ge(s_x1, TT)
            sp.dma_start(wo_sb, wo.rearrange("(c p) n -> p c n", p=P)).then_inc(s_wo, 16)
            sp.wait_ge(s_qa, scalar_fills(FILLS - 1))
            sp.wait_ge(s_qd, vector_fills(FILLS - 1))
            early_w3 = (K_AT - E * KD * I) // (KD * I)
            for e in range(E):
                sp.dma_start(ew1[:, e], m_w1[:, e]).then_inc(s_e13, 16)
            for e in range(early_w3):
                sp.dma_start(ew3[:, e], m_w3[:, e]).then_inc(s_e13, 16)
            sp.dma_start(out[T:, :], pad[:, 0:D]).then_inc(s_out, 16)
            for t in range(TT - 1):
                sp.wait_ge(s_x3, t + 1)
                sp.dma_start(out[t * P:(t + 1) * P, :], x[:, t, :]).then_inc(s_out, 16)
            for e in range(early_w3, E):
                heads_over = -(-(E * KD * I + (e + 1) * KD * I - K_AT) // T)
                sp.wait_ge(s_sc, (TT - 1) * HEADS + min(heads_over, HEADS))
                sp.dma_start(ew3[:, e], m_w3[:, e]).then_inc(s_e13, 16)
            sp.wait_ge(s_sc, TT * HEADS)
            below_v = 2 * QB * T // (IB * D)
            for e in range(below_v):
                sp.dma_start(ew2[:, e, 0:(IB - 1) * D], m_w2[:, e]).then_inc(s_e2, 16)
            sp.wait_ge(s_pv, TT * HEADS // 2)
            for e in range(below_v, E):
                sp.dma_start(ew2[:, e, 0:(IB - 1) * D], m_w2[:, e]).then_inc(s_e2, 16)
            sp.dma_start(mid[0:ILAST, :].rearrange("p (e r) -> p e r", e=E)[:, :, (IB - 1) * D:],
                         m_w2t).then_inc(s_e2, 16)
            sp.wait_ge(s_x3, TT)
            sp.dma_start(out[(TT - 1) * P:T, :], x[:, TT - 1, :]).then_inc(s_out, 16)

            def load_slots(i, b):
                tile = nc.sync.value_load(region[0:1, bass.ds(i, 1)], min_val=0, max_val=SLOT_TILES - 1)
                sp.dma_start(xs[:, b], slots_in[bass.ts(tile, P), :]).then_inc(s_xs[b], 16)

            sp.wait_ge(s_table, 1)
            sp.wait_ge(s_scat, TOP * TT * 16)
            for b in range(2):
                load_slots(b, b)
            with sp.Fori(0, LAST // 2 - 1) as j:
                for b in range(2):
                    sp.wait_ge(s_ext, 2 * j + b + 1)
                    sp.wait_ge(s_dest, 2 * j + b + 1)
                    load_slots(2 * j + b + 2, b)
            sp.wait_ge(s_ext, LAST - 1)
            sp.wait_ge(s_dest, LAST - 1)
            load_slots(LAST, 0)
            sp.wait_ge(s_eys, 16 * TILES_MAX)

        @block.gpsimd
        def _(pool):
            n_pool = [0]

            def link(ins):
                n_pool[0] += 1
                ins.then_inc(s_pool, 1)
                pool.wait_ge(s_pool, n_pool[0])

            nc.gpsimd.memset(mhalf[:, :], -0.5).then_inc(s_pool0, 1)
            nc.gpsimd.memset(xpad[:, :, 0:TAPS - 1], 0.0).then_inc(s_pool0, 1)
            pool.wait_ge(s_pool0, 2)
            nc.gpsimd.memset(pad[:, 0:D], 0.0)
            nc.gpsimd.memset(pad[:, D + 1:D + 2], -1.0)
            nc.gpsimd.memset(pad[:, D + 2:], 0.0)

            def by_head(a):
                return a.rearrange("p (h l) -> p h l", h=H_SSD)

            def along(a):
                return a.unsqueeze(2).broadcast_to([P, H_SSD, P])

            def rstds(ph, g):
                pool.wait_ge(s_var, GROUPS * ph + g + 1)
                c = slice(g * GT, (g + 1) * GT)
                nc.gpsimd.tensor_tensor(rstd[:, c], veps[:, c], mhalf[:, c], ALU.pow).then_inc(s_rstd, 1)
                if ph == PH_MIX:
                    pool.wait_ge(s_var2, g + 1)
                    nc.gpsimd.tensor_tensor(rstd2[:, c], veps2[:, c], mhalf[:, c],
                                            ALU.pow).then_inc(s_rstd2, 1)

            for g in range(GROUPS):
                rstds(PH_MIX, g)
            pool.wait_ge(s_const, 16)
            nc.gpsimd.tensor_copy(pad[:, D:D + 1], cst[:, C_TOKEN + TT:C_TOKEN + TT + 1]).then_inc(s_pad, 1)
            pool.wait_ge(s_fac, 16)
            for r in range(1, RANK):
                link(nc.gpsimd.tensor_tensor(fac_sb[:, 0], fac_sb[:, 0], fac_sb[:, r], ALU.add))
            nc.gpsimd.tensor_scalar(fac_sb[:, 0], fac_sb[:, 0], float(1.0 / np.sqrt(RANK)), None,
                                    ALU.mult).then_inc(s_fsum, 1)
            for c in range(TT):
                b = c % 2
                if c == 0:
                    pool.wait_ge(s_dtv, 4)
                if c >= 2:
                    pool.wait_ge(s_front_seg, c - 1)
                nc.gpsimd.tensor_tensor(by_head(ramp[:, b]), le_m.unsqueeze(1).broadcast_to([P, H_SSD, P]),
                                        along(dts[1][:, c, :]), ALU.mult).then_inc(s_ramp, 1)
                if c == 0:
                    pool.wait_ge(s_dd, 1)
                pool.wait_ge(s_tok, c + 1)
                if c >= 2:
                    pool.wait_ge(s_y, c - 1)
                    pool.wait_ge(s_st, c - 1)
                if c < TT - 1:
                    nc.gpsimd.tensor_tensor(by_head(ddx[:, b]), tok[:, b, 0:P].unsqueeze(1).broadcast_to([P, H_SSD, P]),
                                            along(dts[2][:, c, :]), ALU.mult).then_inc(s_ddx, 1)
                if c > 0:
                    pool.wait_ge(s_exp, c + 1)
                    nc.gpsimd.tensor_tensor(by_head(ce[:, b]), cv[:, 2:4, c * P:(c + 1) * P],
                                            by_head(decays[:, b, 2 * P:]), ALU.mult).then_inc(s_ce, 1)
            pool.wait_ge(s_yv, 1)
            nc.gpsimd.tensor_tensor(rstd2[:, :], veps2[:, :], mhalf[:, :], ALU.pow).then_inc(s_yr, 1)
            for g in range(GROUPS):
                rstds(PH_FFN, g)
            for t in range(TT):
                pool.wait_ge(s_r2, t + 1)
                nc.gpsimd.tensor_tensor(x[:, t, :], x[:, t, :], xn[:, t, :], ALU.add).then_inc(s_xr, 1)
            pool.wait_ge(s_wq, 16)
            for r in range(1, QH):
                ins = nc.gpsimd.tensor_tensor(wq_sb[:, 0], wq_sb[:, 0], wq_sb[:, r], ALU.add)
                if r < QH - 1:
                    link(ins)
            ins.then_inc(s_wqsum, 1)
            pool.wait_ge(s_gate, 32)
            for g in range(GROUPS):
                rstds(PH_FAC, g)
                for t in range(g * GT, (g + 1) * GT):
                    pool.wait_ge(s_hh, TT * PH_FAC + t + 1)
                    nc.gpsimd.tensor_tensor(x[:, t, :], x[:, t, :], bias_sb[:, :], ALU.add).then_inc(s_xb, 1)
            for g in range(GROUPS):
                rstds(PH_ATT, g)
            def split_queries(m):
                i, pair = divmod(m, HEADS // 2)
                if m >= HEADS // 2:
                    pool.wait_ge(s_sc, 2 * (m - HEADS // 2) + 2)
                for h in range(2):
                    half, other = slice(h * DH, (h + 1) * DH), slice((1 - h) * DH, (2 - h) * DH)
                    nc.gpsimd.tensor_copy(q_split[half, 2 * pair + h, :],
                                          qT[half, pair, i * P:(i + 1) * P]).then_inc(s_qhi, 1)
                pool.wait_ge(s_qhi, 2 * m + 2)
                for h in range(2):
                    half, other = slice(h * DH, (h + 1) * DH), slice((1 - h) * DH, (2 - h) * DH)
                    nc.gpsimd.tensor_tensor(q_split[other, 2 * pair + h, :], qT[half, pair, i * P:(i + 1) * P],
                                            q_split[half, 2 * pair + h, :].bitcast(F32), ALU.subtract).then_inc(s_qs, 1)
                    pool.wait_ge(s_qs, 2 * m + h + 1)

            pool.wait_ge(s_padded, (E + 1) * 16)
            pool.wait_ge(s_rstd, GROUPS * PH_MOE)
            pool.wait_ge(s_qa, scalar_fills(QB - 1))
            pool.wait_ge(s_qd, vector_fills(QB - 1))
            for m in range(HEADS // 2):
                split_queries(m)
            for i in range(TT + 2):
                if i + 1 < TT:
                    for pair in range(2):
                        split_queries((i + 1) * HEADS // 2 + pair)
                if i >= 2:
                    t = i - 2
                    pool.wait_ge(s_slots, t + 1)
                    for k in range(TOP):
                        nc.gpsimd.indirect_dma_start(
                            out=slots_in, out_offset=bass.IndirectOffsetOnAxis(ap=slot_i[:, t, k:k + 1], axis=0),
                            in_=slot_rows[:, t, :], in_offset=None).then_inc(s_scat, 16)
                if 1 <= i <= TT:
                    t = i - 1
                    pool.wait_ge(s_var, GROUPS * PH_MOE + t + 1)
                    nc.gpsimd.tensor_tensor(rstd[:, t:t + 1], veps[:, t:t + 1], mhalf[:, t:t + 1],
                                            ALU.pow).then_inc(s_rstd, 1)
                    pool.wait_ge(s_rstd, GROUPS * PH_MOE + t + 1)
                if i + 1 < TT:
                    if i >= 2:
                        pool.wait_ge(s_scat, (i - 1) * TOP * 16)
                    for pair in range(2, 4):
                        split_queries((i + 1) * HEADS // 2 + pair)

            def return_rows(i, b, first=False):
                pool.wait_ge(s_eyc, i + 1)
                if not first:
                    pool.wait_ge(s_eys, 16 * i)
                    pool.wait_ge(s_idle, i)
                nc.gpsimd.tensor_tensor(rstd2[:, 0:1], mhalf[:, 0:1], mhalf[:, 0:1], ALU.mult).then_inc(s_idle, 1)
                nc.gpsimd.indirect_dma_start(
                    out=out, out_offset=bass.IndirectOffsetOnAxis(ap=dest_now[:, b:b + 1], axis=0),
                    in_=ey[:, b], in_offset=None, compute_op=ALU.add).then_inc(s_eys, 16)

            pool.wait_ge(s_out, (TT + 1) * 16)
            return_rows(0, 0, first=True)
            return_rows(1, 1)
            with pool.Fori(1, LAST // 2) as j:
                for b in range(2):
                    return_rows(2 * j + b, b)
            return_rows(LAST, 0)

        @block.scalar
        def _(act):
            n_act = [0]

            def link(ins):
                n_act[0] += 1
                ins.then_inc(s_act, 1)
                act.wait_ge(s_act, n_act[0])

            def feature_major(ph, g, scale_col=None):
                act.wait_ge(s_tr, GROUPS * ph + g + 1)
                for k in range(KD):
                    dst = hT[:, k, g * GW:(g + 1) * GW]
                    if scale_col is None:
                        last = nc.scalar.copy(dst, ps[:, k, :])
                    else:
                        last = nc.scalar.activation(dst, ps[:, k, :], ACT.Copy,
                                                    scale=small[:, scale_col + k:scale_col + k + 1])
                last.then_inc(s_hT, 1)

            act.dma_start(cst[:, 0:P], const_in[:, 0:P]).then_inc(s_ident, 16)
            act.dma_start(small[:, :], small_in).then_inc(s_small, 16)
            act.dma_start(cst[:, P:], const_in[:, P:]).then_inc(s_const, 16)
            act.wait_ge(s_small, 16)
            act.wait_ge(s_pool0, 2)
            feature_major(PH_MIX, 0, C_LN1)
            feature_major(PH_MIX, 1, C_LN1)
            def projected(q):
                g, fb = IN_FILLS[q]
                act.wait_ge(s_proj, q + 1)
                bank = ps[:, 2 + q % 4, :]
                if fb < 2:
                    last = nc.scalar.activation(zs[:, fb, g * GW:(g + 1) * GW], bank, ACT.Silu)
                else:
                    c = fb - 2
                    nc.scalar.copy(xpad[:, c, TAPS - 1 + g * GW:TAPS - 1 + (g + 1) * GW], bank)
                    last = nc.scalar.activation(
                        cv[:, c, g * GW:(g + 1) * GW], bank, ACT.Identity,
                        scale=small[:, C_CONVW + 4 * c + 3:C_CONVW + 4 * c + 4],
                        bias=small[:, C_CONVB + c:C_CONVB + c + 1])
                last.then_inc(s_evac, 1)

            def convolved(g):
                for c in range(CONV_BLOCKS):
                    act.wait_ge(s_conv, g * 12 + 8 + c + 1)
                    a = cv[:, c, g * GW:(g + 1) * GW]
                    nc.scalar.activation(a, a, ACT.Silu).then_inc(s_xbc, 1)

            for q in range(CONV_BLOCKS):
                projected(q)
            act.wait_ge(s_dtv, 1)
            nc.scalar.activation(dts[3], dts[3], ACT.Exp).then_inc(s_dta, 1)
            nc.scalar.activation(ea_log[:, :], small[:, C_ALOG:C_ALOG + H_SSD], ACT.Exp).then_inc(s_dta, 1)
            for q in range(CONV_BLOCKS, 2 * CONV_BLOCKS):
                projected(q)
            act.wait_ge(s_dtv, 2)
            nc.scalar.activation(dts[5], dts[4], ACT.Ln).then_inc(s_dta, 1)
            convolved(0)
            for q in range(2 * CONV_BLOCKS, len(IN_FILLS)):
                projected(q)
            convolved(1)
            act.wait_ge(s_decp, 1)
            nc.scalar.activation(dec_t[:, :], ps[:, 6, 0:2 * TT * H_SSD], ACT.Exp).then_inc(s_dec, 1)

            def squares(c):
                act.wait_ge(s_yg, c + 1)
                if c >= 2:
                    act.wait_ge(s_ss, c - 1)
                nc.scalar.activation(sq[:, c % 2].rearrange("p (h l) -> p h l", h=H_SSD),
                                     yg[:, :, c * P:(c + 1) * P], ACT.Square).then_inc(s_sq, 1)

            for c in range(TT):
                b = c % 2
                act.wait_ge(s_front_tr, c + 1)
                if c >= 2:
                    act.wait_ge(s_st, c - 1)
                nc.scalar.copy(tok[:, b], ps[:, 0, 0:2 * P]).then_inc(s_tok, 1)
                act.wait_ge(s_front_seg, c + 1)
                nc.scalar.activation(decays[:, b], ps[:, 2, :], ACT.Exp).then_inc(s_exp, 1)
                if c >= 1:
                    squares(c - 1)
            squares(TT - 1)
            feature_major(PH_FFN, 0, C_LN2)
            for q in range(GROUPS * FB):
                if q == FB:
                    feature_major(PH_FFN, 1, C_LN2)
                act.wait_ge(s_gu, q + 1)
                if q >= 2:
                    act.wait_ge(s_fa, q - 1)
                nc.scalar.activation(sgate[q % 2], ps[:, 2 + q % 2, :], ACT.Silu).then_inc(s_sg, 1)
            for g in range(GROUPS):
                feature_major(PH_FAC, g)
            feature_major(PH_ATT, 0)
            for q in range(FILLS):
                if q == 10:
                    feature_major(PH_ATT, 1)
                if is_k(q):
                    act.wait_ge(s_qkv, q + 1)
                    for half, hi, hi_other, lo in k_parts(q):
                        nc.scalar.copy(hi, ps[half, 2 + q % 6, :])
                        last = nc.scalar.copy(hi_other, ps[half, 2 + q % 6, :])
                    last.then_inc(s_qa, 1)
                elif q % 2 == 0:
                    act.wait_ge(s_qkv, q + 1)
                    dst, scale = qv_dst(q)
                    nc.scalar.activation(dst, ps[:, 2 + q % 6, :], ACT.Copy, scale=scale).then_inc(s_qa, 1)

            def attend(u):
                i, n = divmod(u, HEADS)
                w = (i + 1) * P
                act.wait_ge(s_max, u + 1)
                if u >= 4:
                    act.wait_ge(s_pt, u - 3)
                src = ps[:, 2 * (u % 2):2 * (u % 2) + 2, :].rearrange("p a b -> p (a b)")[:, 0:w]
                nc.scalar.activation(probs[u % 4][:, 0:w], src, ACT.Exp, bias=nmax[:, u:u + 1],
                                     accum_out=psums[:, u:u + 1]).then_inc(s_pr, 1)

            def probs_feature_major(u):
                w = (u // HEADS + 1) * P
                act.wait_ge(s_pt, u + 1)
                if u >= 4:
                    act.wait_ge(s_pv, u // 2 - 1)
                nc.scalar.copy(pT[u % 4][:, 0:w],
                               ps[:, 4:6, :].rearrange("p a b -> p (a b)")[:, 0:w]).then_inc(s_pT, 1)

            def z_feature_major(i):
                act.wait_ge(s_pv, (i + 1) * HEADS // 2)
                if i >= 1:
                    act.wait_ge(s_ao, i)
                nc.scalar.copy(zT.rearrange("p a b -> p (a b)"), ps[:, 6 + i % 2, :]).then_inc(s_zT, 1)

            def routed_feature_major(i):
                act.wait_ge(s_rT, i + 1)
                if i >= 2:
                    act.wait_ge(s_lg, i - 1)
                nc.scalar.copy(routed_T[:, i % 2], ps[:, 6 + i % 2, 0:D]).then_inc(s_rTc, 1)

            def logits_exp(i):
                act.wait_ge(s_lmax, i + 1)
                nc.scalar.activation(prob_e[:, i, :], ps[:, 6 + i % 2, D:D + E], ACT.Exp, bias=rs[0][:, i:i + 1],
                                     accum_out=rs[1][:, i:i + 1]).then_inc(s_lexp, 1)

            for u in range((TT + 1) * HEADS + 5):
                if u >= 2 * HEADS and u % HEADS == 0:
                    routed_feature_major(u // HEADS - 2)
                if u >= 2 * HEADS and u % HEADS == 2:
                    logits_exp(u // HEADS - 2)
                if HEADS <= u < (TT + 1) * HEADS and u % HEADS == 4:
                    z_feature_major(u // HEADS - 1)
                if 3 <= u < TT * HEADS + 3:
                    probs_feature_major(u - 3)
                if u < TT * HEADS:
                    attend(u)

            def expert_silu(i):
                act.wait_ge(s_eg, i + 1)
                act.wait_ge(s_ea, i)
                nc.scalar.activation(eg, ps[:, 0:2, 0:IH], ACT.Silu).then_inc(s_esg, 1)

            def expert_aT(i, b):
                act.wait_ge(s_eat, i + 1)
                nc.scalar.copy(eaT[:, b, 0:4, :].rearrange("p a b -> p (a b)"), ps[:, 4, :]).then_inc(s_eaa, 1)

            def expert_y(i, b, first=False):
                act.wait_ge(s_ey, i + 1)
                act.wait_ge(s_now, i + 1)
                if not first:
                    act.wait_ge(s_eys, 16 * (i - 1))
                nc.scalar.activation(ey[:, b], ps[:, 6, 0:D], ACT.Copy, scale=w_now[:, b:b + 1]).then_inc(s_eyc, 1)

            def weights_hi(e, w):
                nc.scalar.copy(split_w[w][0].rearrange("p k n -> p (k n)").unsqueeze(1),
                               (ew1, ew3)[w][:, bass.ds(e, 1), :]).then_inc(s_whi[w], 1)

            def expert_of(i):
                return nc.scalar.value_load(eid[0:1, bass.ds(i, 1)], min_val=0, max_val=E - 1)

            def slot_tile_hi(i, b):
                act.wait_ge(s_ext, i + 1)
                nc.scalar.copy(xsT[0][b], ps[:, 7, 0:D].rearrange("p (k t) -> p k t", k=KD)).then_inc(s_xhi, 1)

            def next_weights(i, first=False):
                if first:
                    act.wait_ge(s_eg, 1)
                    nc.scalar.activation(eg, ps[:, 0:2, 0:IH], ACT.Silu).then_inc(s_esg, 1)
                else:
                    expert_silu(i)
                e = expert_of(i + 1)
                weights_hi(e, 0)
                act.wait_ge(s_eu, i + 1)
                nc.scalar.copy(idle_act[:, 0:1], mhalf[:, 0:1])
                weights_hi(e, 1)

            act.wait_ge(s_table, 1)
            act.wait_ge(s_e13, 2 * E * 16)
            act.wait_ge(s_out, (TT + 1) * 16)
            act.wait_ge(s_lg, TT)
            nc.scalar.copy(idle_act[:, 1:2], mhalf[:, 0:1])
            e = expert_of(0)
            for w in range(2):
                weights_hi(e, w)
            for b in range(2):
                slot_tile_hi(b, b)
            next_weights(0, first=True)

            def body(i, b, first=False):
                slot_tile_hi(i + 2, b)
                expert_aT(i, b)
                next_weights(i + 1)
                expert_y(i, b, first)

            body(0, 0, first=True)
            body(1, 1, first=True)
            with act.Fori(1, LAST // 2 - 1) as j:
                for b in range(2):
                    body(2 * j + b, b)
            body(LAST - 2, 0)
            expert_aT(LAST - 1, 1)
            expert_silu(LAST)
            expert_y(LAST - 1, 1)
            expert_aT(LAST, 0)
            expert_y(LAST, 0)

        @block.vector
        def _(dve):
            n_dve = [0]

            def link(ins):
                n_dve[0] += 1
                ins.then_inc(s_dve, 1)
                dve.wait_ge(s_dve, n_dve[0])

            V = nc.vector

            def variances(ph, src, g):
                for t in range(g * GT, (g + 1) * GT):
                    if ph == PH_FFN:
                        dve.wait_ge(s_r2, t + 1)
                    elif ph == PH_FAC:
                        dve.wait_ge(s_x1, t + 1)
                    elif ph == PH_ATT:
                        dve.wait_ge(s_x2, t + 1)
                    ins = V.bn_stats(stats[:, t, :], src[:, t, :])
                link(ins)
                for t in range(g * GT, (g + 1) * GT):
                    ins = V.bn_aggr(mv[:, t, :], stats[:, t, :])
                link(ins)
                c = slice(g * GT, (g + 1) * GT)
                if ph == PH_FFN:
                    link(V.tensor_tensor(veps2[:, c], mv[:, c, 0], mv[:, c, 0], ALU.mult))
                    V.scalar_tensor_tensor(veps[:, c], mv[:, c, 1], EPS, veps2[:, c], ALU.add,
                                           ALU.add).then_inc(s_var, 1)
                else:
                    V.tensor_scalar(veps[:, c], mv[:, c, 1], EPS, None, ALU.add).then_inc(s_var, 1)

            def normalise(ph, src, g):
                dve.wait_ge(s_rstd, GROUPS * ph + g + 1)
                for t in range(g * GT, (g + 1) * GT):
                    if ph > 0:
                        dve.wait_ge(s_tr, GROUPS * (ph - 1) + g + 1)
                    if ph == PH_FFN:
                        V.tensor_scalar(hh[:, t, :], src[:, t, :], rstd[:, t:t + 1], None,
                                        ALU.mult).then_inc(s_hh, 1)
                    else:
                        V.tensor_scalar(hh[:, t, :], src[:, t, :], mv[:, t, 0:1], rstd[:, t:t + 1],
                                        ALU.subtract, ALU.mult).then_inc(s_hh, 1)

            for g in range(GROUPS):
                dve.wait_ge(s_x[g], 16)
                variances(PH_MIX, x, g)
            for g in range(GROUPS):
                c = slice(g * GT, (g + 1) * GT)
                dve.wait_ge(s_rstd, g + 1)
                link(V.tensor_tensor(veps2[:, c], rstd[:, c], rstd[:, c], ALU.mult))
                link(V.tensor_tensor(veps2[:, c], veps2[:, c], mv[:, c, 1], ALU.mult))
                V.tensor_scalar(veps2[:, c], veps2[:, c], EPS, None, ALU.add).then_inc(s_var2, 1)
            for g in range(GROUPS):
                c = slice(g * GT, (g + 1) * GT)
                dve.wait_ge(s_rstd2, g + 1)
                link(V.tensor_tensor(rstd2[:, c], rstd2[:, c], rstd[:, c], ALU.mult))
                for t in range(g * GT, (g + 1) * GT):
                    V.tensor_scalar(hh[:, t, :], x[:, t, :], mv[:, t, 0:1], rstd2[:, t:t + 1],
                                    ALU.subtract, ALU.mult).then_inc(s_hh, 1)
            for t in range(TT):
                V.tensor_scalar(xn[:, t, :], x[:, t, :], mv[:, t, 0:1], rstd[:, t:t + 1],
                                ALU.subtract, ALU.mult)

            dve.wait_ge(s_const, 16)
            V.tensor_copy(ident_b[:, :], ident)
            for h in range(H_SSD):
                V.tensor_copy(neg_s[:, h * P:(h + 1) * P], cst[:, C_NEGS:C_NEGS + P])
            V.tensor_copy(neg_a[:, :], cst[:, C_NEGA:C_NEGA + P]).then_inc(s_cbf, 1)

            dve.wait_ge(s_small, 16)
            dve.wait_ge(s_mixw, 16)
            for k in range(KD):
                V.tensor_scalar(wout_sb[:, k, :], wout_sb[:, k, :], small[:, C_NORM + k:C_NORM + k + 1], None,
                                ALU.mult).then_inc(s_wn, 1)

            def row(c):
                return small[:, c:c + H_SSD].unsqueeze(1).broadcast_to([P, TT, H_SSD])

            dve.wait_ge(s_dtp, 1)
            link(V.tensor_tensor(dts[6], ps[:, 6, 64:64 + TT * H_SSD].rearrange("p (t h) -> p t h", h=H_SSD),
                                 row(C_DTB), ALU.add))
            V.scalar_tensor_tensor(dts_t[:, 48:64], dts_t[:, 96:112], -1.0, dts_t[:, 96:112], ALU.mult,
                                   ALU.min).then_inc(s_dtv, 1)

            def convolve(g):
                dve.wait_ge(s_evac, (g + 1) * CONV_BLOCKS)
                for k in range(TAPS - 1):
                    for c in range(CONV_BLOCKS):
                        if k:
                            dve.wait_ge(s_conv, (g * (TAPS - 1) + k - 1) * CONV_BLOCKS + c + 1)
                        a = cv[:, c, g * GW:(g + 1) * GW]
                        V.scalar_tensor_tensor(a, xpad[:, c, k + g * GW:k + (g + 1) * GW],
                                               small[:, C_CONVW + 4 * c + k:C_CONVW + 4 * c + k + 1], a,
                                               ALU.mult, ALU.add).then_inc(s_conv, 1)

            convolve(0)
            dve.wait_ge(s_dta, 1)
            V.tensor_scalar(dts[4], dts[3], 1.0, None, ALU.add).then_inc(s_dtv, 1)
            dve.wait_ge(s_dtv, 2)
            link(V.tensor_scalar(dts[7], dts[4], -1.0, None, ALU.add))
            link(V.tensor_scalar(dts[8], dts[7], 0.0, None, ALU.is_equal))
            link(V.tensor_tensor(dts[7], dts[7], dts[8], ALU.add))
            link(V.reciprocal(dts[9], dts[7]))
            dve.wait_ge(s_dta, 3)
            link(V.tensor_tensor(dts[9], dts[9], dts[5], ALU.mult))
            link(V.tensor_tensor(dts[9], dts[9], dts[8], ALU.add))
            link(V.tensor_tensor(dts[9], dts[9], dts[3], ALU.mult))
            V.scalar_tensor_tensor(dts_t[:, 0:16], dts_t[:, 96:112], 0.0, dts_t[:, 144:160], ALU.max,
                                   ALU.add).then_inc(s_dtv, 1)
            dve.wait_ge(s_dtv, 3)
            link(V.tensor_scalar(ea_log[:, :], ea_log[:, :], -1.0, None, ALU.mult))
            V.tensor_tensor(dts[1], dts[0], ea_log[:, :].unsqueeze(1).broadcast_to([P, TT, H_SSD]),
                            ALU.mult).then_inc(s_dtv, 1)
            convolve(1)
            dve.wait_ge(s_dec, 1)
            V.tensor_tensor(dts[2], dec[:, 0], dts[0], ALU.mult).then_inc(s_dd, 1)

            def masked(c):
                b = c % 2
                dve.wait_ge(s_front_g, c + 1)
                dve.wait_ge(s_exp, c + 1)
                if c >= 2:
                    dve.wait_ge(s_y, c - 1)
                for h in range(H_SSD):
                    last = V.scalar_tensor_tensor(
                        mt[:, b, h * P:(h + 1) * P], ps[:, 1, h * P:(h + 1) * P], dts[0][:, c, h:h + 1],
                        decays[:, b, h * P:(h + 1) * P], ALU.mult, ALU.mult)
                last.then_inc(s_mt, 1)

            masked(0)
            for c in range(TT):
                b = c % 2
                if c < TT - 1:
                    masked(c + 1)
                    dve.wait_ge(s_st, c + 1)
                    for h in range(H_SSD):
                        if c == 0:
                            last = V.tensor_copy(state[:, 1, h], ps[:, 5, h * P:(h + 1) * P])
                        else:
                            dve.wait_ge(s_state, c)
                            last = V.scalar_tensor_tensor(state[:, 1 - b, h], state[:, b, h], dec[:, 1, c, h:h + 1],
                                                          ps[:, 5, h * P:(h + 1) * P], ALU.mult, ALU.add)
                    last.then_inc(s_state, 1)
                dve.wait_ge(s_y, c + 1)
                for h in range(H_SSD):
                    ins = V.scalar_tensor_tensor(
                        yg[:, h, c * P:(c + 1) * P], cv[:, 0, c * P:(c + 1) * P], small[:, C_D + h:C_D + h + 1],
                        ps[:, 3 + b, h * P:(h + 1) * P], ALU.mult, ALU.add)
                link(ins)
                V.tensor_tensor(yg[:, :, c * P:(c + 1) * P], yg[:, :, c * P:(c + 1) * P],
                                zs[:, :, c * P:(c + 1) * P], ALU.mult).then_inc(s_yg, 1)
            dve.wait_ge(s_ss, TT)
            V.tensor_scalar(veps2[:, :], ps[:, 7, 0:TT], 1.0 / D, EPS, ALU.mult, ALU.add).then_inc(s_yv, 1)
            dve.wait_ge(s_yr, 1)
            def mixer_residual(g):
                for t in range(g * GT, (g + 1) * GT):
                    dve.wait_ge(s_mo, t + 1)
                    V.scalar_tensor_tensor(xn[:, t, :], ps[:, 5 + t % 2, 0:D], rstd2[:, t:t + 1], xn[:, t, :],
                                           ALU.mult, ALU.add).then_inc(s_r2, 1)

            def swiglu(g):
                for f in range(FB):
                    q = g * FB + f
                    dve.wait_ge(s_sg, q + 1)
                    V.tensor_tensor(ffn_a[g][:, f, :], sgate[q % 2], ps[:, 4 + q % 2, :],
                                    ALU.mult).then_inc(s_fa, 1)

            def residual(g, ready, base, done):
                for t in range(g * GT, (g + 1) * GT):
                    dve.wait_ge(ready, t + 1)
                    dve.wait_ge(base, t + 1)
                    V.tensor_tensor(x[:, t, :], x[:, t, :], ps[:, 6 + t % 2, 0:D], ALU.add).then_inc(done, 1)

            mixer_residual(0)
            variances(PH_FFN, xn, 0)
            mixer_residual(1)
            normalise(PH_FFN, xn, 0)
            variances(PH_FFN, xn, 1)
            normalise(PH_FFN, xn, 1)
            swiglu(0)
            residual(0, s_fo, s_xr, s_x1)
            variances(PH_FAC, x, 0)
            normalise(PH_FAC, x, 0)
            swiglu(1)
            residual(1, s_fo, s_xr, s_x1)
            variances(PH_FAC, x, 1)
            normalise(PH_FAC, x, 1)
            residual(0, s_mx, s_xb, s_x2)
            variances(PH_ATT, x, 0)
            normalise(PH_ATT, x, 0)
            residual(1, s_mx, s_xb, s_x2)
            variances(PH_ATT, x, 1)
            normalise(PH_ATT, x, 1)
            for q in range(FILLS):
                if is_k(q):
                    dve.wait_ge(s_qa, scalar_fills(q))
                    for half, hi, hi_other, lo in k_parts(q):
                        last = V.tensor_tensor(lo, ps[half, 2 + q % 6, :], hi.bitcast(F32), ALU.subtract)
                    last.then_inc(s_qd, 1)
                elif q % 2:
                    dve.wait_ge(s_qkv, q + 1)
                    dst, scale = qv_dst(q)
                    V.tensor_scalar(dst, ps[:, 2 + q % 6, :], scale, None, ALU.mult).then_inc(s_qd, 1)

            def row_max(u):
                w = (u // HEADS + 1) * P
                dve.wait_ge(s_sc, u + 1)
                src = ps[:, 2 * (u % 2):2 * (u % 2) + 2, :].rearrange("p a b -> p (a b)")[:, 0:w]
                V.tensor_reduce(nmax[:, u:u + 1], src, AX_X, ALU.max, negate=True).then_inc(s_max, 1)

            def normalised(u):
                w = (u // HEADS + 1) * P
                dve.wait_ge(s_pr, u + 1)
                V.reciprocal(pinv[:, u:u + 1], psums[:, u:u + 1]).then_inc(s_pinv, 1)
                dve.wait_ge(s_pinv, u + 1)
                V.tensor_scalar(probs[u % 4][:, 0:w], probs[u % 4][:, 0:w], pinv[:, u:u + 1], None,
                                ALU.mult).then_inc(s_pn, 1)

            def add_attention(i):
                dve.wait_ge(s_ao, i + 1)
                V.tensor_tensor(x[:, i, :], x[:, i, :], ps[:, 6 + i % 2, 0:D], ALU.add).then_inc(s_x3, 1)

            iota_e = iota[:, 0:E].unsqueeze(1).broadcast_to([P, TOP, E])

            def route_variance(t):
                dve.wait_ge(s_x3, t + 1)
                link(V.bn_stats(stats[:, t, :], x[:, t, :]))
                link(V.bn_aggr(mv[:, t, :], stats[:, t, :]))
                V.tensor_scalar(veps[:, t:t + 1], mv[:, t, 1:2], EPS, None, ALU.add).then_inc(s_var, 1)

            def route_normalise(t):
                dve.wait_ge(s_rstd, GROUPS * PH_MOE + t + 1)
                V.tensor_scalar(hh[:, t, :], x[:, t, :], mv[:, t, 0:1], rstd[:, t:t + 1],
                                ALU.subtract, ALU.mult).then_inc(s_hh, 1)

            def route_max(t):
                dve.wait_ge(s_lg, t + 1)
                V.tensor_reduce(rs[0][:, t:t + 1], ps[:, 6 + t % 2, D:D + E], AX_X, ALU.max,
                                negate=True).then_inc(s_lmax, 1)

            def route_choice(t):
                dve.wait_ge(s_lexp, t + 1)
                link(V.reciprocal(rs[2][:, t:t + 1], rs[1][:, t:t + 1]))
                link(V.tensor_scalar(prob_e[:, t, :], prob_e[:, t, :], rs[2][:, t:t + 1], None, ALU.mult))
                link(V.max(top_v[:, t, :], prob_e[:, t, :]))
                link(V.max_index(top_i[:, t, :], top_v[:, t, :], prob_e[:, t, :]))
                link(V.tensor_copy(top_f[:, t, :], top_i[:, t, 0:TOP]))
                link(V.tensor_tensor(onehot[:, t], iota_e, top_f[:, t, :].unsqueeze(2).broadcast_to([P, TOP, E]),
                                     ALU.is_equal))
                V.tensor_tensor(chosen[:, t, :], onehot[:, t, 0, :], onehot[:, t, 1, :],
                                ALU.add).then_inc(s_chosen, 1)
                V.tensor_copy(slot_rows[:, t, D:D + 1], cst[:, C_TOKEN + t:C_TOKEN + t + 1])
                V.tensor_copy(slot_rows[:, t, D + 1:D + 2], top_f[:, t, 0:1])
                link(V.tensor_tensor(rs[3][:, t:t + 1], top_v[:, t, 0:1], top_v[:, t, 1:2], ALU.add))
                link(V.reciprocal(rs[4][:, t:t + 1], rs[3][:, t:t + 1]))
                V.tensor_scalar(slot_rows[:, t, D + 2:], top_v[:, t, 0:TOP], rs[4][:, t:t + 1], None, ALU.mult)

            def route_slots(t):
                dve.wait_ge(s_cnt, t + 1)
                before = ps[:, 6 + t % 2, D + E:D + 2 * E]
                totals = ps[:, 6 + t % 2, D + 2 * E:D + 3 * E]
                V.tensor_tensor(rank_e[:, t, :], base_e[:, t, :], before, ALU.add)
                link(V.tensor_tensor(base_e[:, t + 1, :], base_e[:, t, :], totals, ALU.add))
                link(V.tensor_tensor(slot_e[:, t], onehot[:, t],
                                     rank_e[:, t, :].unsqueeze(1).broadcast_to([P, TOP, E]), ALU.mult))
                link(V.tensor_reduce(slot_f[:, t, :], slot_e[:, t], AX_X, ALU.add))
                V.tensor_copy(slot_i[:, t, :], slot_f[:, t, :]).then_inc(s_slots, 1)

            link(V.tensor_scalar(base_e[:, 0, :], iota[:, 0:E], float(T), None, ALU.mult))
            for u in range((TT + 1) * HEADS + 5):
                if u < TT * HEADS:
                    row_max(u)
                if 1 <= u < TT * HEADS + 1:
                    normalised(u - 1)
                if HEADS <= u < (TT + 1) * HEADS and u % HEADS == 5:
                    add_attention(u // HEADS - 1)
                    route_variance(u // HEADS - 1)
                if HEADS <= u < (TT + 1) * HEADS and u % HEADS == 6:
                    route_normalise(u // HEADS - 1)
                if u >= 2 * HEADS and u % HEADS == 1:
                    route_max(u // HEADS - 2)
                if u >= 2 * HEADS and u % HEADS == 2:
                    route_choice(u // HEADS - 2)
                if u >= 2 * HEADS and u % HEADS == 4:
                    route_slots(u // HEADS - 2)
            link(V.tensor_scalar(rs[8], iota[:, 0:E], float(P), None, ALU.mult))
            link(V.scalar_tensor_tensor(rs[9], iota[:, 0:E], -float(T), base_e[:, TT, :], ALU.mult, ALU.add))
            link(V.tensor_tensor(prob_e, rs[9].unsqueeze(2).broadcast_to([P, E, TT]),
                                 rs[8].unsqueeze(1).broadcast_to([P, E, TT]), ALU.is_gt))
            link(V.tensor_reduce(rs[9], prob_e, AX_X, ALU.add))
            link(V.tensor_tensor_scan(rs[8], cst[:, C_ONES:C_ONES + E], rs[9], 0.0, ALU.mult, ALU.add))
            link(V.tensor_tensor(ecmp, iota.unsqueeze(2).broadcast_to([P, 24, E]),
                                 rs[8].unsqueeze(1).broadcast_to([P, 24, E]), ALU.is_ge))
            link(V.tensor_reduce(eid_f, ecmp, AX_X, ALU.add))
            link(V.tensor_tensor(ecmp, ecmp, rs[9].unsqueeze(1).broadcast_to([P, 24, E]), ALU.mult))
            first_tile = bias_sb[:, 192:216]
            link(V.tensor_reduce(first_tile, ecmp, AX_X, ALU.add))
            link(V.scalar_tensor_tensor(first_tile, eid_f, float(TT), first_tile, ALU.mult, ALU.subtract))
            link(V.tensor_tensor(first_tile, first_tile, iota, ALU.add))
            V.tensor_scalar(region[:, :], first_tile, float(SLOT_TILES - 1), None, ALU.min)
            V.tensor_scalar(eid[:, :], eid_f, float(E - 1), None, ALU.min).then_inc(s_table, 1)
            def expert_act(i, b):
                dve.wait_ge(s_esg, i + 1)
                dve.wait_ge(s_eu, i + 1)
                V.tensor_tensor(ea[:, b].rearrange("p (a c) -> p a c", a=2), eg, ps[:, 2:4, 0:IH],
                                ALU.mult).then_inc(s_ea, 1)

            def expert_xT(i, b):
                dve.wait_ge(s_xhi, i + 1)
                V.tensor_tensor(xsT[1][b], ps[:, 7, 0:D].rearrange("p (k t) -> p k t", k=KD), xsT[0][b].bitcast(F32),
                                ALU.subtract).then_inc(s_exT, 1)
                now = bass.ds(i, 1)
                V.tensor_copy(dest[:, now], xs[:, b, D:D + 1])
                V.tensor_scalar(w_first[:, now], xs[:, b, D + 1:D + 2], eid_f[:, now], xs[:, b, D + 2:D + 3],
                                ALU.is_equal, ALU.mult)
                V.tensor_scalar(w_second[:, now], xs[:, b, D + 1:D + 2], eid_f[:, now], xs[:, b, D + 3:D + 4],
                                ALU.not_equal, ALU.mult).then_inc(s_dest, 1)

            def weights_lo(i, w, e):
                dve.wait_ge(s_whi[w], i + 1)
                hi, lo = (a.rearrange("p k n -> p (k n)").unsqueeze(1) for a in split_w[w])
                V.tensor_tensor(lo, (ew1, ew3)[w][:, bass.ds(e, 1), :], hi.bitcast(F32),
                                ALU.subtract).then_inc(s_wlo[w], 1)

            def expert_of(i):
                return nc.vector.value_load(eid[0:1, bass.ds(i, 1)], min_val=0, max_val=E - 1)

            def slot_tails(i, b, first=False):
                dve.wait_ge(s_dest, i + 1)
                if not first:
                    dve.wait_ge(s_eys, 16 * (i - 1))
                now = bass.ds(i, 1)
                V.tensor_copy(dest_now[:, b:b + 1], dest[:, now])
                V.tensor_tensor(w_now[:, b:b + 1], w_first[:, now], w_second[:, now], ALU.add).then_inc(s_now, 1)

            def expert_aT(i, b):
                dve.wait_ge(s_eat, i + 1)
                V.tensor_copy(eaT[:, b, 4, :], ps[:, 5, 0:P])
                V.tensor_copy(eaT[0:ILAST, b, 5, :], ps[0:ILAST, 5, P:2 * P]).then_inc(s_ead, 1)

            dve.wait_ge(s_table, 1)
            e = expert_of(0)
            for w in range(2):
                weights_lo(0, w, e)
            expert_xT(0, 0)
            expert_xT(1, 1)
            e = expert_of(1)
            weights_lo(1, 0, e)
            expert_act(0, 0)
            weights_lo(1, 1, e)

            def body(i, b, first=False):
                e = expert_of(i + 2)
                expert_xT(i + 2, b)
                expert_aT(i, b)
                slot_tails(i, b, first)
                expert_act(i + 1, 1 - b)
                for w in range(2):
                    weights_lo(i + 2, w, e)

            body(0, 0, first=True)
            body(1, 1, first=True)
            with dve.Fori(1, LAST // 2 - 1) as j:
                for b in range(2):
                    body(2 * j + b, b)
            body(LAST - 2, 0)
            expert_aT(LAST - 1, 1)
            expert_act(LAST, 0)
            slot_tails(LAST - 1, 1)
            expert_aT(LAST, 0)
            slot_tails(LAST, 0)

        @block.tensor
        def _(pe):
            mm = nc.tensor.matmul

            def transposes(ph, g):
                if ph or g:
                    pe.wait_ge(s_hT, GROUPS * ph + g)
                for t in range(g * GT, (g + 1) * GT):
                    pe.wait_ge(s_hh, TT * ph + t + 1)
                    for k in range(KD):
                        last = nc.tensor.transpose(ps[:, k, (t % GT) * P:(t % GT + 1) * P],
                                                   hh[:, t, k * P:(k + 1) * P], ident)
                last.then_inc(s_tr, 1)

            pe.wait_ge(s_ident, 16)
            transposes(PH_MIX, 0)
            transposes(PH_MIX, 1)
            pe.wait_ge(s_const, 16)
            pe.wait_ge(s_win, 16)
            for q, (g, fb) in enumerate(IN_FILLS):
                if q < 2 * CONV_BLOCKS and q % CONV_BLOCKS == 0:
                    pe.wait_ge(s_hT, g + 1)
                if q == CONV_BLOCKS:
                    for t in range(TT):
                        for k in range(KD):
                            last = mm(ps[:, 6, 64 + H_SSD * t:64 + H_SSD * (t + 1)], hT[:, k, t * P:(t + 1) * P],
                                      win_sb[:, k, 6 * P:], start=(k == 0), stop=(k == KD - 1))
                    last.then_inc(s_dtp, 1)
                if q >= 4:
                    pe.wait_ge(s_evac, q - 3)
                for k in range(KD):
                    last = mm(ps[:, 2 + q % 4, :], win_sb[:, k, fb * P:(fb + 1) * P],
                              hT[:, k, g * GW:(g + 1) * GW], start=(k == 0), stop=(k == KD - 1))
                last.then_inc(s_proj, 1)
            pe.wait_ge(s_dtv, 4)
            da = dts_t[:, 16:32]
            mm(ps[:, 6, 0:16], gt_m, da, start=True, stop=True)
            mm(ps[:, 6, 16:32], ones, da, start=True, stop=True).then_inc(s_decp, 1)

            def front(c):
                cols = slice(c * P, (c + 1) * P)
                if c == 0:
                    pe.wait_ge(s_cbf, 1)
                    pe.wait_ge(s_evac, len(IN_FILLS))
                if c in (0, GT):
                    pe.wait_ge(s_xbc, (c // GT + 1) * CONV_BLOCKS)
                if c >= 1:
                    pe.wait_ge(s_tok, c)
                for k in range(2):
                    last = nc.tensor.transpose(ps[:, 0, k * P:(k + 1) * P], cv[:, k, cols], ident)
                last.then_inc(s_front_tr, 1)
                pe.wait_ge(s_ramp, c + 1)
                if c >= 1:
                    pe.wait_ge(s_exp, c)
                rmp = ramp[:, c % 2]
                mm(ps[:, 2, 0:2 * P], gt_m, rmp, start=True, stop=False)
                mm(ps[:, 2, 0:2 * P], ident_b[:, :], neg_s[:, :], start=False, stop=True)
                mm(ps[:, 2, 2 * P:4 * P], ones, rmp, start=True, stop=True).then_inc(s_front_seg, 1)
                if c >= 1:
                    pe.wait_ge(s_mt, c)
                mm(ps[:, 1, 0:2 * P], cv[:, 1, cols], cv[:, 2:4, cols], start=True, stop=True).then_inc(s_front_g, 1)

            def back(c):
                b = c % 2
                if c >= 1:
                    pe.wait_ge(s_state, c)
                if c < TT - 1:
                    pe.wait_ge(s_ddx, c + 1)
                    mm(ps[:, 5, 0:2 * P], tok[:, b, P:2 * P], ddx[:, b], start=True, stop=True).then_inc(s_st, 1)
                pe.wait_ge(s_mt, c + 1)
                if c >= 2:
                    pe.wait_ge(s_yg, c - 1)
                last = mm(ps[:, 3 + b, 0:2 * P], tok[:, b, 0:P], mt[:, b], start=True, stop=(c == 0))
                if c:
                    pe.wait_ge(s_ce, c)
                    for h in range(H_SSD):
                        last = mm(ps[:, 3 + b, h * P:(h + 1) * P], state[:, b, h], ce[:, b, h * P:(h + 1) * P],
                                  start=False, stop=(h == 1))
                last.then_inc(s_y, 1)

            def square_sum(c):
                pe.wait_ge(s_sq, c + 1)
                for h in range(H_SSD):
                    last = mm(ps[:, 7, c:c + 1], sq[:, c % 2, h * P:(h + 1) * P], ones[:, 0:1],
                              start=(h == 0), stop=(h == 1))
                last.then_inc(s_ss, 1)

            front(0)
            for c in range(TT):
                if c < TT - 1:
                    front(c + 1)
                back(c)
                if c:
                    square_sum(c - 1)
            square_sum(TT - 1)
            pe.wait_ge(s_wn, KD)
            for t in range(TT):
                if t >= 2:
                    pe.wait_ge(s_r2, t - 1)
                for k in range(KD):
                    last = mm(ps[:, 5 + t % 2, 0:D], yg[:, k, t * P:(t + 1) * P], wout_sb[:, k, :],
                              start=(k == 0), stop=(k == KD - 1))
                last.then_inc(s_mo, 1)
            transposes(PH_FFN, 0)
            pe.wait_ge(s_ffnw, 32)
            pe.wait_ge(s_r2, TT)
            for g in range(GROUPS):
                pe.wait_ge(s_hT, GROUPS * PH_FFN + g + 1)
                for f in range(FB):
                    q = g * FB + f
                    if q >= 2:
                        pe.wait_ge(s_fa, q - 1)
                    for w in range(2):
                        for k in range(KD):
                            last = mm(ps[:, 2 + 2 * w + q % 2, :], fw13[:, w, k, f * P:(f + 1) * P],
                                      hT[:, k, g * GW:(g + 1) * GW], start=(k == 0), stop=(k == KD - 1))
                    last.then_inc(s_gu, 1)
                transposes(*((PH_FFN, 1) if g == 0 else (PH_FAC, 0)))
                for t in range(g * GT, (g + 1) * GT):
                    if t >= 2:
                        pe.wait_ge(s_x1, t - 1)
                    pe.wait_ge(s_fa, (g + 1) * FB)
                    for f in range(FB):
                        last = mm(ps[:, 6 + t % 2, 0:D], ffn_a[g][:, f, (t % GT) * P:(t % GT + 1) * P],
                                  fw2[:, f, :], start=(f == 0), stop=(f == FB - 1))
                    last.then_inc(s_fo, 1)
            pe.wait_ge(s_fsum, 1)
            for t in range(TT):
                if t == GT:
                    transposes(PH_FAC, 1)
                if t % GT == 0:
                    pe.wait_ge(s_hT, GROUPS * PH_FAC + t // GT + 1)
                pe.wait_ge(*((s_x1, TT - 1 + t) if t < 2 else (s_x2, t - 1)))
                for k in range(KD):
                    last = mm(ps[:, 6 + t % 2, 0:D], hT[:, k, t * P:(t + 1) * P], mixed_w[:, k, :],
                              start=(k == 0), stop=(k == KD - 1))
                last.then_inc(s_mx, 1)
            transposes(PH_ATT, 0)
            pe.wait_ge(s_wqsum, 1)
            pe.wait_ge(s_kv, 32)
            for q in range(GROUPS * 12):
                g, j = divmod(q, 12)
                if q == 9:
                    transposes(PH_ATT, 1)
                if j == 0:
                    pe.wait_ge(s_hT, GROUPS * PH_ATT + g + 1)
                if q == 4:
                    pe.wait_ge(s_x2, TT)
                if q >= 6:
                    if is_k(q - 6) or q % 2:
                        pe.wait_ge(s_qd, vector_fills(q - 6))
                    else:
                        pe.wait_ge(s_qa, scalar_fills(q - 6))
                for k in range(KD):
                    bank = ps[:, 2 + q % 6, :]
                    if j < 8:
                        w = wq_sum if j < 4 else wk_sb
                        last = mm(bank, w[:, k, (j % 4) * P:(j % 4 + 1) * P], hT[:, k, g * GW:(g + 1) * GW],
                                  start=(k == 0), stop=(k == KD - 1))
                    else:
                        t = g * GT + j - 8
                        last = mm(bank, hT[:, k, t * P:(t + 1) * P], wv_sb[:, k, :],
                                  start=(k == 0), stop=(k == KD - 1))
                last.then_inc(s_qkv, 1)
            pe.wait_ge(s_qa, scalar_fills(FILLS - 1))
            pe.wait_ge(s_qd, vector_fills(FILLS - 1))

            def scores(u):
                i, n = divmod(u, HEADS)
                half = slice(64 * (n % 2), 64 * (n % 2) + 64)
                if u >= 2:
                    pe.wait_ge(s_pr, u - 1)
                pe.wait_ge(s_qs, 2 * (u // 2) + 2)
                for a in range(i // 4 + 1):
                    w = min((i + 1) * P - a * 512, 512)
                    mm(ps[:, 2 * (u % 2) + a, 0:w], q_split[:, n, :], k_hi[:, n, a * 512:a * 512 + w],
                       start=True, stop=False)
                    mm(ps[:, 2 * (u % 2) + a, 0:w], q_split[half, n, :], k_lo[half, n // 2, a * 512:a * 512 + w],
                       start=False, stop=(a < i // 4))
                c = (i % 4) * P
                mm(ps[:, 2 * (u % 2) + i // 4, c:c + P], ident_b[:, :], neg_a[:, :],
                   start=False, stop=True).then_inc(s_sc, 1)

            def probs_transposed(u):
                i, n = divmod(u, HEADS)
                pe.wait_ge(s_pn, u + 1)
                if u >= 1:
                    pe.wait_ge(s_pT, u)
                for j in range(i + 1):
                    last = nc.tensor.transpose(ps[:, 4 + j // 4, (j % 4) * P:(j % 4 + 1) * P],
                                               probs[u % 4][:, j * P:(j + 1) * P], ident)
                last.then_inc(s_pt, 1)

            def attended(m):
                i, pair = divmod(m, HEADS // 2)
                pe.wait_ge(s_pT, 2 * m + 2)
                if pair == 0 and i >= 2:
                    pe.wait_ge(s_slots, i - 1)
                for j in range(i + 1):
                    for h in range(2):
                        n = 2 * pair + h
                        last = mm(ps[h * DH:(h + 1) * DH, 6 + i % 2, pair * P:(pair + 1) * P],
                                  v_sb[:, j, n * DH:(n + 1) * DH], pT[(2 * m + h) % 4][:, j * P:(j + 1) * P],
                                  start=(j == 0), stop=(j == i))
                last.then_inc(s_pv, 1)

            def attention_out(i):
                pe.wait_ge(s_zT, i + 1)
                for c in range(QB):
                    last = mm(ps[:, 6 + i % 2, 0:D], zT[:, c, :], wo_sb[:, c, :], start=(c == 0), stop=(c == QB - 1))
                last.then_inc(s_ao, 1)

            pe.wait_ge(s_wo, 16)
            def route_transposed(i):
                pe.wait_ge(s_hh, TT * PH_MOE + i + 1)
                for k in range(KD):
                    last = nc.tensor.transpose(ps[:, 6 + i % 2, k * P:(k + 1) * P], hh[:, i, k * P:(k + 1) * P], ident)
                last.then_inc(s_rT, 1)

            def route_logits(i):
                pe.wait_ge(s_rTc, i + 1)
                for k in range(KD):
                    last = mm(ps[:, 6 + i % 2, D:D + E], routed_T[:, i % 2, k * P:(k + 1) * P], gate_sb[:, k, :],
                              start=(k == 0), stop=(k == KD - 1))
                last.then_inc(s_lg, 1)

            def route_counts(i):
                pe.wait_ge(s_chosen, i + 1)
                mm(ps[:, 6 + i % 2, D + E:D + 2 * E], lt_m, chosen[:, i, :], start=True, stop=True)
                mm(ps[:, 6 + i % 2, D + 2 * E:D + 3 * E], ones, chosen[:, i, :], start=True, stop=True).then_inc(s_cnt, 1)

            pe.wait_ge(s_gate, 32)
            for u in range((TT + 1) * HEADS + 5):
                if u < TT * HEADS:
                    scores(u)
                if 3 <= u < TT * HEADS + 3:
                    probs_transposed(u - 3)
                if HEADS <= u < (TT + 1) * HEADS and u % HEADS == 5:
                    attention_out(u // HEADS - 1)
                if HEADS <= u < (TT + 1) * HEADS and u % HEADS == 7:
                    route_transposed(u // HEADS - 1)
                if u >= 2 * HEADS and u % HEADS == 0:
                    route_logits(u // HEADS - 2)
                if u >= 2 * HEADS and u % HEADS == 4:
                    route_counts(u // HEADS - 2)
                if 4 <= u < TT * HEADS + 4 and u % 2:
                    attended((u - 4) // 2)

            def expert_x(i, b):
                pe.wait_ge(s_xs[b], 8 * (i - b) + 16)
                for k in range(KD):
                    last = nc.tensor.transpose(ps[:, 7, k * P:(k + 1) * P], xs[:, b, k * P:(k + 1) * P], ident)
                last.then_inc(s_ext, 1)

            def expert_up(i, b):
                pe.wait_ge(s_exT, i + 1)
                for w, done in enumerate((s_eg, s_eu)):
                    pe.wait_ge(s_wlo[w], i + 1)
                    for a in range(2):
                        for k in range(KD):
                            for px, pw in ((0, 0), (0, 1), (1, 0)):
                                last = mm(ps[:, 2 * w + a, 0:IH], xsT[px][b][:, k, :],
                                          split_w[w][pw][:, k, a * IH:(a + 1) * IH],
                                          start=(k == 0 and px == pw), stop=(k == KD - 1 and px == 1))
                    last.then_inc(done, 1)

            def expert_aT(i, b):
                pe.wait_ge(s_ea, i + 1)
                for c in range(IB):
                    w = min(P, I - c * P)
                    last = nc.tensor.transpose(ps[0:w, 4 + c // 4, (c % 4) * P:(c % 4 + 1) * P],
                                               ea[:, b, c * P:c * P + w], ident)
                last.then_inc(s_eat, 1)

            def expert_down(i, b, first=False):
                e = nc.tensor.value_load(eid[0:1, bass.ds(i, 1)], min_val=0, max_val=E - 1)
                pe.wait_ge(s_eaa, i + 1)
                pe.wait_ge(s_ead, i + 1)
                if not first:
                    pe.wait_ge(s_eyc, i)
                we = ew2[:, bass.ds(e, 1), :].rearrange("p e (c n) -> p (e c) n", c=IB)
                for c in range(IB):
                    w = min(P, I - c * P)
                    last = mm(ps[:, 6, 0:D], eaT[0:w, b, c, :], we[0:w, c, :], start=(c == 0), stop=(c == IB - 1))
                last.then_inc(s_ey, 1)

            pe.wait_ge(s_e13, 2 * E * 16)
            pe.wait_ge(s_table, 1)
            expert_x(0, 0)
            pe.wait_ge(s_exT, 1)
            expert_x(1, 1)
            expert_up(0, 0)
            pe.wait_ge(s_e2, (E + 1) * 16)

            def body(i, b, first=False):
                pe.wait_ge(s_exT, i + 2)
                expert_x(i + 2, b)
                expert_aT(i, b)
                expert_up(i + 1, 1 - b)
                expert_down(i, b, first)

            body(0, 0, first=True)
            body(1, 1)
            with pe.Fori(1, LAST // 2 - 1) as j:
                for b in range(2):
                    body(2 * j + b, b)
            body(LAST - 2, 0)
            expert_aT(LAST - 1, 1)
            expert_up(LAST, 0)
            expert_down(LAST - 1, 1)
            expert_aT(LAST, 0)
            expert_down(LAST, 0)


def constants():
    c = np.zeros((P, N_CONST), np.float32)
    r = np.arange(P)
    c[:, C_IDENT:C_IDENT + P] = np.eye(P)
    c[:, C_LE:C_LE + P] = r[:, None] <= r[None, :]
    c[:, C_GT:C_GT + P] = r[:, None] > r[None, :]
    c[:, C_LT:C_LT + P] = r[:, None] < r[None, :]
    c[:, C_ONES:C_ONES + P] = 1.0
    c[:, C_NEGS:C_NEGS + P] = np.where(r[None, :] < r[:, None], MASK, 0.0)
    c[:, C_NEGA:C_NEGA + P] = np.where(r[None, :] > r[:, None], MASK, 0.0)
    c[:, C_IOTA:C_IOTA + 24] = np.arange(24)[None, :]
    c[:, C_TOKEN:C_TOKEN + TT + 1] = np.arange(TT + 1)[None, :] * P + r[:, None]
    return c


def kernel(**inputs):
    import concourse.bacc as bacc
    from concourse.bass_utils import run_bass_kernel_spmd as run

    a = {k: np.asarray(v) for k, v in inputs.items()}

    def cols(v, n):
        return v.reshape(n, P).T

    def chunks(w):
        return w.reshape(w.shape[0] // P, P, w.shape[1]).transpose(1, 0, 2)

    small = np.concatenate(
        [cols(a["L0_attn_ln1_w"], 2), cols(a["L0_attn_norm_w"], 2), cols(a["L0_attn_ln2_w"], 2),
         a["L0_attn_conv_w"].reshape(TAPS, CONV_BLOCKS, P).transpose(2, 1, 0).reshape(P, -1),
         cols(a["L0_attn_conv_b"], CONV_BLOCKS)]
        + [np.broadcast_to(a[n][None, :], (P, H_SSD)) for n in ("L0_attn_dt_bias", "L0_attn_A_log", "L0_attn_D")],
        axis=1)
    heads_q = a["L1_attn_W_Q"].reshape(HEADS, QH, KD, P, DH).transpose(3, 1, 2, 0, 4).reshape(P, QH, KD * QKV)

    def heads(w):
        return w.reshape(HEADS, KD, P, DH).transpose(2, 1, 0, 3).reshape(P, KD, QKV)

    def expert_up(w):
        return w.transpose(2, 0, 1).reshape(KD, P, E, I).transpose(1, 2, 0, 3).reshape(P, E, KD * I)

    w2 = a["L1_ffn_w2"].transpose(0, 2, 1)
    full = (IB - 1) * P
    data = {
        "x_in": a["L0_attn_hidden_states"].reshape(T, D),
        "small_in": small,
        "const_in": constants(),
        "w_in": a["L0_attn_W_in"],
        "w_out": a["L0_attn_W_out"],
        "f_w13": np.stack([chunks(a["L0_attn_w1"]), chunks(a["L0_attn_w3"])], axis=1),
        "f_w2": a["L0_attn_w2"],
        "factors": a["L0_ffn_factors"].reshape(RANK, KD, P, D).transpose(2, 0, 1, 3).reshape(P, RANK, KD * D),
        "ffn_bias": np.broadcast_to(a["L0_ffn_bias"][None, :], (P, D)),
        "wq": heads_q,
        "wk": heads(a["L1_attn_W_K"]),
        "wv": heads(a["L1_attn_W_V"]),
        "wo": a["L1_attn_W_O"].reshape(QKV, D),
        "gate": a["L1_ffn_gate_w"].T.reshape(KD, P, E).transpose(1, 0, 2),
        "m_w1": expert_up(a["L1_ffn_w1"]),
        "m_w3": expert_up(a["L1_ffn_w3"]),
        "m_w2": w2[:, :full].reshape(E, IB - 1, P, D).transpose(2, 0, 1, 3).reshape(P, E, full // P * D),
        "m_w2t": w2[:, full:].transpose(1, 0, 2),
    }
    nc = bacc.Bacc("TRN2", target_bir_lowering=False, num_devices=1)
    arrays, args = {}, []
    for name, v in data.items():
        v = np.ascontiguousarray(v)
        arrays[name] = v
        args.append(nc.dram_tensor(name, v.shape, mybir.dt.from_np(v.dtype), kind="ExternalInput").ap())
    out = nc.dram_tensor("out", (T + P, D), F32, kind="ExternalOutput").ap()
    build(nc, *args, out)
    r = run(nc, [arrays], core_ids=[0])
    return r.results[0]["out"][:T].reshape(1, T, D)
```

```python
from contextlib import ExitStack

import numpy as np

import concourse.bass as bass
from concourse import mybir

F32 = mybir.dt.float32
F32R = mybir.dt.float32r
BF16 = mybir.dt.bfloat16
I32 = mybir.dt.int32
U32 = mybir.dt.uint32
ALU = mybir.AluOpType
ACT = mybir.ActivationFunctionType
AX_X = mybir.AxisListType.X

P = 128
T = 1024
TT = T // P
D = 256
KD = D // P
GT = 4
GROUPS = TT // GT
GW = GT * P
EPS = 1e-5
H_SSD = 2
N_IN = 770
CONV_BLOCKS = 4
TAPS = 4
FF = 1024
FB = FF // P
RANK = 8
HEADS = 8
DH = 64
QH = 32 // HEADS
QKV = HEADS * DH
QB = QKV // P
E = 8
I = 704
IH = I // 2
IB = (I + P - 1) // P
ILAST = I - (IB - 1) * P
TOP = 2
TILES_MAX = TOP * T // P + E - 1
SLOT_TILES = E * TT + 1
SLOT_W = D + 4
MASK = -1.0e30

C_LN1, C_NORM, C_LN2, C_CONVW, C_CONVB, C_DTB, C_ALOG, C_D = 0, 2, 4, 6, 22, 26, 28, 30
N_SMALL = 32
C_IDENT, C_LE, C_GT, C_LT, C_ONES, C_NEGS, C_NEGA, C_IOTA = 0, 128, 256, 384, 512, 640, 768, 896
C_TOKEN = C_IOTA + 24
N_CONST = C_TOKEN + TT + 1


def build(nc, x_in, small_in, const_in, w_in, w_out, f_w13, f_w2, factors, ffn_bias, wq, wk, wv, wo,
          gate, m_w1, m_w3, m_w2, m_w2t, out):
    slots_in = nc.dram_tensor("expert_in", [SLOT_TILES * P, SLOT_W], F32, kind="Internal").ap()
    with ExitStack() as ctx:
        def sb(name, cols, dt=F32):
            return ctx.enter_context(nc.sbuf_tensor(name, [P, cols], dt))

        def sem(name):
            return ctx.enter_context(nc.semaphore(name))

        def view(tensor, start, *dims):
            n = int(np.prod(dims))
            a = tensor[:, start:start + n]
            if len(dims) == 2:
                return a.rearrange("p (a b) -> p a b", a=dims[0])
            if len(dims) == 3:
                return a.rearrange("p (a b c) -> p a b c", a=dims[0], b=dims[1])
            return a

        def overlay(name, below, cols):
            with ExitStack() as scope:
                if below:
                    scope.enter_context(nc.sbuf_tensor(name + "_below", [P, below], F32))
                return scope.enter_context(nc.sbuf_tensor(name, [P, cols], F32R))

        K_AT = 2 * E * KD * I - HEADS * T
        k_hi = view(overlay("k_hi", K_AT, HEADS * T), 0, HEADS, T)
        FAC_AT = -(-KD * N_IN // 8) * 8
        WQ_AT = FAC_AT + RANK * KD * D
        qkv_w = [view(overlay(name, below, 3 * KD * QKV), 0, 3, KD * QKV)
                 for name, below in (("qkv_w_hi", WQ_AT + KD * QKV), ("qkv_w_lo", FAC_AT + KD * D))]
        hT_lo = view(overlay("hT_lo", WQ_AT + QH * KD * QKV + KD * T, KD * T), 0, KD, T)
        A_AT = WQ_AT + QH * KD * QKV + 2 * KD * T
        ffn_a = [view(overlay(name, A_AT + i * FB * GW, FB * GW), 0, FB, GW)
                 for i, name in enumerate(("ffn_a_hi", "ffn_a_lo"))]
        early = sb("early", 2 * E * KD * I)
        k_lo = view(overlay("k_lo", QB * T, QB * T), 0, QB, T)
        fw13_split = [view(overlay(name, below, 2 * KD * FF), 0, 2 * KD, FF)
                      for name, below in (("ffn_w_hi", E * IB * D - 2 * KD * FF), ("ffn_w_lo", 0))]
        fw2_split = [view(overlay(name, below, FB * D), 0, FB, D)
                     for name, below in (("ffn_w2_hi", 2 * KD * FF + FB * D), ("ffn_w2_lo", 2 * KD * FF))]
        mid = sb("mid", E * IB * D)
        at = 0
        win_sb = view(early, at, KD, N_IN); at += FAC_AT
        fac_sb = view(early, at, RANK, KD * D); at += RANK * KD * D
        wq_sb = view(early, at, QH, KD * QKV); at += QH * KD * QKV
        zs = view(early, at, KD, T); kv_at = at; at += KD * T
        yg = view(early, at, KD, T); at += KD * T
        xpad = view(early, at, CONV_BLOCKS, T + TAPS - 1)
        at += CONV_BLOCKS * (T + TAPS - 1)
        cv = view(early, at, CONV_BLOCKS, T)
        at += CONV_BLOCKS * T
        assert at <= 2 * E * KD * I
        mixed_w = view(early, FAC_AT, KD, D)
        ffn_act = [early[:, i * GW:(i + 1) * GW] for i in range(2)]
        qkv_src = [early[:, c:c + KD * QKV] for c in (WQ_AT, kv_at, kv_at + KD * QKV)]
        ew1 = view(early, 0, E, KD * I)
        ew3 = view(early, E * KD * I, E, KD * I)

        at = 0
        fw13 = mid[:, at:at + 2 * KD * FF].rearrange("p (w k n) -> p w k n", w=2, k=KD); at += 2 * KD * FF
        fw2 = view(mid, at, FB, D); at += FB * D
        wout_sb = view(mid, at, KD, D); at += KD * D
        tok = view(mid, at, 2, 2 * P); at += 4 * P
        ddx = view(mid, at, 2, H_SSD * P); at += 4 * P
        ramp = view(mid, at, 2, H_SSD * P); at += 4 * P
        decays = view(mid, at, 2, 4 * P); at += 8 * P
        mt = view(mid, at, 2, H_SSD * P); at += 4 * P
        ce = view(mid, at, 2, H_SSD * P); at += 4 * P
        sq = view(mid, at, 2, H_SSD * P); at += 4 * P
        state = view(mid, at, 2, H_SSD, P); at += 2 * H_SSD * P
        assert at <= E * IB * D
        qT = view(mid, 0, QB, T)
        v_sb = view(mid, 2 * QB * T, TT, QKV)
        ew2 = view(mid, 0, E, IB * D)

        q_split = view(overlay("q_split", 5120, HEADS * P), 0, HEADS, P)
        work = sb("work", 7 * 1024)
        wo_sb = view(work, 6144, QB, D)
        sgate = [view(work, 0, GW), view(work, GW, GW)]
        at = 0
        xs = view(work, at, 2, SLOT_W); at += 2 * SLOT_W
        eg = view(work, at, 2, IH); at += I
        ea = view(work, at, 2, I); at += 2 * I
        eaT = view(work, at, 2, IB, P); at += 2 * IB * P
        ey = view(work, at, 2, D); at += 2 * D
        assert at <= 7 * 1024
        cst = sb("cst", N_CONST)
        ident, le_m, gt_m, lt_m, ones = (cst[:, c:c + P] for c in (C_IDENT, C_LE, C_GT, C_LT, C_ONES))
        iota = cst[:, C_IOTA:C_IOTA + 24]
        small = sb("small", N_SMALL)
        bias_sb = sb("bias_sb", D)
        gate_t = sb("gate_sb", KD * E); gate_sb = view(gate_t, 0, KD, E)
        ident_b = sb("ident_b", P, BF16)
        neg_s = sb("neg_s", H_SSD * P, BF16)
        neg_a = sb("neg_a", P, BF16)
        stats_t = sb("stats", TT * 6); stats = view(stats_t, 0, TT, 6)
        mv_t = sb("mv", TT * 2); mv = view(mv_t, 0, TT, 2)
        veps = sb("veps", TT); rstd = sb("rstd", TT)
        veps2 = sb("veps2", TT); rstd2 = sb("rstd2", TT)
        mhalf = sb("mhalf", TT)
        idle_act = veps2
        pad = sb("pad", SLOT_W)
        dts_t = sb("dts", 10 * TT * H_SSD)
        dts = [view(dts_t, i * TT * H_SSD, TT, H_SSD) for i in range(10)]
        ea_log = sb("ea_log", H_SSD)
        dec_t = sb("dec", 2 * TT * H_SSD)
        dec = view(dec_t, 0, 2, TT, H_SSD)
        nmax = sb("nmax", TT * HEADS)
        psums = sb("psums", TT * HEADS)
        pinv = sb("pinv", TT * HEADS)
        rt_t = sb("rt", 8 * TT * E)
        prob_e, top_v, chosen = (view(rt_t, i * TT * E, TT, E) for i in range(3))
        onehot = view(rt_t, 3 * TT * E, TT, TOP, E)
        slot_e = view(rt_t, 5 * TT * E, TT, TOP, E)
        rank_e = view(rt_t, 7 * TT * E, TT, E)
        base_e = view(dts_t, 0, TT + 1, E)
        rs_t = sb("rs", 12 * TT)
        rs = [rs_t[:, i * TT:(i + 1) * TT] for i in range(12)]
        top_f = view(rs_t, 8 * TT, TT, TOP)
        slot_f = view(rs_t, 10 * TT, TT, TOP)
        top_i_t = sb("top_i", TT * 8, U32); top_i = view(top_i_t, 0, TT, 8)
        slot_i_t = sb("slot_i", TOP * TT, U32); slot_i = view(slot_i_t, 0, TT, TOP)
        ecmp = view(bias_sb, 0, 24, E)
        eid_f = bias_sb[:, 216:240]
        eid = sb("eid", 24, I32)
        region = sb("region", 24, I32)
        dest = top_i_t[:, 0:24]
        w_first, w_second = bias_sb[:, 0:24], bias_sb[:, 24:48]
        dest_now = slot_i_t[:, 0:2]
        w_now = rs_t[:, 0:2]
        hT_hi = view(overlay("hT_hi", 2 * TT * D, KD * T), 0, KD, T)
        hT_split = (hT_hi, hT_lo)
        with nc.sbuf_tensor("rows", [P, 2 * TT * D + KD * T + TT * SLOT_W], F32) as rows_t:
            x = view(rows_t, 0, TT, D)
            xn_t = rows_t[:, TT * D:2 * TT * D]
            xn = view(xn_t, 0, TT, D)
            hT_t = rows_t[:, 2 * TT * D:2 * TT * D + KD * T]
            hT = view(hT_t, 0, KD, T)
            slot_rows = view(rows_t, 2 * TT * D + KD * T, TT, SLOT_W); hh = slot_rows[:, :, 0:D]
        zT = view(hT_t, 1024, QB, P)
        routed_T = view(hT_t, 1536, 2, KD * P)
        probs = [work[:, b * 1024:(b + 1) * 1024] for b in range(3)] + [hT_t[:, 0:1024]]
        pT = [work[:, 3072:4096], work[:, 4096:5120], xn_t[:, 0:1024], xn_t[:, 1024:2048]]
        split_t = sb("split", 4 * KD * I, F32R)
        split_w = [[view(split_t, (w * 2 + part) * KD * I, KD, I) for part in range(2)] for w in range(2)]
        xsT_t = sb("xsT", 4 * D, F32R)
        xsT = [[view(xsT_t, (2 * part + b) * D, KD, P) for b in range(2)] for part in range(2)]
        ps = ctx.enter_context(nc.psum_tensor("ps", [P, 8, 512], F32))

        s_x = [sem(f"x_loaded{g}") for g in range(GROUPS)]
        s_ident = sem("identity_loaded")
        s_small, s_const, s_win, s_mixw, s_ffnw = (sem(n) for n in (
            "small_loaded", "const_loaded", "win_loaded", "wout_loaded", "ffnw_loaded"))
        s_fac, s_wq, s_kv, s_wo, s_gate = (sem(n) for n in (
            "factors_loaded", "wq_loaded", "kv_loaded", "wo_loaded", "gate_loaded"))
        s_e13, s_e2 = sem("expert_w13_loaded"), sem("expert_w2_loaded")
        s_pad, s_padded = sem("pad_set"), sem("slots_padded")
        s_cbf = sem("bf16_constants")
        s_pool0 = sem("pool_constants")
        s_var, s_rstd, s_hh, s_tr, s_hT = (sem(n) for n in (
            "variance", "rstd", "normalised", "transposed", "feature_major"))
        s_var2, s_rstd2 = sem("variance2"), sem("rstd2")
        s_proj, s_evac, s_conv, s_xbc = (sem(n) for n in ("in_proj", "in_evac", "conv_tap", "conv_silu"))
        s_dtp, s_dtv, s_dta = sem("dt_proj"), sem("dt_vector"), sem("dt_scalar")
        s_decp, s_dec, s_dd = sem("decay_sum"), sem("decay_exp"), sem("decay_dt")
        s_ramp, s_front_tr, s_front_seg, s_front_g = (sem(n) for n in (
            "ramp", "chunk_transposed", "segments", "bc_product"))
        s_tok, s_exp, s_mt, s_ce, s_ddx = (sem(n) for n in ("chunk_tokens", "decays", "mt", "ce", "ddx"))
        s_y, s_st, s_state, s_yg, s_sq, s_ss = (sem(n) for n in (
            "y_sum", "state_sum", "state", "y_gated", "y_squared", "square_sum"))
        s_yv, s_yr = sem("y_variance"), sem("y_rstd")
        s_wn = sem("wout_scaled")
        s_mo, s_r2 = sem("mixer_out"), sem("mixer_residual")
        s_xr = sem("x_plus_residual")
        s_gu, s_sg, s_fa, s_fo, s_x1 = (sem(n) for n in (
            "ffn_gate_up", "ffn_silu", "ffn_act", "ffn_out", "x1"))
        s_fsum, s_wqsum = sem("factors_summed"), sem("wq_summed")
        s_xb, s_mx, s_x2 = sem("x_plus_bias"), sem("mixing"), sem("x2")
        s_qkv, s_qa, s_qd = sem("qkv"), sem("qkv_scalar"), sem("qkv_vector")
        s_qhi, s_qs = sem("q_hi"), sem("q_split")
        s_sc, s_max, s_pr, s_pt, s_pT, s_pv = (sem(n) for n in (
            "scores", "row_max", "exponentials", "probs_transposed", "pT", "attended"))
        s_pinv, s_pn = sem("sum_reciprocal"), sem("probs_normalised")
        s_zT, s_ao, s_x3 = sem("zT"), sem("attn_out"), sem("x3")
        s_rT, s_rTc, s_lg, s_lmax, s_lexp, s_chosen, s_cnt = (sem(n) for n in (
            "routed_transposed", "routed_T", "logits", "logit_max", "logit_exp", "chosen", "counts"))
        s_slots, s_scat, s_table, s_dest = sem("slots"), sem("scattered"), sem("tile_table"), sem("destinations")
        s_now, s_idle = sem("slot_tails_ready"), sem("pool_waited")
        s_xs = [sem(f"slot_tile_loaded{b}") for b in range(2)]
        s_ext, s_exT, s_eg, s_eu, s_esg, s_ea = (sem(n) for n in (
            "slot_tile_transposed", "slot_tile_T", "expert_gate", "expert_up", "expert_silu", "expert_act"))
        s_eat, s_eaa, s_ead, s_ey, s_eyc = (sem(n) for n in (
            "act_transposed", "act_T_scalar", "act_T_vector", "expert_y", "expert_y_copied"))
        s_eys = sem("expert_y_scattered")
        s_xhi, s_eid = sem("slot_tile_hi"), sem("tile_experts")
        s_hTlo, s_fwhi, s_fwlo = sem("feature_major_lo"), sem("ffn_w_hi"), sem("ffn_w_lo")
        s_ahi, s_alo, s_f2hi, s_f2lo = (sem(n) for n in ("ffn_act_hi", "ffn_act_lo", "ffn_w2_hi", "ffn_w2_lo"))
        s_pwhi, s_pwlo = sem("qkv_w_hi"), sem("qkv_w_lo")
        s_whi = [sem(f"expert_w{w}_hi") for w in (1, 3)]
        s_wlo = [sem(f"expert_w{w}_lo") for w in (1, 3)]
        s_out = sem("residual_stored")
        s_dve, s_act, s_pool = sem("vector_chain"), sem("scalar_chain"), sem("pool_chain")

        FILLS = GROUPS * 12
        W_PARTS = ((0, 0), (1, 0), (0, 1))
        PARTS = ((0, 0), (0, 1), (1, 0))

        def is_k(q):
            return 4 <= q % 12 < 8

        def scalar_fills(q):
            return sum(is_k(i) or i % 2 == 0 for i in range(q + 1))

        def vector_fills(q):
            return sum(is_k(i) or i % 2 == 1 for i in range(q + 1))

        def qv_dst(q):
            g, j = divmod(q, 12)
            if j < 4:
                return qT[:, j, g * GW:(g + 1) * GW], float(DH) ** -0.5
            return v_sb[:, g * GT + j - 8, :], 1.0

        def k_parts(q):
            g, j = divmod(q, 12)
            c = slice(g * GW, (g + 1) * GW)
            for h in range(2):
                half, other = slice(h * DH, (h + 1) * DH), slice((1 - h) * DH, (2 - h) * DH)
                n = 2 * (j - 4) + h
                yield half, k_hi[half, n, c], k_hi[other, n, c], k_lo[half, j - 4, c]

        block = ctx.enter_context(nc.Block())
        PH_MIX, PH_FFN, PH_FAC, PH_ATT, PH_MOE = range(5)
        NORMS = [(PH_MIX, 0), (PH_MIX, 1), (PH_FFN, 0), (PH_FFN, 1), (PH_FAC, 0), (PH_ATT, 0), (PH_FAC, 1), (PH_ATT, 1)]

        def norms_to(ph, g):
            return NORMS.index((ph, g)) + 1

        def mixer_bank(t):
            return ps[:, 3 + t // 2, (t % 2) * D:(t % 2 + 1) * D]

        def mixing_bank(t):
            at = (t % 2) * D
            return ps[:, 2 + t // 2 if t < GT else (t - GT) // 2, at:at + D]

        IN_FILLS = [(g, fb) for g in range(GROUPS) for fb in range(2, 6)] + [(g, fb) for g in range(GROUPS)
                                                                            for fb in range(2)]
        LAST = TILES_MAX - 1

        @block.sync
        def _(sp):
            xv = x_in.rearrange("(t p) d -> p t d", p=P)
            for g in range(GROUPS):
                sp.dma_start(x[:, g * GT:(g + 1) * GT, :], xv[:, g * GT:(g + 1) * GT, :]).then_inc(s_x[g], 16)
            sp.dma_start(win_sb, w_in.rearrange("(k p) n -> p k n", p=P)).then_inc(s_win, 16)
            sp.dma_start(wout_sb, w_out.rearrange("(k p) n -> p k n", p=P)).then_inc(s_mixw, 16)
            sp.dma_start(fac_sb, factors).then_inc(s_fac, 16)
            sp.dma_start(wq_sb, wq).then_inc(s_wq, 16)
            sp.dma_start(fw13, f_w13).then_inc(s_ffnw, 16)
            sp.dma_start(fw2, f_w2.rearrange("(f p) n -> p f n", p=P)).then_inc(s_ffnw, 16)
            sp.dma_start(bias_sb[:, :], ffn_bias).then_inc(s_gate, 16)
            sp.dma_start(gate_sb, gate).then_inc(s_gate, 16)
            sp.wait_ge(s_pad, 1)
            for e in range(E):
                sp.dma_start(slots_in[e * T:(e + 1) * T, :].rearrange("(t p) w -> p t w", p=P),
                             pad[:, :].unsqueeze(1).broadcast_to([P, TT, SLOT_W])).then_inc(s_padded, 16)
            sp.dma_start(slots_in[E * T:, :], pad[:, :]).then_inc(s_padded, 16)
            sp.wait_ge(s_r2, TT)
            for dst, w in zip(qkv_src[1:], (wk, wv)):
                sp.dma_start(dst, w.rearrange("p k n -> p (k n)")).then_inc(s_kv, 16)
            sp.wait_ge(s_x1, TT)
            sp.dma_start(wo_sb, wo.rearrange("(c p) n -> p c n", p=P)).then_inc(s_wo, 16)
            sp.wait_ge(s_qa, scalar_fills(FILLS - 1))
            sp.wait_ge(s_qd, vector_fills(FILLS - 1))
            early_w3 = (K_AT - E * KD * I) // (KD * I)
            for e in range(E):
                sp.dma_start(ew1[:, e], m_w1[:, e]).then_inc(s_e13, 16)
            for e in range(early_w3):
                sp.dma_start(ew3[:, e], m_w3[:, e]).then_inc(s_e13, 16)
            sp.dma_start(out[T:, :], pad[:, 0:D]).then_inc(s_out, 16)
            for t in range(TT - 1):
                sp.wait_ge(s_x3, t + 1)
                sp.dma_start(out[t * P:(t + 1) * P, :], x[:, t, :]).then_inc(s_out, 16)
            for e in range(early_w3, E):
                heads_over = -(-(E * KD * I + (e + 1) * KD * I - K_AT) // T)
                sp.wait_ge(s_sc, (TT - 1) * HEADS + min(heads_over, HEADS))
                sp.dma_start(ew3[:, e], m_w3[:, e]).then_inc(s_e13, 16)
            sp.wait_ge(s_sc, TT * HEADS)
            below_v = 2 * QB * T // (IB * D)
            for e in range(below_v):
                sp.dma_start(ew2[:, e, 0:(IB - 1) * D], m_w2[:, e]).then_inc(s_e2, 16)
            sp.wait_ge(s_pv, TT * HEADS // 2)
            for e in range(below_v, E):
                sp.dma_start(ew2[:, e, 0:(IB - 1) * D], m_w2[:, e]).then_inc(s_e2, 16)
            sp.dma_start(mid[0:ILAST, :].rearrange("p (e r) -> p e r", e=E)[:, :, (IB - 1) * D:],
                         m_w2t).then_inc(s_e2, 16)
            sp.wait_ge(s_x3, TT)
            sp.dma_start(out[(TT - 1) * P:T, :], x[:, TT - 1, :]).then_inc(s_out, 16)

            def load_slots(i, b):
                tile = nc.sync.value_load(region[0:1, bass.ds(i, 1)], min_val=0, max_val=SLOT_TILES - 1)
                sp.dma_start(xs[:, b], slots_in[bass.ts(tile, P), :]).then_inc(s_xs[b], 16)

            sp.wait_ge(s_table, 1)
            sp.wait_ge(s_scat, TOP * TT * 16)
            for b in range(2):
                load_slots(b, b)
            with sp.Fori(0, LAST // 2 - 1) as j:
                for b in range(2):
                    sp.wait_ge(s_ext, 2 * j + b + 1)
                    sp.wait_ge(s_dest, 2 * j + b + 1)
                    load_slots(2 * j + b + 2, b)
            sp.wait_ge(s_ext, LAST - 1)
            sp.wait_ge(s_dest, LAST - 1)
            load_slots(LAST, 0)
            sp.wait_ge(s_eys, 16 * TILES_MAX)

        @block.gpsimd
        def _(pool):
            n_pool = [0]

            def link(ins):
                n_pool[0] += 1
                ins.then_inc(s_pool, 1)
                pool.wait_ge(s_pool, n_pool[0])

            nc.gpsimd.memset(mhalf[:, :], -0.5).then_inc(s_pool0, 1)
            nc.gpsimd.memset(xpad[:, :, 0:TAPS - 1], 0.0).then_inc(s_pool0, 1)
            pool.wait_ge(s_pool0, 2)
            nc.gpsimd.memset(pad[:, 0:D], 0.0)
            nc.gpsimd.memset(pad[:, D + 1:D + 2], -1.0)
            nc.gpsimd.memset(pad[:, D + 2:], 0.0)

            def by_head(a):
                return a.rearrange("p (h l) -> p h l", h=H_SSD)

            def along(a):
                return a.unsqueeze(2).broadcast_to([P, H_SSD, P])

            def rstds(ph, g):
                pool.wait_ge(s_var, norms_to(ph, g))
                c = slice(g * GT, (g + 1) * GT)
                nc.gpsimd.tensor_tensor(rstd[:, c], veps[:, c], mhalf[:, c], ALU.pow).then_inc(s_rstd, 1)
                if ph == PH_MIX:
                    pool.wait_ge(s_var2, g + 1)
                    nc.gpsimd.tensor_tensor(rstd2[:, c], veps2[:, c], mhalf[:, c],
                                            ALU.pow).then_inc(s_rstd2, 1)

            for g in range(GROUPS):
                rstds(PH_MIX, g)
            pool.wait_ge(s_const, 16)
            nc.gpsimd.tensor_copy(pad[:, D:D + 1], cst[:, C_TOKEN + TT:C_TOKEN + TT + 1]).then_inc(s_pad, 1)
            pool.wait_ge(s_fac, 16)
            for r in range(1, RANK):
                link(nc.gpsimd.tensor_tensor(fac_sb[:, 0], fac_sb[:, 0], fac_sb[:, r], ALU.add))
            nc.gpsimd.tensor_scalar(fac_sb[:, 0], fac_sb[:, 0], float(1.0 / np.sqrt(RANK)), None,
                                    ALU.mult).then_inc(s_fsum, 1)
            for c in range(TT):
                b = c % 2
                if c == 0:
                    pool.wait_ge(s_dtv, 4)
                if c >= 2:
                    pool.wait_ge(s_front_seg, c - 1)
                nc.gpsimd.tensor_tensor(by_head(ramp[:, b]), le_m.unsqueeze(1).broadcast_to([P, H_SSD, P]),
                                        along(dts[1][:, c, :]), ALU.mult).then_inc(s_ramp, 1)
                if c == 0:
                    pool.wait_ge(s_dd, 1)
                pool.wait_ge(s_tok, c + 1)
                if c >= 2:
                    pool.wait_ge(s_y, c - 1)
                    pool.wait_ge(s_st, c - 1)
                if c < TT - 1:
                    nc.gpsimd.tensor_tensor(by_head(ddx[:, b]), tok[:, b, 0:P].unsqueeze(1).broadcast_to([P, H_SSD, P]),
                                            along(dts[2][:, c, :]), ALU.mult).then_inc(s_ddx, 1)
                if c > 0:
                    pool.wait_ge(s_exp, c + 1)
                    nc.gpsimd.tensor_tensor(by_head(ce[:, b]), cv[:, 2:4, c * P:(c + 1) * P],
                                            by_head(decays[:, b, 2 * P:]), ALU.mult).then_inc(s_ce, 1)
            pool.wait_ge(s_yv, 1)
            nc.gpsimd.tensor_tensor(rstd2[:, :], veps2[:, :], mhalf[:, :], ALU.pow).then_inc(s_yr, 1)
            rstds(PH_FFN, 0)
            pool.wait_ge(s_f2hi, 1)
            nc.gpsimd.tensor_tensor(fw2_split[1], fw2, fw2_split[0].bitcast(F32), ALU.subtract).then_inc(s_f2lo, 1)
            rstds(PH_FFN, 1)
            for t in range(TT):
                pool.wait_ge(s_r2, t + 1)
                nc.gpsimd.tensor_tensor(x[:, t, :], x[:, t, :], xn[:, t, :], ALU.add).then_inc(s_xr, 1)
            pool.wait_ge(s_wq, 16)
            for r in range(1, QH):
                ins = nc.gpsimd.tensor_tensor(wq_sb[:, 0], wq_sb[:, 0], wq_sb[:, r], ALU.add)
                if r < QH - 1:
                    link(ins)
            ins.then_inc(s_wqsum, 1)
            pool.wait_ge(s_gate, 32)
            for g in range(GROUPS):
                rstds(PH_FAC, g)
                for t in range(g * GT, (g + 1) * GT):
                    pool.wait_ge(s_hh, GT * (norms_to(PH_FAC, g) - 1) + t % GT + 1)
                    nc.gpsimd.tensor_tensor(x[:, t, :], x[:, t, :], bias_sb[:, :], ALU.add).then_inc(s_xb, 1)
                rstds(PH_ATT, g)

            def split_queries(m):
                i, pair = divmod(m, HEADS // 2)
                if m >= HEADS // 2:
                    pool.wait_ge(s_sc, 2 * (m - HEADS // 2) + 2)
                for h in range(2):
                    half = slice(h * DH, (h + 1) * DH)
                    nc.gpsimd.tensor_copy(q_split[half, 2 * pair + h, :],
                                          qT[half, pair, i * P:(i + 1) * P]).then_inc(s_qhi, 1)
                pool.wait_ge(s_qhi, 2 * m + 2)
                for h in range(2):
                    half, other = slice(h * DH, (h + 1) * DH), slice((1 - h) * DH, (2 - h) * DH)
                    nc.gpsimd.tensor_tensor(q_split[other, 2 * pair + h, :], qT[half, pair, i * P:(i + 1) * P],
                                            q_split[half, 2 * pair + h, :].bitcast(F32), ALU.subtract).then_inc(s_qs, 1)
                    pool.wait_ge(s_qs, 2 * m + h + 1)

            pool.wait_ge(s_padded, (E + 1) * 16)
            pool.wait_ge(s_rstd, GROUPS * PH_MOE)
            pool.wait_ge(s_qa, scalar_fills(QB - 1))
            pool.wait_ge(s_qd, vector_fills(QB - 1))
            for m in range(HEADS // 2):
                split_queries(m)
            for i in range(TT + 2):
                if i + 1 < TT:
                    for pair in range(2):
                        split_queries((i + 1) * HEADS // 2 + pair)
                if i >= 2:
                    t = i - 2
                    pool.wait_ge(s_slots, t + 1)
                    for k in range(TOP):
                        nc.gpsimd.indirect_dma_start(
                            out=slots_in, out_offset=bass.IndirectOffsetOnAxis(ap=slot_i[:, t, k:k + 1], axis=0),
                            in_=slot_rows[:, t, :], in_offset=None).then_inc(s_scat, 16)
                if 1 <= i <= TT:
                    t = i - 1
                    pool.wait_ge(s_var, GROUPS * PH_MOE + t + 1)
                    nc.gpsimd.tensor_tensor(rstd[:, t:t + 1], veps[:, t:t + 1], mhalf[:, t:t + 1],
                                            ALU.pow).then_inc(s_rstd, 1)
                    pool.wait_ge(s_rstd, GROUPS * PH_MOE + t + 1)
                if i + 1 < TT:
                    if i >= 2:
                        pool.wait_ge(s_scat, (i - 1) * TOP * 16)
                    for pair in range(2, 4):
                        split_queries((i + 1) * HEADS // 2 + pair)

            def return_rows(i, b, first=False):
                pool.wait_ge(s_eyc, i + 1)
                if not first:
                    pool.wait_ge(s_eys, 16 * i)
                    pool.wait_ge(s_idle, i)
                nc.gpsimd.tensor_tensor(rstd2[:, 0:1], mhalf[:, 0:1], mhalf[:, 0:1], ALU.mult).then_inc(s_idle, 1)
                nc.gpsimd.indirect_dma_start(
                    out=out, out_offset=bass.IndirectOffsetOnAxis(ap=dest_now[:, b:b + 1], axis=0),
                    in_=ey[:, b], in_offset=None, compute_op=ALU.add).then_inc(s_eys, 16)

            pool.wait_ge(s_out, (TT + 1) * 16)
            return_rows(0, 0, first=True)
            return_rows(1, 1)
            with pool.Fori(1, LAST // 2) as j:
                for b in range(2):
                    return_rows(2 * j + b, b)
            return_rows(LAST, 0)

        @block.scalar
        def _(act):
            n_act = [0]

            def link(ins):
                n_act[0] += 1
                ins.then_inc(s_act, 1)
                act.wait_ge(s_act, n_act[0])

            def feature_major(ph, g, scale_col=None):
                act.wait_ge(s_tr, norms_to(ph, g))
                for k in range(KD):
                    dst = (hT_hi if ph in (PH_FFN, PH_ATT) else hT)[:, k, g * GW:(g + 1) * GW]
                    if scale_col is None:
                        last = nc.scalar.copy(dst, ps[:, k, :])
                    else:
                        last = nc.scalar.activation(dst, ps[:, k, :], ACT.Copy,
                                                    scale=small[:, scale_col + k:scale_col + k + 1])
                last.then_inc(s_hT, 1)

            act.dma_start(cst[:, 0:P], const_in[:, 0:P]).then_inc(s_ident, 16)
            act.dma_start(small[:, :], small_in).then_inc(s_small, 16)
            act.dma_start(cst[:, P:], const_in[:, P:]).then_inc(s_const, 16)
            act.wait_ge(s_pool0, 2)
            nc.scalar.activation(psums[:, 0:1], mhalf[:, 0:1], ACT.Copy)
            act.wait_ge(s_small, 16)
            feature_major(PH_MIX, 0, C_LN1)
            feature_major(PH_MIX, 1, C_LN1)
            def projected(q):
                g, fb = IN_FILLS[q]
                act.wait_ge(s_proj, q + 1)
                bank = ps[:, 2 + q % 4, :]
                if fb < 2:
                    last = nc.scalar.activation(zs[:, fb, g * GW:(g + 1) * GW], bank, ACT.Silu)
                else:
                    c = fb - 2
                    nc.scalar.copy(xpad[:, c, TAPS - 1 + g * GW:TAPS - 1 + (g + 1) * GW], bank)
                    last = nc.scalar.activation(
                        cv[:, c, g * GW:(g + 1) * GW], bank, ACT.Identity,
                        scale=small[:, C_CONVW + 4 * c + 3:C_CONVW + 4 * c + 4],
                        bias=small[:, C_CONVB + c:C_CONVB + c + 1])
                last.then_inc(s_evac, 1)

            def convolved(g):
                for c in range(CONV_BLOCKS):
                    act.wait_ge(s_conv, g * 12 + 8 + c + 1)
                    a = cv[:, c, g * GW:(g + 1) * GW]
                    nc.scalar.activation(a, a, ACT.Silu).then_inc(s_xbc, 1)

            for q in range(CONV_BLOCKS):
                projected(q)
            act.wait_ge(s_dtv, 1)
            nc.scalar.activation(dts[3], dts[3], ACT.Exp).then_inc(s_dta, 1)
            nc.scalar.activation(ea_log[:, :], small[:, C_ALOG:C_ALOG + H_SSD], ACT.Exp).then_inc(s_dta, 1)
            for q in range(CONV_BLOCKS, 2 * CONV_BLOCKS):
                projected(q)
            act.wait_ge(s_dtv, 2)
            nc.scalar.activation(dts[5], dts[4], ACT.Ln).then_inc(s_dta, 1)
            convolved(0)
            for q in range(2 * CONV_BLOCKS, len(IN_FILLS)):
                projected(q)
            act.wait_ge(s_decp, 1)
            nc.scalar.activation(dec_t[:, :], ps[:, 6, 0:2 * TT * H_SSD], ACT.Exp).then_inc(s_dec, 1)

            def squares(c):
                act.wait_ge(s_yg, c + 1)
                if c >= 2:
                    act.wait_ge(s_ss, c - 1)
                nc.scalar.activation(sq[:, c % 2].rearrange("p (h l) -> p h l", h=H_SSD),
                                     yg[:, :, c * P:(c + 1) * P], ACT.Square).then_inc(s_sq, 1)

            def chunk(c):
                b = c % 2
                act.wait_ge(s_front_tr, c + 1)
                if c >= 2:
                    act.wait_ge(s_st, c - 1)
                nc.scalar.copy(tok[:, b], ps[:, 0, 0:2 * P]).then_inc(s_tok, 1)
                act.wait_ge(s_front_seg, c + 1)
                nc.scalar.activation(decays[:, b], ps[:, 2, :], ACT.Exp).then_inc(s_exp, 1)

            chunk(0)
            convolved(1)
            for c in range(1, TT):
                chunk(c)
                squares(c - 1)
            squares(TT - 1)
            act.wait_ge(s_ffnw, 32)
            act.wait_ge(s_ss, TT)
            w13 = fw13.rearrange("p w k n -> p (w k) n")
            for f in range(FB):
                c = slice(f * P, (f + 1) * P)
                nc.scalar.copy(fw13_split[0][:, :, c], w13[:, :, c]).then_inc(s_fwhi, 1)
            act.wait_ge(s_mo, TT)
            nc.scalar.copy(fw2_split[0], fw2).then_inc(s_f2hi, 1)
            feature_major(PH_FFN, 0, C_LN2)
            def act_hi(q):
                act.wait_ge(s_fa, q + 1)
                nc.scalar.copy(ffn_a[0][:, q % FB, :], ffn_act[q % 2]).then_inc(s_ahi, 1)

            for q in range(GROUPS * FB):
                if FB + 2 <= q < FB + 5:
                    if q == FB + 2:
                        act.wait_ge(s_wqsum, 1)
                        act.wait_ge(s_kv, 32)
                        act.wait_ge(s_fsum, 1)
                    nc.scalar.copy(qkv_w[0][:, q - FB - 2, :], qkv_src[q - FB - 2]).then_inc(s_pwhi, 1)
                if q == FB:
                    feature_major(PH_FFN, 1, C_LN2)
                act.wait_ge(s_gu, q + 1)
                if q >= 2:
                    act.wait_ge(s_fa, q - 1)
                nc.scalar.activation(sgate[q % 2], ps[:, 2 + q % 2, :], ACT.Silu).then_inc(s_sg, 1)
                if q % FB:
                    act_hi(q - 1)
                if q % FB == FB - 1:
                    act_hi(q)
            feature_major(PH_FAC, 0)
            feature_major(PH_ATT, 0)
            for q in range(FILLS):
                if q == 1:
                    feature_major(PH_FAC, 1)
                if q == 10:
                    feature_major(PH_ATT, 1)
                if is_k(q):
                    act.wait_ge(s_qkv, q + 1)
                    for half, hi, hi_other, lo in k_parts(q):
                        nc.scalar.copy(hi, ps[half, 2 + q % 6, :])
                        last = nc.scalar.copy(hi_other, ps[half, 2 + q % 6, :])
                    last.then_inc(s_qa, 1)
                elif q % 2 == 0:
                    act.wait_ge(s_qkv, q + 1)
                    dst, scale = qv_dst(q)
                    nc.scalar.activation(dst, ps[:, 2 + q % 6, :], ACT.Copy, scale=scale).then_inc(s_qa, 1)

            def attend(u):
                i, n = divmod(u, HEADS)
                w = (i + 1) * P
                act.wait_ge(s_max, u + 1)
                if u >= 4:
                    act.wait_ge(s_pt, u - 3)
                src = ps[:, 2 * (u % 2):2 * (u % 2) + 2, :].rearrange("p a b -> p (a b)")[:, 0:w]
                nc.scalar.activation(probs[u % 4][:, 0:w], src, ACT.Exp, bias=nmax[:, u:u + 1],
                                     accum_out=psums[:, u:u + 1]).then_inc(s_pr, 1)

            def probs_feature_major(u):
                w = (u // HEADS + 1) * P
                act.wait_ge(s_pt, u + 1)
                if u >= 4:
                    act.wait_ge(s_pv, u // 2 - 1)
                nc.scalar.copy(pT[u % 4][:, 0:w],
                               ps[:, 4:6, :].rearrange("p a b -> p (a b)")[:, 0:w]).then_inc(s_pT, 1)

            def z_feature_major(i):
                act.wait_ge(s_pv, (i + 1) * HEADS // 2)
                if i >= 1:
                    act.wait_ge(s_ao, i)
                nc.scalar.copy(zT.rearrange("p a b -> p (a b)"), ps[:, 6 + i % 2, :]).then_inc(s_zT, 1)

            def routed_feature_major(i):
                act.wait_ge(s_rT, i + 1)
                if i >= 2:
                    act.wait_ge(s_lg, i - 1)
                nc.scalar.copy(routed_T[:, i % 2], ps[:, 6 + i % 2, 0:D]).then_inc(s_rTc, 1)

            def logits_exp(i):
                act.wait_ge(s_lmax, i + 1)
                nc.scalar.activation(prob_e[:, i, :], ps[:, 6 + i % 2, D:D + E], ACT.Exp, bias=rs[0][:, i:i + 1],
                                     accum_out=rs[1][:, i:i + 1]).then_inc(s_lexp, 1)

            for u in range((TT + 1) * HEADS + 5):
                if u >= 2 * HEADS and u % HEADS == 0:
                    routed_feature_major(u // HEADS - 2)
                if u >= 2 * HEADS and u % HEADS == 2:
                    logits_exp(u // HEADS - 2)
                if HEADS <= u < (TT + 1) * HEADS and u % HEADS == 4:
                    z_feature_major(u // HEADS - 1)
                if 3 <= u < TT * HEADS + 3:
                    probs_feature_major(u - 3)
                if u < TT * HEADS:
                    attend(u)

            def expert_silu(i):
                act.wait_ge(s_eg, i + 1)
                act.wait_ge(s_ea, i)
                nc.scalar.activation(eg, ps[:, 0:2, 0:IH], ACT.Silu).then_inc(s_esg, 1)

            def expert_aT(i, b):
                act.wait_ge(s_eat, i + 1)
                nc.scalar.copy(eaT[:, b, 0:4, :].rearrange("p a b -> p (a b)"), ps[:, 4, :]).then_inc(s_eaa, 1)

            def expert_y(i, b, first=False):
                act.wait_ge(s_ey, i + 1)
                act.wait_ge(s_now, i + 1)
                if not first:
                    act.wait_ge(s_eys, 16 * (i - 1))
                nc.scalar.activation(ey[:, b], ps[:, 6, 0:D], ACT.Copy, scale=w_now[:, b:b + 1]).then_inc(s_eyc, 1)

            def weights_hi(e, w):
                nc.scalar.copy(split_w[w][0].rearrange("p k n -> p (k n)").unsqueeze(1),
                               (ew1, ew3)[w][:, bass.ds(e, 1), :]).then_inc(s_whi[w], 1)

            def expert_of(i):
                return nc.scalar.value_load(eid[0:1, bass.ds(i, 1)], min_val=0, max_val=E - 1)

            def slot_tile_hi(i, b):
                act.wait_ge(s_ext, i + 1)
                nc.scalar.copy(xsT[0][b], ps[:, 7, 0:D].rearrange("p (k t) -> p k t", k=KD)).then_inc(s_xhi, 1)

            def next_weights(i, first=False):
                if first:
                    act.wait_ge(s_eg, 1)
                    nc.scalar.activation(eg, ps[:, 0:2, 0:IH], ACT.Silu).then_inc(s_esg, 1)
                else:
                    expert_silu(i)
                e = expert_of(i + 1)
                weights_hi(e, 0)
                act.wait_ge(s_eu, i + 1)
                nc.scalar.copy(idle_act[:, 0:1], mhalf[:, 0:1])
                weights_hi(e, 1)

            act.wait_ge(s_eid, 1)
            act.wait_ge(s_e13, 2 * E * 16)
            act.wait_ge(s_out, (TT + 1) * 16)
            act.wait_ge(s_lg, TT)
            nc.scalar.copy(idle_act[:, 1:2], mhalf[:, 0:1])
            e = expert_of(0)
            for w in range(2):
                weights_hi(e, w)
            for b in range(2):
                slot_tile_hi(b, b)
            next_weights(0, first=True)

            def body(i, b, first=False):
                slot_tile_hi(i + 2, b)
                expert_aT(i, b)
                next_weights(i + 1)
                expert_y(i, b, first)

            body(0, 0, first=True)
            body(1, 1, first=True)
            with act.Fori(1, LAST // 2 - 1) as j:
                for b in range(2):
                    body(2 * j + b, b)
            body(LAST - 2, 0)
            expert_aT(LAST - 1, 1)
            expert_silu(LAST)
            expert_y(LAST - 1, 1)
            expert_aT(LAST, 0)
            expert_y(LAST, 0)

        @block.vector
        def _(dve):
            n_dve = [0]

            def link(ins):
                n_dve[0] += 1
                ins.then_inc(s_dve, 1)
                dve.wait_ge(s_dve, n_dve[0])

            V = nc.vector

            def variances(ph, src, g, given=0):
                for t in range(g * GT + given, (g + 1) * GT):
                    if ph == PH_FFN:
                        dve.wait_ge(s_r2, t + 1)
                    elif ph == PH_FAC:
                        dve.wait_ge(s_x1, t + 1)
                    elif ph == PH_ATT:
                        dve.wait_ge(s_x2, t + 1)
                    ins = V.bn_stats(stats[:, t, :], src[:, t, :])
                link(ins)
                for t in range(g * GT, (g + 1) * GT):
                    ins = V.bn_aggr(mv[:, t, :], stats[:, t, :])
                link(ins)
                c = slice(g * GT, (g + 1) * GT)
                if ph == PH_FFN:
                    link(V.tensor_tensor(veps2[:, c], mv[:, c, 0], mv[:, c, 0], ALU.mult))
                    V.scalar_tensor_tensor(veps[:, c], mv[:, c, 1], EPS, veps2[:, c], ALU.add,
                                           ALU.add).then_inc(s_var, 1)
                else:
                    V.tensor_scalar(veps[:, c], mv[:, c, 1], EPS, None, ALU.add).then_inc(s_var, 1)

            def normalise(ph, src, g):
                dve.wait_ge(s_rstd, norms_to(ph, g))
                for t in range(g * GT, (g + 1) * GT):
                    if ph > 0:
                        dve.wait_ge(s_tr, norms_to(ph - 1, g))
                    if ph == PH_FFN:
                        V.tensor_scalar(hh[:, t, :], src[:, t, :], rstd[:, t:t + 1], None,
                                        ALU.mult).then_inc(s_hh, 1)
                    else:
                        V.tensor_scalar(hh[:, t, :], src[:, t, :], mv[:, t, 0:1], rstd[:, t:t + 1],
                                        ALU.subtract, ALU.mult).then_inc(s_hh, 1)

            for g in range(GROUPS):
                dve.wait_ge(s_x[g], 16)
                variances(PH_MIX, x, g)
            for g in range(GROUPS):
                c = slice(g * GT, (g + 1) * GT)
                dve.wait_ge(s_rstd, g + 1)
                link(V.tensor_tensor(veps2[:, c], rstd[:, c], rstd[:, c], ALU.mult))
                link(V.tensor_tensor(veps2[:, c], veps2[:, c], mv[:, c, 1], ALU.mult))
                V.tensor_scalar(veps2[:, c], veps2[:, c], EPS, None, ALU.add).then_inc(s_var2, 1)
                dve.wait_ge(s_rstd2, g + 1)
                link(V.tensor_tensor(rstd2[:, c], rstd2[:, c], rstd[:, c], ALU.mult))
                for t in range(g * GT, (g + 1) * GT):
                    V.tensor_scalar(hh[:, t, :], x[:, t, :], mv[:, t, 0:1], rstd2[:, t:t + 1],
                                    ALU.subtract, ALU.mult).then_inc(s_hh, 1)
            for t in range(TT):
                V.tensor_scalar(xn[:, t, :], x[:, t, :], mv[:, t, 0:1], rstd[:, t:t + 1],
                                ALU.subtract, ALU.mult)

            dve.wait_ge(s_const, 16)
            V.tensor_copy(ident_b[:, :], ident)
            for h in range(H_SSD):
                V.tensor_copy(neg_s[:, h * P:(h + 1) * P], cst[:, C_NEGS:C_NEGS + P])
            V.tensor_copy(neg_a[:, :], cst[:, C_NEGA:C_NEGA + P]).then_inc(s_cbf, 1)

            dve.wait_ge(s_small, 16)
            dve.wait_ge(s_mixw, 16)
            for k in range(KD):
                V.tensor_scalar(wout_sb[:, k, :], wout_sb[:, k, :], small[:, C_NORM + k:C_NORM + k + 1], None,
                                ALU.mult).then_inc(s_wn, 1)

            def row(c):
                return small[:, c:c + H_SSD].unsqueeze(1).broadcast_to([P, TT, H_SSD])

            dve.wait_ge(s_dtp, 1)
            link(V.tensor_tensor(dts[6], ps[:, 6, 64:64 + TT * H_SSD].rearrange("p (t h) -> p t h", h=H_SSD),
                                 row(C_DTB), ALU.add))
            V.scalar_tensor_tensor(dts_t[:, 48:64], dts_t[:, 96:112], -1.0, dts_t[:, 96:112], ALU.mult,
                                   ALU.min).then_inc(s_dtv, 1)

            def convolve(g):
                dve.wait_ge(s_evac, (g + 1) * CONV_BLOCKS)
                for k in range(TAPS - 1):
                    for c in range(CONV_BLOCKS):
                        if k:
                            dve.wait_ge(s_conv, (g * (TAPS - 1) + k - 1) * CONV_BLOCKS + c + 1)
                        a = cv[:, c, g * GW:(g + 1) * GW]
                        V.scalar_tensor_tensor(a, xpad[:, c, k + g * GW:k + (g + 1) * GW],
                                               small[:, C_CONVW + 4 * c + k:C_CONVW + 4 * c + k + 1], a,
                                               ALU.mult, ALU.add).then_inc(s_conv, 1)

            convolve(0)
            dve.wait_ge(s_dta, 1)
            V.tensor_scalar(dts[4], dts[3], 1.0, None, ALU.add).then_inc(s_dtv, 1)
            dve.wait_ge(s_dtv, 2)
            link(V.tensor_scalar(dts[7], dts[4], -1.0, None, ALU.add))
            link(V.tensor_scalar(dts[8], dts[7], 0.0, None, ALU.is_equal))
            link(V.tensor_tensor(dts[7], dts[7], dts[8], ALU.add))
            link(V.reciprocal(dts[9], dts[7]))
            dve.wait_ge(s_dta, 3)
            link(V.tensor_tensor(dts[9], dts[9], dts[5], ALU.mult))
            link(V.tensor_tensor(dts[9], dts[9], dts[8], ALU.add))
            link(V.tensor_tensor(dts[9], dts[9], dts[3], ALU.mult))
            V.scalar_tensor_tensor(dts_t[:, 0:16], dts_t[:, 96:112], 0.0, dts_t[:, 144:160], ALU.max,
                                   ALU.add).then_inc(s_dtv, 1)
            dve.wait_ge(s_dtv, 3)
            link(V.tensor_scalar(ea_log[:, :], ea_log[:, :], -1.0, None, ALU.mult))
            V.tensor_tensor(dts[1], dts[0], ea_log[:, :].unsqueeze(1).broadcast_to([P, TT, H_SSD]),
                            ALU.mult).then_inc(s_dtv, 1)
            convolve(1)
            dve.wait_ge(s_dec, 1)
            V.tensor_tensor(dts[2], dec[:, 0], dts[0], ALU.mult).then_inc(s_dd, 1)

            def masked(c):
                b = c % 2
                dve.wait_ge(s_front_g, c + 1)
                dve.wait_ge(s_exp, c + 1)
                if c >= 2:
                    dve.wait_ge(s_y, c - 1)
                for h in range(H_SSD):
                    last = V.scalar_tensor_tensor(
                        mt[:, b, h * P:(h + 1) * P], ps[:, 1, h * P:(h + 1) * P], dts[0][:, c, h:h + 1],
                        decays[:, b, h * P:(h + 1) * P], ALU.mult, ALU.mult)
                last.then_inc(s_mt, 1)

            masked(0)
            for c in range(TT):
                b = c % 2
                if c < TT - 1:
                    masked(c + 1)
                    dve.wait_ge(s_st, c + 1)
                    for h in range(H_SSD):
                        if c == 0:
                            last = V.tensor_copy(state[:, 1, h], ps[:, 5, h * P:(h + 1) * P])
                        else:
                            dve.wait_ge(s_state, c)
                            last = V.scalar_tensor_tensor(state[:, 1 - b, h], state[:, b, h], dec[:, 1, c, h:h + 1],
                                                          ps[:, 5, h * P:(h + 1) * P], ALU.mult, ALU.add)
                    last.then_inc(s_state, 1)
                dve.wait_ge(s_y, c + 1)
                for h in range(H_SSD):
                    ins = V.scalar_tensor_tensor(
                        yg[:, h, c * P:(c + 1) * P], cv[:, 0, c * P:(c + 1) * P], small[:, C_D + h:C_D + h + 1],
                        ps[:, 3 + b, h * P:(h + 1) * P], ALU.mult, ALU.add)
                link(ins)
                V.tensor_tensor(yg[:, :, c * P:(c + 1) * P], yg[:, :, c * P:(c + 1) * P],
                                zs[:, :, c * P:(c + 1) * P], ALU.mult).then_inc(s_yg, 1)
            dve.wait_ge(s_ss, TT)
            V.tensor_scalar(veps2[:, :], ps[:, 7, 0:TT], 1.0 / D, EPS, ALU.mult, ALU.add).then_inc(s_yv, 1)
            dve.wait_ge(s_yr, 1)
            def mixer_residual(t):
                dve.wait_ge(s_mo, t - t % 2 + 2)
                V.scalar_tensor_tensor(xn[:, t, :], mixer_bank(t), rstd2[:, t:t + 1], xn[:, t, :],
                                       ALU.mult, ALU.add).then_inc(s_r2, 1)

            def feature_major_lo(ph, g):
                dve.wait_ge(s_hT, norms_to(ph, g))
                c = slice(g * GW, (g + 1) * GW)
                for k in range(KD):
                    hi = hT_hi[:, k, c].bitcast(F32)
                    if ph == PH_FFN:
                        last = V.scalar_tensor_tensor(hT_lo[:, k, c], ps[:, k, :], small[:, C_LN2 + k:C_LN2 + k + 1],
                                                      hi, ALU.mult, ALU.subtract)
                    else:
                        last = V.tensor_tensor(hT_lo[:, k, c], ps[:, k, :], hi, ALU.subtract)
                last.then_inc(s_hTlo, 1)

            def ffn_w_lo(f):
                dve.wait_ge(s_fwhi, f + 1)
                c = slice(f * P, (f + 1) * P)
                V.tensor_tensor(fw13_split[1][:, :, c], fw13.rearrange("p w k n -> p (w k) n")[:, :, c],
                                fw13_split[0][:, :, c].bitcast(F32), ALU.subtract).then_inc(s_fwlo, 1)

            def qkv_w_lo(j):
                dve.wait_ge(s_pwhi, j + 1)
                V.tensor_tensor(qkv_w[1][:, j, :], qkv_src[j], qkv_w[0][:, j, :].bitcast(F32),
                                ALU.subtract).then_inc(s_pwlo, 1)

            def act_lo(q):
                dve.wait_ge(s_ahi, q + 1)
                V.tensor_tensor(ffn_a[1][:, q % FB, :], ffn_act[q % 2], ffn_a[0][:, q % FB, :].bitcast(F32),
                                ALU.subtract).then_inc(s_alo, 1)

            def swiglu(g):
                for f in range(FB):
                    if g == 1 and 3 <= f < 6:
                        qkv_w_lo(f - 3)
                    q = g * FB + f
                    dve.wait_ge(s_sg, q + 1)
                    if q >= 2:
                        dve.wait_ge(s_alo, q - 1)
                    V.tensor_tensor(ffn_act[q % 2], sgate[q % 2], ps[:, 4 + q % 2, :],
                                    ALU.mult).then_inc(s_fa, 1)
                    if f:
                        act_lo(q - 1)
                    if f == FB - 1:
                        act_lo(q)
                    if g == 0 and f + 2 < FB:
                        ffn_w_lo(f + 2)

            def ffn_residual(tiles):
                for t in tiles:
                    dve.wait_ge(s_fo, t + 1)
                    dve.wait_ge(s_xr, t + 1)
                    V.tensor_tensor(x[:, t, :], x[:, t, :], ps[:, 6 + t % 2, 0:D], ALU.add).then_inc(s_x1, 1)

            def mixing_residual(tiles):
                for t in tiles:
                    dve.wait_ge(s_mx, t - t % 2 + 2)
                    dve.wait_ge(s_xb, t + 1)
                    V.tensor_tensor(x[:, t, :], x[:, t, :], mixing_bank(t), ALU.add).then_inc(s_x2, 1)

            for t in range(GT):
                mixer_residual(t)
                if t:
                    dve.wait_ge(s_r2, t)
                    V.bn_stats(stats[:, t - 1, :], xn[:, t - 1, :])
            variances(PH_FFN, xn, 0, given=GT - 1)
            for t in range(GT, TT):
                mixer_residual(t)
            normalise(PH_FFN, xn, 0)
            for f in range(2):
                ffn_w_lo(f)
            feature_major_lo(PH_FFN, 0)
            variances(PH_FFN, xn, 1)
            normalise(PH_FFN, xn, 1)
            swiglu(0)
            feature_major_lo(PH_FFN, 1)
            ffn_residual(range(GT))
            variances(PH_FAC, x, 0)
            normalise(PH_FAC, x, 0)
            swiglu(1)
            ffn_residual(range(GT, TT - 2))
            mixing_residual(range(GT))
            variances(PH_ATT, x, 0)
            ffn_residual(range(TT - 2, TT - 1))
            normalise(PH_ATT, x, 0)
            ffn_residual(range(TT - 1, TT))
            variances(PH_FAC, x, 1)
            feature_major_lo(PH_ATT, 0)
            normalise(PH_FAC, x, 1)
            for q in range(FILLS):
                if q == 4:
                    mixing_residual(range(GT, TT))
                    variances(PH_ATT, x, 1)
                if q == 6:
                    normalise(PH_ATT, x, 1)
                if q == 9:
                    feature_major_lo(PH_ATT, 1)
                if is_k(q):
                    dve.wait_ge(s_qa, scalar_fills(q))
                    for half, hi, hi_other, lo in k_parts(q):
                        last = V.tensor_tensor(lo, ps[half, 2 + q % 6, :], hi.bitcast(F32), ALU.subtract)
                    last.then_inc(s_qd, 1)
                elif q % 2:
                    dve.wait_ge(s_qkv, q + 1)
                    dst, scale = qv_dst(q)
                    V.tensor_scalar(dst, ps[:, 2 + q % 6, :], scale, None, ALU.mult).then_inc(s_qd, 1)

            def row_max(u):
                w = (u // HEADS + 1) * P
                dve.wait_ge(s_sc, u + 1)
                src = ps[:, 2 * (u % 2):2 * (u % 2) + 2, :].rearrange("p a b -> p (a b)")[:, 0:w]
                V.tensor_reduce(nmax[:, u:u + 1], src, AX_X, ALU.max, negate=True).then_inc(s_max, 1)

            def normalised(u):
                w = (u // HEADS + 1) * P
                dve.wait_ge(s_pr, u + 1)
                V.reciprocal(pinv[:, u:u + 1], psums[:, u:u + 1]).then_inc(s_pinv, 1)
                dve.wait_ge(s_pinv, u + 1)
                V.tensor_scalar(probs[u % 4][:, 0:w], probs[u % 4][:, 0:w], pinv[:, u:u + 1], None,
                                ALU.mult).then_inc(s_pn, 1)

            def add_attention(i):
                dve.wait_ge(s_ao, i + 1)
                V.tensor_tensor(x[:, i, :], x[:, i, :], ps[:, 6 + i % 2, 0:D], ALU.add).then_inc(s_x3, 1)

            iota_e = iota[:, 0:E].unsqueeze(1).broadcast_to([P, TOP, E])

            def route_variance(t):
                dve.wait_ge(s_x3, t + 1)
                link(V.bn_stats(stats[:, t, :], x[:, t, :]))
                link(V.bn_aggr(mv[:, t, :], stats[:, t, :]))
                V.tensor_scalar(veps[:, t:t + 1], mv[:, t, 1:2], EPS, None, ALU.add).then_inc(s_var, 1)

            def route_normalise(t):
                dve.wait_ge(s_rstd, GROUPS * PH_MOE + t + 1)
                V.tensor_scalar(hh[:, t, :], x[:, t, :], mv[:, t, 0:1], rstd[:, t:t + 1],
                                ALU.subtract, ALU.mult).then_inc(s_hh, 1)

            def route_max(t):
                dve.wait_ge(s_lg, t + 1)
                V.tensor_reduce(rs[0][:, t:t + 1], ps[:, 6 + t % 2, D:D + E], AX_X, ALU.max,
                                negate=True).then_inc(s_lmax, 1)

            def route_choice(t):
                dve.wait_ge(s_lexp, t + 1)
                link(V.reciprocal(rs[2][:, t:t + 1], rs[1][:, t:t + 1]))
                link(V.tensor_scalar(prob_e[:, t, :], prob_e[:, t, :], rs[2][:, t:t + 1], None, ALU.mult))
                link(V.max(top_v[:, t, :], prob_e[:, t, :]))
                link(V.max_index(top_i[:, t, :], top_v[:, t, :], prob_e[:, t, :]))
                link(V.tensor_copy(top_f[:, t, :], top_i[:, t, 0:TOP]))
                link(V.tensor_tensor(onehot[:, t], iota_e, top_f[:, t, :].unsqueeze(2).broadcast_to([P, TOP, E]),
                                     ALU.is_equal))
                V.tensor_tensor(chosen[:, t, :], onehot[:, t, 0, :], onehot[:, t, 1, :],
                                ALU.add).then_inc(s_chosen, 1)

            def route_tail(t):
                V.tensor_copy(slot_rows[:, t, D:D + 1], cst[:, C_TOKEN + t:C_TOKEN + t + 1])
                V.tensor_copy(slot_rows[:, t, D + 1:D + 2], top_f[:, t, 0:1])
                link(V.tensor_tensor(rs[3][:, t:t + 1], top_v[:, t, 0:1], top_v[:, t, 1:2], ALU.add))
                link(V.reciprocal(rs[4][:, t:t + 1], rs[3][:, t:t + 1]))
                V.tensor_scalar(slot_rows[:, t, D + 2:], top_v[:, t, 0:TOP], rs[4][:, t:t + 1], None, ALU.mult)

            def route_slots(t):
                dve.wait_ge(s_cnt, t + 1)
                before = ps[:, 6 + t % 2, D + E:D + 2 * E]
                totals = ps[:, 6 + t % 2, D + 2 * E:D + 3 * E]
                V.tensor_tensor(rank_e[:, t, :], base_e[:, t, :], before, ALU.add)
                link(V.tensor_tensor(base_e[:, t + 1, :], base_e[:, t, :], totals, ALU.add))
                link(V.tensor_tensor(slot_e[:, t], onehot[:, t],
                                     rank_e[:, t, :].unsqueeze(1).broadcast_to([P, TOP, E]), ALU.mult))
                link(V.tensor_reduce(slot_f[:, t, :], slot_e[:, t], AX_X, ALU.add))
                V.tensor_copy(slot_i[:, t, :], slot_f[:, t, :]).then_inc(s_slots, 1)

            link(V.tensor_scalar(base_e[:, 0, :], iota[:, 0:E], float(T), None, ALU.mult))
            for u in range((TT + 1) * HEADS + 5):
                if u < TT * HEADS:
                    row_max(u)
                if 1 <= u < TT * HEADS + 1:
                    normalised(u - 1)
                if HEADS <= u < (TT + 1) * HEADS and u % HEADS == 5:
                    add_attention(u // HEADS - 1)
                    route_variance(u // HEADS - 1)
                if HEADS <= u < (TT + 1) * HEADS and u % HEADS == 6:
                    route_normalise(u // HEADS - 1)
                if u >= 2 * HEADS and u % HEADS == 1:
                    route_max(u // HEADS - 2)
                if u >= 2 * HEADS and u % HEADS == 2:
                    route_choice(u // HEADS - 2)
                if u >= 2 * HEADS and u % HEADS == 3:
                    route_tail(u // HEADS - 2)
                if u >= 2 * HEADS and u % HEADS == 4:
                    route_slots(u // HEADS - 2)
            link(V.tensor_scalar(rs[8], iota[:, 0:E], float(P), None, ALU.mult))
            link(V.scalar_tensor_tensor(rs[9], iota[:, 0:E], -float(T), base_e[:, TT, :], ALU.mult, ALU.add))
            link(V.tensor_tensor(prob_e, rs[9].unsqueeze(2).broadcast_to([P, E, TT]),
                                 rs[8].unsqueeze(1).broadcast_to([P, E, TT]), ALU.is_gt))
            link(V.tensor_reduce(rs[9], prob_e, AX_X, ALU.add))
            link(V.tensor_tensor_scan(rs[8], cst[:, C_ONES:C_ONES + E], rs[9], 0.0, ALU.mult, ALU.add))
            link(V.tensor_tensor(ecmp, iota.unsqueeze(2).broadcast_to([P, 24, E]),
                                 rs[8].unsqueeze(1).broadcast_to([P, 24, E]), ALU.is_ge))
            link(V.tensor_reduce(eid_f, ecmp, AX_X, ALU.add))
            link(V.tensor_tensor(ecmp, ecmp, rs[9].unsqueeze(1).broadcast_to([P, 24, E]), ALU.mult))
            first_tile = bias_sb[:, 192:216]
            link(V.tensor_reduce(first_tile, ecmp, AX_X, ALU.add))
            V.tensor_scalar(eid[:, :], eid_f, float(E - 1), None, ALU.min).then_inc(s_eid, 1)
            link(V.scalar_tensor_tensor(first_tile, eid_f, float(TT), first_tile, ALU.mult, ALU.subtract))
            link(V.tensor_tensor(first_tile, first_tile, iota, ALU.add))
            V.tensor_scalar(region[:, :], first_tile, float(SLOT_TILES - 1), None, ALU.min).then_inc(s_table, 1)
            def expert_act(i, b):
                dve.wait_ge(s_esg, i + 1)
                dve.wait_ge(s_eu, i + 1)
                V.tensor_tensor(ea[:, b].rearrange("p (a c) -> p a c", a=2), eg, ps[:, 2:4, 0:IH],
                                ALU.mult).then_inc(s_ea, 1)

            def expert_xT(i, b):
                dve.wait_ge(s_xhi, i + 1)
                V.tensor_tensor(xsT[1][b], ps[:, 7, 0:D].rearrange("p (k t) -> p k t", k=KD), xsT[0][b].bitcast(F32),
                                ALU.subtract).then_inc(s_exT, 1)
                now = bass.ds(i, 1)
                V.tensor_copy(dest[:, now], xs[:, b, D:D + 1])
                V.tensor_scalar(w_first[:, now], xs[:, b, D + 1:D + 2], eid_f[:, now], xs[:, b, D + 2:D + 3],
                                ALU.is_equal, ALU.mult)
                V.tensor_scalar(w_second[:, now], xs[:, b, D + 1:D + 2], eid_f[:, now], xs[:, b, D + 3:D + 4],
                                ALU.not_equal, ALU.mult).then_inc(s_dest, 1)

            def weights_lo(i, w, e):
                dve.wait_ge(s_whi[w], i + 1)
                hi, lo = (a.rearrange("p k n -> p (k n)").unsqueeze(1) for a in split_w[w])
                V.tensor_tensor(lo, (ew1, ew3)[w][:, bass.ds(e, 1), :], hi.bitcast(F32),
                                ALU.subtract).then_inc(s_wlo[w], 1)

            def expert_of(i):
                return nc.vector.value_load(eid[0:1, bass.ds(i, 1)], min_val=0, max_val=E - 1)

            def slot_tails(i, b, first=False):
                dve.wait_ge(s_dest, i + 1)
                if not first:
                    dve.wait_ge(s_eys, 16 * (i - 1))
                now = bass.ds(i, 1)
                V.tensor_copy(dest_now[:, b:b + 1], dest[:, now])
                V.tensor_tensor(w_now[:, b:b + 1], w_first[:, now], w_second[:, now], ALU.add).then_inc(s_now, 1)

            def expert_aT(i, b):
                dve.wait_ge(s_eat, i + 1)
                V.tensor_copy(eaT[:, b, 4, :], ps[:, 5, 0:P])
                V.tensor_copy(eaT[0:ILAST, b, 5, :], ps[0:ILAST, 5, P:2 * P]).then_inc(s_ead, 1)

            dve.wait_ge(s_eid, 1)
            e = expert_of(0)
            weights_lo(0, 0, e)
            expert_xT(0, 0)
            weights_lo(0, 1, e)
            expert_xT(1, 1)
            expert_act(0, 0)
            e = expert_of(1)
            for w in range(2):
                weights_lo(1, w, e)

            def body(i, b, first=False):
                e = expert_of(i + 2)
                expert_xT(i + 2, b)
                expert_aT(i, b)
                slot_tails(i, b, first)
                expert_act(i + 1, 1 - b)
                for w in range(2):
                    weights_lo(i + 2, w, e)

            body(0, 0, first=True)
            body(1, 1, first=True)
            with dve.Fori(1, LAST // 2 - 1) as j:
                for b in range(2):
                    body(2 * j + b, b)
            body(LAST - 2, 0)
            expert_aT(LAST - 1, 1)
            expert_act(LAST, 0)
            slot_tails(LAST - 1, 1)
            expert_aT(LAST, 0)
            slot_tails(LAST, 0)

        @block.tensor
        def _(pe):
            mm = nc.tensor.matmul

            def transposes(ph, g):
                before = norms_to(ph, g) - 1
                if before:
                    pe.wait_ge(s_hT, before)
                lo_before = sum(p in (PH_FFN, PH_ATT) for p, _ in NORMS[:before])
                if lo_before:
                    pe.wait_ge(s_hTlo, lo_before)
                for t in range(g * GT, (g + 1) * GT):
                    pe.wait_ge(s_hh, GT * before + t % GT + 1)
                    for k in range(KD):
                        last = nc.tensor.transpose(ps[:, k, (t % GT) * P:(t % GT + 1) * P],
                                                   hh[:, t, k * P:(k + 1) * P], ident)
                last.then_inc(s_tr, 1)

            pe.wait_ge(s_ident, 16)
            transposes(PH_MIX, 0)
            transposes(PH_MIX, 1)
            pe.wait_ge(s_const, 16)
            pe.wait_ge(s_win, 16)
            for q, (g, fb) in enumerate(IN_FILLS):
                if q < 2 * CONV_BLOCKS and q % CONV_BLOCKS == 0:
                    pe.wait_ge(s_hT, g + 1)
                if q == CONV_BLOCKS:
                    for t in range(TT):
                        for k in range(KD):
                            last = mm(ps[:, 6, 64 + H_SSD * t:64 + H_SSD * (t + 1)], hT[:, k, t * P:(t + 1) * P],
                                      win_sb[:, k, 6 * P:], start=(k == 0), stop=(k == KD - 1))
                    last.then_inc(s_dtp, 1)
                if q >= 4:
                    pe.wait_ge(s_evac, q - 3)
                for k in range(KD):
                    last = mm(ps[:, 2 + q % 4, :], win_sb[:, k, fb * P:(fb + 1) * P],
                              hT[:, k, g * GW:(g + 1) * GW], start=(k == 0), stop=(k == KD - 1))
                last.then_inc(s_proj, 1)
            pe.wait_ge(s_dtv, 4)
            da = dts_t[:, 16:32]
            mm(ps[:, 6, 0:16], gt_m, da, start=True, stop=True)
            mm(ps[:, 6, 16:32], ones, da, start=True, stop=True).then_inc(s_decp, 1)

            def front(c):
                cols = slice(c * P, (c + 1) * P)
                if c == 0:
                    pe.wait_ge(s_cbf, 1)
                    pe.wait_ge(s_evac, len(IN_FILLS))
                if c in (0, GT):
                    pe.wait_ge(s_xbc, (c // GT + 1) * CONV_BLOCKS)
                if c >= 1:
                    pe.wait_ge(s_tok, c)
                for k in range(2):
                    last = nc.tensor.transpose(ps[:, 0, k * P:(k + 1) * P], cv[:, k, cols], ident)
                last.then_inc(s_front_tr, 1)
                pe.wait_ge(s_ramp, c + 1)
                if c >= 1:
                    pe.wait_ge(s_exp, c)
                rmp = ramp[:, c % 2]
                mm(ps[:, 2, 0:2 * P], gt_m, rmp, start=True, stop=False)
                mm(ps[:, 2, 0:2 * P], ident_b[:, :], neg_s[:, :], start=False, stop=True)
                mm(ps[:, 2, 2 * P:4 * P], ones, rmp, start=True, stop=True).then_inc(s_front_seg, 1)
                if c >= 1:
                    pe.wait_ge(s_mt, c)
                mm(ps[:, 1, 0:2 * P], cv[:, 1, cols], cv[:, 2:4, cols], start=True, stop=True).then_inc(s_front_g, 1)

            def back(c):
                b = c % 2
                if c >= 1:
                    pe.wait_ge(s_state, c)
                if c < TT - 1:
                    pe.wait_ge(s_ddx, c + 1)
                    mm(ps[:, 5, 0:2 * P], tok[:, b, P:2 * P], ddx[:, b], start=True, stop=True).then_inc(s_st, 1)
                pe.wait_ge(s_mt, c + 1)
                if c >= 2:
                    pe.wait_ge(s_yg, c - 1)
                last = mm(ps[:, 3 + b, 0:2 * P], tok[:, b, 0:P], mt[:, b], start=True, stop=(c == 0))
                if c:
                    pe.wait_ge(s_ce, c)
                    for h in range(H_SSD):
                        last = mm(ps[:, 3 + b, h * P:(h + 1) * P], state[:, b, h], ce[:, b, h * P:(h + 1) * P],
                                  start=False, stop=(h == 1))
                last.then_inc(s_y, 1)

            def square_sum(c):
                pe.wait_ge(s_sq, c + 1)
                for h in range(H_SSD):
                    last = mm(ps[:, 7, c:c + 1], sq[:, c % 2, h * P:(h + 1) * P], ones[:, 0:1],
                              start=(h == 0), stop=(h == 1))
                last.then_inc(s_ss, 1)

            front(0)
            for c in range(TT):
                if c < TT - 1:
                    front(c + 1)
                back(c)
                if c:
                    square_sum(c - 1)
            square_sum(TT - 1)
            pe.wait_ge(s_wn, KD)
            for t in range(TT):
                for k in range(KD):
                    last = mm(mixer_bank(t), yg[:, k, t * P:(t + 1) * P], wout_sb[:, k, :],
                              start=(k == 0), stop=(k == KD - 1))
                last.then_inc(s_mo, 1)
            transposes(PH_FFN, 0)
            def mixing(g):
                pe.wait_ge(s_fsum, 1)
                pe.wait_ge(s_hT, norms_to(PH_FAC, g))
                for t in range(g * GT, (g + 1) * GT):
                    for k in range(KD):
                        last = mm(mixing_bank(t), hT[:, k, t * P:(t + 1) * P], mixed_w[:, k, :],
                                  start=(k == 0), stop=(k == KD - 1))
                    last.then_inc(s_mx, 1)

            pe.wait_ge(s_ffnw, 32)
            pe.wait_ge(s_r2, TT)
            for g in range(GROUPS):
                pe.wait_ge(s_hT, norms_to(PH_FFN, g))
                for f in range(FB):
                    q = g * FB + f
                    if q >= 2:
                        pe.wait_ge(s_fa, q - 1)
                    pe.wait_ge(s_fwlo, f + 1)
                    for w in range(2):
                        for part, (pw, ph) in enumerate(W_PARTS):
                            if f == 0 and ph:
                                pe.wait_ge(s_hTlo, g + 1)
                            for k in range(KD):
                                last = mm(ps[:, 2 + 2 * w + q % 2, :],
                                          fw13_split[pw][:, w * KD + k, f * P:(f + 1) * P],
                                          hT_split[ph][:, k, g * GW:(g + 1) * GW],
                                          start=(part == 0 and k == 0), stop=(part == 2 and k == KD - 1))
                    last.then_inc(s_gu, 1)
                transposes(*((PH_FFN, 1) if g == 0 else (PH_FAC, 0)))
                for t in range(g * GT, (g + 1) * GT):
                    if t == TT - 2:
                        mixing(0)
                    if t >= 2:
                        pe.wait_ge(s_x1, t - 1)
                    if t % GT == 0:
                        pe.wait_ge(s_ahi, (g + 1) * FB)
                        pe.wait_ge(s_f2lo, 1)
                    for part, (pw, pa) in enumerate(W_PARTS):
                        if t % GT == 0 and pa:
                            pe.wait_ge(s_alo, (g + 1) * FB)
                        for f in range(FB):
                            last = mm(ps[:, 6 + t % 2, 0:D], ffn_a[pa][:, f, (t % GT) * P:(t % GT + 1) * P],
                                      fw2_split[pw][:, f, :], start=(part == 0 and f == 0),
                                      stop=(part == 2 and f == FB - 1))
                    last.then_inc(s_fo, 1)
            transposes(PH_ATT, 0)
            pe.wait_ge(s_pwlo, 3)
            for q in range(GROUPS * 12):
                g, j = divmod(q, 12)
                if q == 1:
                    transposes(PH_FAC, 1)
                if q == 3:
                    mixing(1)
                if q == 9:
                    transposes(PH_ATT, 1)
                if j == 0:
                    pe.wait_ge(s_hT, norms_to(PH_ATT, g))
                if q == 0:
                    pe.wait_ge(s_x2, GT)
                if q == 4:
                    pe.wait_ge(s_x1, TT)
                if q >= 6:
                    if is_k(q - 6) or q % 2:
                        pe.wait_ge(s_qd, vector_fills(q - 6))
                    else:
                        pe.wait_ge(s_qa, scalar_fills(q - 6))
                bank = ps[:, 2 + q % 6, :]
                for part, (pw, ph) in enumerate(W_PARTS):
                    if j == 0 and ph:
                        pe.wait_ge(s_hTlo, GROUPS + g + 1)
                    for k in range(KD):
                        ends = dict(start=(part == 0 and k == 0), stop=(part == 2 and k == KD - 1))
                        if j < 8:
                            at = k * QKV + (j % 4) * P
                            last = mm(bank, qkv_w[pw][:, j // 4, at:at + P], hT_split[ph][:, k, g * GW:(g + 1) * GW],
                                      **ends)
                        else:
                            t = g * GT + j - 8
                            last = mm(bank, hT_split[ph][:, k, t * P:(t + 1) * P],
                                      qkv_w[pw][:, 2, k * QKV:(k + 1) * QKV], **ends)
                last.then_inc(s_qkv, 1)
            pe.wait_ge(s_qa, scalar_fills(FILLS - GT - 1))
            pe.wait_ge(s_qd, vector_fills(FILLS - GT - 1))

            def scores(u):
                i, n = divmod(u, HEADS)
                half = slice(64 * (n % 2), 64 * (n % 2) + 64)
                if u >= 2:
                    pe.wait_ge(s_pr, u - 1)
                pe.wait_ge(s_qs, 2 * (u // 2) + 2)
                for a in range(i // 4 + 1):
                    w = min((i + 1) * P - a * 512, 512)
                    mm(ps[:, 2 * (u % 2) + a, 0:w], q_split[:, n, :], k_hi[:, n, a * 512:a * 512 + w],
                       start=True, stop=False)
                    mm(ps[:, 2 * (u % 2) + a, 0:w], q_split[half, n, :], k_lo[half, n // 2, a * 512:a * 512 + w],
                       start=False, stop=(a < i // 4))
                c = (i % 4) * P
                mm(ps[:, 2 * (u % 2) + i // 4, c:c + P], ident_b[:, :], neg_a[:, :],
                   start=False, stop=True).then_inc(s_sc, 1)

            def probs_transposed(u):
                i, n = divmod(u, HEADS)
                pe.wait_ge(s_pn, u + 1)
                if u >= 1:
                    pe.wait_ge(s_pT, u)
                for j in range(i + 1):
                    last = nc.tensor.transpose(ps[:, 4 + j // 4, (j % 4) * P:(j % 4 + 1) * P],
                                               probs[u % 4][:, j * P:(j + 1) * P], ident)
                last.then_inc(s_pt, 1)

            def attended(m):
                i, pair = divmod(m, HEADS // 2)
                pe.wait_ge(s_pT, 2 * m + 2)
                if pair == 0 and i >= 2:
                    pe.wait_ge(s_slots, i - 1)
                for j in range(i + 1):
                    for h in range(2):
                        n = 2 * pair + h
                        last = mm(ps[h * DH:(h + 1) * DH, 6 + i % 2, pair * P:(pair + 1) * P],
                                  v_sb[:, j, n * DH:(n + 1) * DH], pT[(2 * m + h) % 4][:, j * P:(j + 1) * P],
                                  start=(j == 0), stop=(j == i))
                last.then_inc(s_pv, 1)

            def attention_out(i):
                pe.wait_ge(s_zT, i + 1)
                for c in range(QB):
                    last = mm(ps[:, 6 + i % 2, 0:D], zT[:, c, :], wo_sb[:, c, :], start=(c == 0), stop=(c == QB - 1))
                last.then_inc(s_ao, 1)

            pe.wait_ge(s_wo, 16)
            def route_transposed(i):
                pe.wait_ge(s_hh, TT * PH_MOE + i + 1)
                for k in range(KD):
                    last = nc.tensor.transpose(ps[:, 6 + i % 2, k * P:(k + 1) * P], hh[:, i, k * P:(k + 1) * P], ident)
                last.then_inc(s_rT, 1)

            def route_logits(i):
                pe.wait_ge(s_rTc, i + 1)
                for k in range(KD):
                    last = mm(ps[:, 6 + i % 2, D:D + E], routed_T[:, i % 2, k * P:(k + 1) * P], gate_sb[:, k, :],
                              start=(k == 0), stop=(k == KD - 1))
                last.then_inc(s_lg, 1)

            def route_counts(i):
                pe.wait_ge(s_chosen, i + 1)
                mm(ps[:, 6 + i % 2, D + E:D + 2 * E], lt_m, chosen[:, i, :], start=True, stop=True)
                mm(ps[:, 6 + i % 2, D + 2 * E:D + 3 * E], ones, chosen[:, i, :], start=True, stop=True).then_inc(s_cnt, 1)

            pe.wait_ge(s_gate, 32)
            for u in range((TT + 1) * HEADS + 5):
                if u < TT * HEADS:
                    scores(u)
                if u == 3:
                    pe.wait_ge(s_qa, scalar_fills(FILLS - 1))
                    pe.wait_ge(s_qd, vector_fills(FILLS - 1))
                if 3 <= u < TT * HEADS + 3:
                    probs_transposed(u - 3)
                if HEADS <= u < (TT + 1) * HEADS and u % HEADS == 5:
                    attention_out(u // HEADS - 1)
                if HEADS <= u < (TT + 1) * HEADS and u % HEADS == 7:
                    route_transposed(u // HEADS - 1)
                if u >= 2 * HEADS and u % HEADS == 0:
                    route_logits(u // HEADS - 2)
                if u >= 2 * HEADS and u % HEADS == 4:
                    route_counts(u // HEADS - 2)
                if 4 <= u < TT * HEADS + 4 and u % 2:
                    attended((u - 4) // 2)

            def expert_x(i, b):
                pe.wait_ge(s_xs[b], 8 * (i - b) + 16)
                for k in range(KD):
                    last = nc.tensor.transpose(ps[:, 7, k * P:(k + 1) * P], xs[:, b, k * P:(k + 1) * P], ident)
                last.then_inc(s_ext, 1)

            def expert_up(i, b):
                pe.wait_ge(s_exT, i + 1)
                for w, done in enumerate((s_eg, s_eu)):
                    pe.wait_ge(s_wlo[w], i + 1)
                    for a in range(2):
                        for k in range(KD):
                            for px, pw in PARTS:
                                last = mm(ps[:, 2 * w + a, 0:IH], xsT[px][b][:, k, :],
                                          split_w[w][pw][:, k, a * IH:(a + 1) * IH],
                                          start=(k == 0 and px == pw), stop=(k == KD - 1 and px == 1))
                    last.then_inc(done, 1)

            def expert_aT(i, b):
                pe.wait_ge(s_ea, i + 1)
                for c in range(IB):
                    w = min(P, I - c * P)
                    last = nc.tensor.transpose(ps[0:w, 4 + c // 4, (c % 4) * P:(c % 4 + 1) * P],
                                               ea[:, b, c * P:c * P + w], ident)
                last.then_inc(s_eat, 1)

            def expert_down(i, b, first=False):
                e = nc.tensor.value_load(eid[0:1, bass.ds(i, 1)], min_val=0, max_val=E - 1)
                pe.wait_ge(s_eaa, i + 1)
                pe.wait_ge(s_ead, i + 1)
                if not first:
                    pe.wait_ge(s_eyc, i)
                we = ew2[:, bass.ds(e, 1), :].rearrange("p e (c n) -> p (e c) n", c=IB)
                for c in range(IB):
                    w = min(P, I - c * P)
                    last = mm(ps[:, 6, 0:D], eaT[0:w, b, c, :], we[0:w, c, :], start=(c == 0), stop=(c == IB - 1))
                last.then_inc(s_ey, 1)

            pe.wait_ge(s_e13, 2 * E * 16)
            pe.wait_ge(s_table, 1)
            expert_x(0, 0)
            pe.wait_ge(s_exT, 1)
            expert_x(1, 1)
            expert_up(0, 0)
            pe.wait_ge(s_e2, (E + 1) * 16)

            def body(i, b, first=False):
                pe.wait_ge(s_exT, i + 2)
                expert_x(i + 2, b)
                expert_aT(i, b)
                expert_up(i + 1, 1 - b)
                expert_down(i, b, first)

            body(0, 0, first=True)
            body(1, 1)
            with pe.Fori(1, LAST // 2 - 1) as j:
                for b in range(2):
                    body(2 * j + b, b)
            body(LAST - 2, 0)
            expert_aT(LAST - 1, 1)
            expert_up(LAST, 0)
            expert_down(LAST - 1, 1)
            expert_aT(LAST, 0)
            expert_down(LAST, 0)


def constants():
    c = np.zeros((P, N_CONST), np.float32)
    r = np.arange(P)
    c[:, C_IDENT:C_IDENT + P] = np.eye(P)
    c[:, C_LE:C_LE + P] = r[:, None] <= r[None, :]
    c[:, C_GT:C_GT + P] = r[:, None] > r[None, :]
    c[:, C_LT:C_LT + P] = r[:, None] < r[None, :]
    c[:, C_ONES:C_ONES + P] = 1.0
    c[:, C_NEGS:C_NEGS + P] = np.where(r[None, :] < r[:, None], MASK, 0.0)
    c[:, C_NEGA:C_NEGA + P] = np.where(r[None, :] > r[:, None], MASK, 0.0)
    c[:, C_IOTA:C_IOTA + 24] = np.arange(24)[None, :]
    c[:, C_TOKEN:C_TOKEN + TT + 1] = np.arange(TT + 1)[None, :] * P + r[:, None]
    return c


def kernel(**inputs):
    import concourse.bacc as bacc
    from concourse.bass_utils import run_bass_kernel_spmd as run

    a = {k: np.asarray(v) for k, v in inputs.items()}

    def cols(v, n):
        return v.reshape(n, P).T

    def chunks(w):
        return w.reshape(w.shape[0] // P, P, w.shape[1]).transpose(1, 0, 2)

    small = np.concatenate(
        [cols(a["L0_attn_ln1_w"], 2), cols(a["L0_attn_norm_w"], 2), cols(a["L0_attn_ln2_w"], 2),
         a["L0_attn_conv_w"].reshape(TAPS, CONV_BLOCKS, P).transpose(2, 1, 0).reshape(P, -1),
         cols(a["L0_attn_conv_b"], CONV_BLOCKS)]
        + [np.broadcast_to(a[n][None, :], (P, H_SSD)) for n in ("L0_attn_dt_bias", "L0_attn_A_log", "L0_attn_D")],
        axis=1)
    heads_q = a["L1_attn_W_Q"].reshape(HEADS, QH, KD, P, DH).transpose(3, 1, 2, 0, 4).reshape(P, QH, KD * QKV)

    def heads(w):
        return w.reshape(HEADS, KD, P, DH).transpose(2, 1, 0, 3).reshape(P, KD, QKV)

    def expert_up(w):
        return w.transpose(2, 0, 1).reshape(KD, P, E, I).transpose(1, 2, 0, 3).reshape(P, E, KD * I)

    w2 = a["L1_ffn_w2"].transpose(0, 2, 1)
    full = (IB - 1) * P
    data = {
        "x_in": a["L0_attn_hidden_states"].reshape(T, D),
        "small_in": small,
        "const_in": constants(),
        "w_in": a["L0_attn_W_in"],
        "w_out": a["L0_attn_W_out"],
        "f_w13": np.stack([chunks(a["L0_attn_w1"]), chunks(a["L0_attn_w3"])], axis=1),
        "f_w2": a["L0_attn_w2"],
        "factors": a["L0_ffn_factors"].reshape(RANK, KD, P, D).transpose(2, 0, 1, 3).reshape(P, RANK, KD * D),
        "ffn_bias": np.broadcast_to(a["L0_ffn_bias"][None, :], (P, D)),
        "wq": heads_q,
        "wk": heads(a["L1_attn_W_K"]),
        "wv": heads(a["L1_attn_W_V"]),
        "wo": a["L1_attn_W_O"].reshape(QKV, D),
        "gate": a["L1_ffn_gate_w"].T.reshape(KD, P, E).transpose(1, 0, 2),
        "m_w1": expert_up(a["L1_ffn_w1"]),
        "m_w3": expert_up(a["L1_ffn_w3"]),
        "m_w2": w2[:, :full].reshape(E, IB - 1, P, D).transpose(2, 0, 1, 3).reshape(P, E, full // P * D),
        "m_w2t": w2[:, full:].transpose(1, 0, 2),
    }
    nc = bacc.Bacc("TRN2", target_bir_lowering=False, num_devices=1)
    arrays, args = {}, []
    for name, v in data.items():
        v = np.ascontiguousarray(v)
        arrays[name] = v
        args.append(nc.dram_tensor(name, v.shape, mybir.dt.from_np(v.dtype), kind="ExternalInput").ap())
    out = nc.dram_tensor("out", (T + P, D), F32, kind="ExternalOutput").ap()
    build(nc, *args, out)
    r = run(nc, [arrays], core_ids=[0])
    return r.results[0]["out"][:T].reshape(1, T, D)
```
